# Optimizing a Trainium2 kernel written in Bass

```python
import numpy as np
import jax
import jax.numpy as jnp

def _softmax(x, axis=-1):
    return jax.nn.softmax(x, axis=axis)

def _gelu(x):
    return jax.nn.gelu(x, approximate=True)

def _silu(x):
    return jax.nn.silu(x)

def _sigmoid(x):
    return jax.nn.sigmoid(x)

def _layernorm(x, axis=-1, eps=1e-05):
    m = jnp.mean(x, axis=axis, keepdims=True)
    v = jnp.var(x, axis=axis, keepdims=True)
    return (x - m) / jnp.sqrt(v + eps)

def _scatter_add(tgt, idx, src, axis=0):
    return tgt.at[idx].add(src)

def _segment_sum(src, seg, n):
    return jax.ops.segment_sum(src, seg, n)
kernel_name = 'mk_decoder_postln_d1_seqx_r4_04f730'

def setup_inputs(seed: int=0):
    np.random.seed(seed)
    _w = jnp.asarray

    def _rec_inputs():
        import jax
        import jax.numpy as jnp
        _rk = jax.random.key(seed)
        x = 7.22e-05 + 1 * jax.random.normal(jax.random.fold_in(_rk, 1), (1, 2048, 256), jnp.float32)
        _lenS = 2048 - jax.random.randint(jax.random.fold_in(_rk, 7), (1,), 0, max(1, 2048 // 4) + 1, jnp.int32)
        _lenS2 = 1601 - jax.random.randint(jax.random.fold_in(_rk, 8), (1,), 0, max(1, 1601 // 4) + 1, jnp.int32)
        _ctx_1024P = jax.random.normal(jax.random.fold_in(_rk, 11), (1, 16, 256), jnp.float32)
        _ctx_1024c = jax.random.dirichlet(jax.random.fold_in(_rk, 511), 0.3 * jnp.ones((16,), jnp.float32), (1, 1601))
        _ctx_1024t = jnp.einsum('bsk,bkd->bsd', _ctx_1024c, _ctx_1024P)
        _ctx_1024t = _ctx_1024t * jax.lax.rsqrt(jnp.mean(jnp.square(_ctx_1024t)) + 1e-12) * 0.953939
        ctx_1024 = 4.13588e-05 + 0.999923 * (_ctx_1024t + 0.3 * jax.random.normal(jax.random.fold_in(_rk, 611), (1, 1601, 256), jnp.float32))
        return (x, ctx_1024)
    x, ctx_1024 = _rec_inputs()

    def _L0_attn_setup():
        import jax, jax.numpy as jnp
        import numpy as np
        D_MODEL = 256
        N_HEADS = 16
        D_K = D_MODEL // N_HEADS

        def _rope_cache(T, dtype):
            half = D_K // 2
            freq = 1.0 / 10000.0 ** (2.0 * jnp.arange(half, dtype=dtype) / D_K)
            angles = jnp.arange(T, dtype=dtype)[:, None] * freq[None, :]
            return (jnp.cos(angles), jnp.sin(angles))

        def _apply_rope(x, cos, sin):
            half = x.shape[-1] // 2
            x1, x2 = (x[..., :half], x[..., half:])
            return jnp.concatenate([x1 * cos - x2 * sin, x1 * sin + x2 * cos], axis=-1)
        key = jax.random.key(seed)
        ks = jax.random.split(key, 9)
        s = 0.02
        return {'x': jax.random.normal(ks[0], (4, 512, D_MODEL), dtype=jnp.float32), 'WQ_w': jax.random.normal(ks[1], (D_MODEL, D_MODEL), dtype=jnp.float32) * s, 'WQ_b': jax.random.normal(ks[2], (D_MODEL,), dtype=jnp.float32) * s, 'WK_w': jax.random.normal(ks[3], (D_MODEL, D_MODEL), dtype=jnp.float32) * s, 'WK_b': jax.random.normal(ks[4], (D_MODEL,), dtype=jnp.float32) * s, 'WV_w': jax.random.normal(ks[5], (D_MODEL, D_MODEL), dtype=jnp.float32) * s, 'WV_b': jax.random.normal(ks[6], (D_MODEL,), dtype=jnp.float32) * s, 'Wo_w': jax.random.normal(ks[7], (D_MODEL, D_MODEL), dtype=jnp.float32) * s, 'Wo_b': jax.random.normal(ks[8], (D_MODEL,), dtype=jnp.float32) * s}
    _L0_attn_all = _L0_attn_setup()
    _L0_attn_in = {k: v for k, v in _L0_attn_all.items() if k in ('WQ_w', 'WQ_b', 'WK_w', 'WK_b', 'WV_w', 'WV_b', 'Wo_w', 'Wo_b')}
    del _L0_attn_all

    def _L0_xattn_setup():
        import jax, jax.numpy as jnp
        import numpy as np
        N_HEAD = 16
        key = jax.random.key(seed)
        ks = jax.random.split(key, 5)
        b, l, d = (4, 512, 256)
        dh = d // N_HEAD
        return {'q': jax.random.normal(ks[0], (b, l, d), dtype=jnp.float32), 'kv': jax.random.normal(ks[1], (b, l, d), dtype=jnp.float32), 'Wq': jax.random.normal(ks[2], (d, d), dtype=jnp.float32) * 0.02, 'Wkv': jax.random.normal(ks[3], (2 * dh, d), dtype=jnp.float32) * 0.02, 'Wc': jax.random.normal(ks[4], (d, d), dtype=jnp.float32) * 0.02}
    _L0_xattn_all = _L0_xattn_setup()
    _L0_xattn_in = {k: v for k, v in _L0_xattn_all.items() if k in ('Wq', 'Wkv', 'Wc')}
    del _L0_xattn_all

    def _L0_ffn_setup():
        import jax, jax.numpy as jnp
        import numpy as np
        N_EMBD = 256
        EXPERT_SIZES = [(4, 256), (4, 512)]
        TOP_K = 2
        B, S = (1, 512)
        WIDTHS = []
        for count, size in EXPERT_SIZES:
            WIDTHS += [size] * count
        OFFSETS = np.concatenate([[0], np.cumsum(WIDTHS)]).astype(np.int64)
        E = len(WIDTHS)
        TOTAL_W = int(OFFSETS[-1])
        MAX_W = max(WIDTHS)

        def _stack_experts(w1, w2):
            W1e, W2e = ([], [])
            for e in range(E):
                off, wd = (int(OFFSETS[e]), WIDTHS[e])
                pad = MAX_W - wd
                W1e.append(jnp.pad(w1[:, off:off + wd], ((0, 0), (0, pad))))
                W2e.append(jnp.pad(w2[off:off + wd, :], ((0, pad), (0, 0))))
            return (jnp.stack(W1e), jnp.stack(W2e))
        key = jax.random.key(seed)
        k1, k2, k3, k4 = jax.random.split(key, 4)
        x = jax.random.normal(k1, (B, S, N_EMBD), jnp.float32)
        router_w = jax.random.normal(k2, (E, N_EMBD), jnp.float32) * 0.02
        w1 = jax.random.truncated_normal(k3, -3.0, 3.0, (N_EMBD, TOTAL_W), jnp.float32) * 0.02
        w2 = jax.random.truncated_normal(k4, -3.0, 3.0, (TOTAL_W, N_EMBD), jnp.float32) * 0.02
        return {'x': x, 'router_w': router_w, 'w1': w1, 'w2': w2}
    _L0_ffn_all = _L0_ffn_setup()
    _L0_ffn_in = {k: v for k, v in _L0_ffn_all.items() if k in ('router_w', 'w1', 'w2')}
    del _L0_ffn_all
    return {'x': x, 'ctx_1024': ctx_1024, 'L0_attn_WQ_w': _L0_attn_in['WQ_w'], 'L0_attn_WQ_b': _L0_attn_in['WQ_b'], 'L0_attn_WK_w': _L0_attn_in['WK_w'], 'L0_attn_WK_b': _L0_attn_in['WK_b'], 'L0_attn_WV_w': _L0_attn_in['WV_w'], 'L0_attn_WV_b': _L0_attn_in['WV_b'], 'L0_attn_Wo_w': _L0_attn_in['Wo_w'], 'L0_attn_Wo_b': _L0_attn_in['Wo_b'], 'L0_xattn_Wq': _L0_xattn_in['Wq'], 'L0_xattn_Wkv': _L0_xattn_in['Wkv'], 'L0_xattn_Wc': _L0_xattn_in['Wc'], 'L0_ffn_router_w': _L0_ffn_in['router_w'], 'L0_ffn_w1': _L0_ffn_in['w1'], 'L0_ffn_w2': _L0_ffn_in['w2']}

def reference(x, ctx_1024, L0_attn_WQ_w, L0_attn_WQ_b, L0_attn_WK_w, L0_attn_WK_b, L0_attn_WV_w, L0_attn_WV_b, L0_attn_Wo_w, L0_attn_Wo_b, L0_xattn_Wq, L0_xattn_Wkv, L0_xattn_Wc, L0_ffn_router_w, L0_ffn_w1, L0_ffn_w2):
    import jax
    import jax.numpy as jnp

    def _L0_attn_ref(x, WQ_w, WQ_b, WK_w, WK_b, WV_w, WV_b, Wo_w, Wo_b):
        import jax, jax.numpy as jnp
        import numpy as np
        D_MODEL = 256
        N_HEADS = 16
        D_K = D_MODEL // N_HEADS

        def _rope_cache(T, dtype):
            half = D_K // 2
            freq = 1.0 / 10000.0 ** (2.0 * jnp.arange(half, dtype=dtype) / D_K)
            angles = jnp.arange(T, dtype=dtype)[:, None] * freq[None, :]
            return (jnp.cos(angles), jnp.sin(angles))

        def _apply_rope(x, cos, sin):
            half = x.shape[-1] // 2
            x1, x2 = (x[..., :half], x[..., half:])
            return jnp.concatenate([x1 * cos - x2 * sin, x1 * sin + x2 * cos], axis=-1)
        B, T, D = x.shape

        def proj(w, b):
            y = jnp.einsum('btd,ed->bte', x, w) + b
            return y.reshape(B, T, N_HEADS, D_K).transpose(0, 2, 1, 3)
        q = proj(WQ_w, WQ_b)
        k = proj(WK_w, WK_b)
        v = proj(WV_w, WV_b)
        cos, sin = _rope_cache(T, x.dtype)
        q = _apply_rope(q, cos, sin)
        k = _apply_rope(k, cos, sin)
        scores = jnp.einsum('bhqd,bhkd->bhqk', q, k) / jnp.sqrt(jnp.asarray(D_K, x.dtype))
        causal = jnp.tril(jnp.ones((T, T), dtype=bool))
        scores = jnp.where(causal[None, None, :, :], scores, -jnp.inf)
        attn = jax.nn.softmax(scores, axis=-1)
        out = jnp.einsum('bhqk,bhkd->bhqd', attn, v)
        out = out.transpose(0, 2, 1, 3).reshape(B, T, D)
        return jnp.einsum('btd,ed->bte', out, Wo_w) + Wo_b

    def _L0_xattn_ref(q, kv, Wq, Wkv, Wc):
        import jax, jax.numpy as jnp
        import numpy as np
        N_HEAD = 16
        b, l, d = q.shape
        h = N_HEAD
        dh = d // h
        qp = jnp.einsum('bld,ed->ble', q, Wq)
        scores = jnp.einsum('bld,bmd->blm', qp, kv)
        idx = jnp.argmax(scores, axis=-1)
        mem = jnp.take_along_axis(kv, idx[..., None], axis=1)
        mkv = jnp.einsum('bld,ed->ble', mem, Wkv)
        mk, mv = jnp.split(mkv, 2, axis=-1)
        qh = qp.reshape(b, l, h, dh).transpose(0, 2, 1, 3)
        scale = 1.0 / np.sqrt(dh).astype(np.float32)
        logits = jnp.einsum('bhld,bmd->bhlm', qh, mk) * scale
        attn = jax.nn.softmax(logits, axis=-1)
        out = jnp.einsum('bhlm,bmd->bhld', attn, mv)
        out = out.transpose(0, 2, 1, 3).reshape(b, l, d)
        return jnp.einsum('bld,ed->ble', out, Wc)

    def _L0_ffn_ref(x, router_w, w1, w2):
        import jax, jax.numpy as jnp
        import numpy as np
        N_EMBD = 256
        EXPERT_SIZES = [(4, 256), (4, 512)]
        TOP_K = 2
        B, S = (1, 512)
        WIDTHS = []
        for count, size in EXPERT_SIZES:
            WIDTHS += [size] * count
        OFFSETS = np.concatenate([[0], np.cumsum(WIDTHS)]).astype(np.int64)
        E = len(WIDTHS)
        TOTAL_W = int(OFFSETS[-1])
        MAX_W = max(WIDTHS)

        def _stack_experts(w1, w2):
            W1e, W2e = ([], [])
            for e in range(E):
                off, wd = (int(OFFSETS[e]), WIDTHS[e])
                pad = MAX_W - wd
                W1e.append(jnp.pad(w1[:, off:off + wd], ((0, 0), (0, pad))))
                W2e.append(jnp.pad(w2[off:off + wd, :], ((0, pad), (0, 0))))
            return (jnp.stack(W1e), jnp.stack(W2e))
        b, s, d = x.shape
        xf = x.reshape(-1, d)
        logits = xf @ router_w.T
        probs = jax.nn.sigmoid(logits.astype(jnp.float32))
        topw, sel = jax.lax.top_k(probs, TOP_K)
        topw = topw / (topw.sum(-1, keepdims=True) + 1e-20)
        topw = topw.astype(x.dtype)
        onehot = sel[:, :, None] == jnp.arange(E)[None, None, :]
        combine = jnp.sum(topw[:, :, None] * onehot, axis=1)
        W1e, W2e = _stack_experts(w1, w2)
        h = jnp.einsum('td,edw->tew', xf, W1e)
        h = jnp.square(jax.nn.relu(h))
        y = jnp.einsum('tew,ewd->ted', h, W2e)
        out = jnp.einsum('ted,te->td', y, combine)
        return out.reshape(b, s, d)
    x = _layernorm(x + _L0_attn_ref(x, L0_attn_WQ_w, L0_attn_WQ_b, L0_attn_WK_w, L0_attn_WK_b, L0_attn_WV_w, L0_attn_WV_b, L0_attn_Wo_w, L0_attn_Wo_b), axis=-1)
    x = _layernorm(x + _L0_xattn_ref(x, ctx_1024, L0_xattn_Wq, L0_xattn_Wkv, L0_xattn_Wc), axis=-1)
    x = _layernorm(x + _L0_ffn_ref(x, L0_ffn_router_w, L0_ffn_w1, L0_ffn_w2), axis=-1)
    return x

_drawn_inputs = setup_inputs


def setup_inputs(seed=0):
    import zlib

    import numpy as np

    out = dict(_drawn_inputs(seed))
    spreads = {}
    factors = {'L0_attn_WQ_w': 8.0,
     'L0_attn_WQ_b': 8.0,
     'L0_attn_WK_w': 8.0,
     'L0_attn_WK_b': 8.0,
     'L0_attn_WV_w': 8.0,
     'L0_attn_WV_b': 8.0,
     'L0_attn_Wo_w': 5.763,
     'L0_attn_Wo_b': 10.142,
     'L0_xattn_Wq': 8.0}
    for name, (base, spread) in spreads.items():
        noise = np.random.default_rng([zlib.crc32(name.encode()), seed]).standard_normal(out[name].shape)
        drawn = base * np.exp(spread * noise) if base else spread * noise
        out[name] = jnp.asarray(drawn.astype(out[name].dtype))
    for name, factor in factors.items():
        out[name] = (out[name] * factor).astype(out[name].dtype)
    return out
```

```python
import concourse.bass as bass
from concourse import mybir
from contextlib import ExitStack

F32 = mybir.dt.float32
BF16 = mybir.dt.bfloat16
U32 = mybir.dt.uint32
ALU = mybir.AluOpType
ACT = mybir.ActivationFunctionType
AX = mybir.AxisListType

P = 128
T = 2048
D = 256
H = 16
DK = D // H
KD = D // P
NT = T // P
C = 512
NC = T // C
GH = 4
NG = H // GH
M = 1601
MT = -(-M // P)
MP = MT * P
E = 8
WIDTHS = [256] * 4 + [512] * 4
W = sum(WIDTHS)
WT = W // P
PAIRS = [(0, 0), (0, 1), (1, 0), (0, 2), (2, 0), (1, 1)]
KS = len(PAIRS) * DK
VW = DK + 1
LOW = -3.0e38
MASKED = -1.0e30
SCALE = DK ** -0.5
EPS = 1e-5


class Count:

    def __init__(self, sem):
        self.sem, self.n = sem, 0

    def inc(self, ins, by=1):
        ins.then_inc(self.sem, by)
        self.n += by
        return self.n


def decoder_layer(nc, x, xT, ctxT, wq, wqs, bq, bqs, wk, wks, bk, bks, wv, bv, wo, bo, xwq, xwk, xwv, xwc, rw, w1, w2,
                  cosT, sinT, identity, sums, causal, iota, out):
    top = ExitStack()
    made = [0]

    def sem(name):
        return top.enter_context(nc.semaphore(name))

    def sb(scope, name, shape, dt=F32):
        return scope.enter_context(nc.sbuf_tensor(name, shape, dt))

    def psum(scope, name, shape, dt=F32):
        return scope.enter_context(nc.psum_tensor(name, shape, dt))

    def chain(eng, name):
        done = Count(sem(name))

        def link(ins):
            eng.wait_ge(done.sem, done.inc(ins))

        return link

    def kt_view(w):
        return w.rearrange("(k p) n -> p k n", p=P)

    with top:
        qparts = nc.dram_tensor("qparts", [3, D, T], BF16).ap()
        kparts = nc.dram_tensor("kparts", [3, D, T], BF16).ap()
        xparts = nc.dram_tensor("xparts", [3, D, T], BF16).ap()

        ident = sb(top, "ident", [P, P])
        sum_sel = sb(top, "sum_sel", [P, P])
        zeros = sb(top, "zeros", [P, C])
        kx = sb(top, "kx", [P, MP], BF16)
        vx = sb(top, "vx", [P, MT, VW])
        maskx = sb(top, "maskx", [MT, P], BF16)

        consts_in = sem("consts_in")

        att = ExitStack()
        with att:
            V = sb(att, "V", [P, NT, H, VW])
            o_first = sb(att, "o_first", [P, T])
            stage = ExitStack()
            with stage:
                xT_sb = sb(stage, "xT_sb", [P, KD, T])
                w_sb = sb(stage, "w_sb", [P, 5, KD, D])
                ctx_sb = sb(stage, "ctx_sb", [P, KD, M])
                wkv_sb = sb(stage, "wkv_sb", [P, 2, KD, DK])
                cs = sb(stage, "cs", [P, 2, T])
                bias = sb(stage, "bias", [P, 4, KD])
                bv_all = sb(stage, "bv_all", [P, D])
                parts = sb(stage, "parts", [P, 2, 3, C], BF16)
                rest = sb(stage, "rest", [P, C])
                turned = sb(stage, "turned", [P, 2, C])
                whole = sb(stage, "whole", [P, C])
                mk = sb(stage, "mk", [DK, MP])
                mk_rest = sb(stage, "mk_rest", [DK, MP])
                mk_parts = sb(stage, "mk_parts", [DK, 3, MP], BF16)
                pq = psum(stage, "pq", [P, 2, 2, C])
                pv = psum(stage, "pv", [P, 2, C])
                pk = psum(stage, "pk", [P, 2, C])

                s_x, s_w, s_b, s_ctx = sem("x_in"), sem("weights_in"), sem("bias_in"), sem("ctx_in")
                s_ones, s_mk_out = sem("ones_set"), sem("mk_out")
                s_parts_out = [sem(f"parts_out{i}") for i in range(2)]
                qk_ready, qk_read = sem("qk_ready"), sem("qk_read")
                v_ready, v_read = sem("v_ready"), sem("v_read")
                mk_ready, mv_ready, mv_read = sem("mk_ready"), sem("mv_ready"), sem("mv_read")
                whole_ready, p1_ready, rest_ready, p2_ready, p3_ready = (
                    sem("whole_ready"), sem("p1_ready"), sem("rest_ready"), sem("p2_ready"), sem("p3_ready"))
                mk_copied, mk1, mkr, mk2, mk3 = (sem("mk_copied"), sem("mk1"), sem("mkr"), sem("mk2"), sem("mk3"))
                units = [(t, m, c) for t in range(2) for m in range(KD) for c in range(NC)]
                mk_cols = [(a, min(a + C, M)) for a in range(0, M, C)]

                with nc.Block() as block:
                    @block.sync
                    def _(sp):
                        sp.dma_start(xT_sb[:], kt_view(xT)).then_inc(s_x, 16)
                        for n, w in enumerate((wq, wqs, wk, wks, wv)):
                            sp.dma_start(w_sb[:, n], kt_view(w)).then_inc(s_w, 16)
                        sp.dma_start(cs[:, 0], cosT).then_inc(s_b, 16)
                        sp.dma_start(cs[:, 1], sinT).then_inc(s_b, 16)
                        for n, b in enumerate((bq, bqs, bk, bks)):
                            sp.dma_start(bias[:, n], b).then_inc(s_b, 16)
                        sp.dma_start(bv_all[:], bv.rearrange("(a n) -> a n", a=1).to_broadcast([P, D])).then_inc(s_b, 16)
                        sp.dma_start(ctx_sb[:], kt_view(ctxT)).then_inc(s_ctx, 16)
                        sp.dma_start(wkv_sb[:, 0], kt_view(xwk)).then_inc(s_ctx, 16)
                        sp.dma_start(wkv_sb[:, 1], kt_view(xwv)).then_inc(s_ctx, 16)
                        sp.dma_start(ident[:], identity).then_inc(consts_in, 16)
                        sp.dma_start(sum_sel[:], sums).then_inc(consts_in, 16)
                        for n, (t, m, c) in enumerate(units):
                            dst = (qparts, kparts)[t][:, m * P:(m + 1) * P, c * C:(c + 1) * C].rearrange("r p t -> p r t")
                            sp.wait_ge(p3_ready, n + 1)
                            sp.dma_start(dst, parts[:, n % 2]).then_inc(s_parts_out[n % 2], 16)
                        sp.wait_ge(mk3, 1)
                        for n, (_, b) in enumerate(PAIRS):
                            sp.dma_start(kx[n * DK:(n + 1) * DK, :], mk_parts[:, b]).then_inc(s_mk_out, 16)
                        for i in range(2):
                            sp.wait_ge(s_parts_out[i], 8 * len(units))
                        sp.wait_ge(s_mk_out, 16 * len(PAIRS))
                        sp.wait_ge(consts_in, 32)

                    @block.gpsimd
                    def _(pool):
                        nc.gpsimd.memset(V[:, :, :, DK:VW], 1.0).then_inc(s_ones, 1)
                        nc.gpsimd.memset(zeros[:], 0.0).then_inc(s_ones, 1)
                        nc.gpsimd.memset(vx[:], 0.0).then_inc(s_ones, 1)
                        pool.wait_ge(s_ones, 3)
                        nc.gpsimd.memset(kx[KS:KS + 3, :], 1.0).then_inc(s_ones, 1)
                        pool.wait_ge(s_ones, 4)
                        nc.gpsimd.memset(mk[:], 0.0).then_inc(s_ones, 1)
                        pool.wait_ge(s_ones, 5)

                    @block.tensor
                    def _(pe):
                        pe.wait_ge(s_x, 16)
                        pe.wait_ge(s_w, 16 * 5)
                        for n, (t, m, c) in enumerate(units):
                            if n >= 2:
                                pe.wait_ge(qk_read, n - 1)
                            for s in range(2):
                                for k in range(KD):
                                    last = nc.tensor.matmul(pq[:, n % 2, s], w_sb[:, 2 * t + s, k, m * P:(m + 1) * P],
                                                            xT_sb[:, k, c * C:(c + 1) * C], start=(k == 0), stop=(k == KD - 1))
                            last.then_inc(qk_ready, 1)
                            if n == 0:
                                pe.wait_ge(s_ctx, 48)
                            if n >= 2:
                                pe.wait_ge(v_read, n - 1)
                            for k in range(KD):
                                last = nc.tensor.matmul(pv[:, n % 2, 0:D], xT_sb[:, k, n * P:(n + 1) * P], w_sb[:, 4, k, :],
                                                        start=(k == 0), stop=(k == KD - 1))
                            last.then_inc(v_ready, 1)
                        for n, (a, b) in enumerate(mk_cols):
                            if n >= 2:
                                pe.wait_ge(mk_copied, n - 1)
                            for k in range(KD):
                                last = nc.tensor.matmul(pk[0:DK, n % 2, 0:b - a], wkv_sb[:, 0, k, :], ctx_sb[:, k, a:b],
                                                        start=(k == 0), stop=(k == KD - 1))
                            last.then_inc(mk_ready, 1)
                        for n in range(MT):
                            rows = min(P, M - n * P)
                            pe.wait_ge(v_read, NT - 1 + (n % 2) if n < 2 else NT)
                            if n >= 2:
                                pe.wait_ge(mv_read, n - 1)
                            for k in range(KD):
                                last = nc.tensor.matmul(pv[0:rows, n % 2, 0:DK], ctx_sb[:, k, n * P:n * P + rows],
                                                        wkv_sb[:, 1, k, :], start=(k == 0), stop=(k == KD - 1))
                            last.then_inc(mv_ready, 1)

                    @block.scalar
                    def _(act):
                        for n in range(len(units)):
                            act.wait_ge(whole_ready, n + 1)
                            if n >= 2:
                                act.wait_ge(s_parts_out[n % 2], 16 * (n // 2))
                            nc.scalar.copy(parts[:, n % 2, 0], whole[:]).then_inc(p1_ready, 1)
                            act.wait_ge(rest_ready, n + 1)
                            nc.scalar.copy(parts[:, n % 2, 1], rest[:]).then_inc(p2_ready, 1)
                        act.wait_ge(s_ones, 5)
                        for n, (a, b) in enumerate(mk_cols):
                            act.wait_ge(mk_ready, n + 1)
                            nc.scalar.copy(mk[:, a:b], pk[0:DK, n % 2, 0:b - a]).then_inc(mk_copied, 1)
                        act.wait_ge(mk_copied, len(mk_cols))
                        nc.scalar.copy(mk_parts[:, 0], mk[:]).then_inc(mk1, 1)
                        act.wait_ge(mkr, 1)
                        nc.scalar.copy(mk_parts[:, 1], mk_rest[:]).then_inc(mk2, 1)

                    @block.vector
                    def _(dve):
                        link = chain(dve, "rope_chain")
                        dve.wait_ge(s_b, 16 * 7)
                        for n, (t, m, c) in enumerate(units):
                            dve.wait_ge(qk_ready, n + 1)
                            if n:
                                dve.wait_ge(p1_ready, n)
                            for s in range(2):
                                last = nc.vector.scalar_tensor_tensor(
                                    out=turned[:, s], in0=pq[:, n % 2, s], scalar=bias[:, 2 * t + s, m:m + 1],
                                    in1=cs[:, s, c * C:(c + 1) * C], op0=ALU.add, op1=ALU.mult)
                            last.then_inc(qk_read, 1)
                            dve.wait_ge(qk_read, n + 1)
                            nc.vector.tensor_tensor(whole[:], turned[:, 0], turned[:, 1], ALU.add).then_inc(whole_ready, 1)
                            dve.wait_ge(v_ready, n + 1)
                            nc.vector.tensor_tensor(V[:, n, :, 0:DK], pv[:, n % 2, 0:D].rearrange("p (h d) -> p h d", h=H),
                                                    bv_all[:].rearrange("p (h d) -> p h d", h=H), ALU.add).then_inc(v_read, 1)
                            dve.wait_ge(p1_ready, n + 1)
                            nc.vector.tensor_tensor(rest[:], whole[:], parts[:, n % 2, 0], ALU.subtract).then_inc(rest_ready, 1)
                            dve.wait_ge(p2_ready, n + 1)
                            nc.vector.tensor_tensor(parts[:, n % 2, 2], rest[:], parts[:, n % 2, 1], ALU.subtract).then_inc(p3_ready, 1)
                        dve.wait_ge(mk1, 1)
                        nc.vector.tensor_tensor(mk_rest[:], mk[:], mk_parts[:, 0], ALU.subtract).then_inc(mkr, 1)
                        dve.wait_ge(mk2, 1)
                        nc.vector.tensor_tensor(mk_parts[:, 2], mk_rest[:], mk_parts[:, 1], ALU.subtract).then_inc(mk3, 1)
                        dve.wait_ge(s_ones, 5)
                        for n in range(MT):
                            rows = min(P, M - n * P)
                            dve.wait_ge(mv_ready, n + 1)
                            nc.vector.tensor_copy(vx[0:rows, n, 0:DK], pv[0:rows, n % 2, 0:DK]).then_inc(mv_read, 1)
                        for n in range(MT):
                            rows = min(P, M - n * P)
                            last = nc.vector.memset(vx[0:rows, n, DK:VW], 1.0)
                        link(last)

            def attention(tag, scope, steps, works, keys_rows, shift_rows, loads, prefetch, o_of, causal_sb):
                probs = sb(scope, f"{tag}_probs", [P, 3, GH, C])
                acc_sb = sb(scope, f"{tag}_acc", [P, 2, C])
                piece_max = sb(scope, f"{tag}_piece_max", [P, NT * GH, 4])
                row_max = sb(scope, f"{tag}_row_max", [P, NT * GH])
                shift = sb(scope, f"{tag}_shift", [NT * GH, 2, 2, P], BF16)
                junk = sb(scope, f"{tag}_junk", [P, 2, C])
                mark = sb(scope, f"{tag}_mark", [P, 1])
                ps = psum(scope, f"{tag}_scores", [P, GH, C])
                po = psum(scope, f"{tag}_out", [P, 2, C])
                pm = psum(scope, f"{tag}_max", [P, 2, C])
                s_load = [sem(f"{tag}_load{n}") for n in range(len(loads))]
                scores_ready, probs_ready, probs_masked, probs_used = (
                    sem(f"{tag}_scores_ready"), sem(f"{tag}_probs_ready"), sem(f"{tag}_probs_masked"), sem(f"{tag}_probs_used"))
                side_ready, side_read = sem(f"{tag}_side_ready"), sem(f"{tag}_side_read")
                acc_copied, inverse_ready = sem(f"{tag}_acc_copied"), sem(f"{tag}_inverse_ready")
                max_ready, shift_ready = sem(f"{tag}_max_ready"), sem(f"{tag}_shift_ready")
                shift_in = [sem(f"{tag}_shift_in{i}") for i in range(2)]
                s_set, s_pre = sem(f"{tag}_set"), sem(f"{tag}_prefetched")

                first_of, count_of = {}, {}
                for i, st in enumerate(steps):
                    first_of.setdefault(st["unit"], i)
                    count_of[st["unit"]] = count_of.get(st["unit"], 0) + 1
                side = [[] for _ in range(len(steps) + 4)]
                before = [("piece", 0, n) for n in range(len(works[0]["pieces"]))] + [("turn", 0)]
                for u in range(1, len(works)):
                    a, n = first_of[u - 1], count_of[u - 1]
                    pieces = [("piece", u, k) for k in range(len(works[u]["pieces"]))]
                    per = -(-len(pieces) // (n - works[u]["spare"]))
                    for k in range(n):
                        side[a + k] += pieces[k * per:(k + 1) * per]
                        if pieces[k * per:(k + 1) * per] and (k + 1) * per >= len(pieces):
                            side[a + k + 1] += [("turn", u)]
                for i, st in enumerate(steps):
                    if st["last"]:
                        side[i + 2] += [("sums", st["chunk"], i)]
                diag_before = [0]
                for st in steps:
                    diag_before.append(diag_before[-1] + st["diag"])

                with nc.Block() as block:
                    @block.sync
                    def _(sp):
                        for n, (pairs, _) in enumerate(loads):
                            for dst, src in pairs:
                                sp.dma_start(dst, src).then_inc(s_load[n], 16)
                        for dst, src in prefetch:
                            sp.dma_start(dst, src).then_inc(s_pre, 16)
                        for u, wk_ in enumerate(works):
                            sp.wait_ge(shift_ready, u + 1)
                            for b, dst in enumerate(wk_["shift_to"]):
                                sp.dma_start(dst, shift[0:wk_["rows"], u % 2, b]).then_inc(shift_in[u % 2], 16)
                        for i in range(2):
                            sp.wait_ge(shift_in[i], 16 * len(works))
                        if prefetch:
                            sp.wait_ge(s_pre, 16 * len(prefetch))

                    @block.gpsimd
                    def _(pool):
                        for n, ap in enumerate(shift_rows):
                            nc.gpsimd.memset(ap, 1.0).then_inc(s_set, 1)
                            pool.wait_ge(s_set, n + 1)
                        for i, st in enumerate(steps):
                            if st["diag"]:
                                pool.wait_ge(probs_ready, 2 * (i + 1))
                                blk = probs[:, i % 3, :, st["off"]:st["off"] + P]
                                nc.gpsimd.affine_select(out=blk, in_=blk, compare_op=ALU.is_ge, fill=0.0, base=0,
                                                        pattern=[[0, GH], [1, P]], channel_multiplier=-1).then_inc(probs_masked, 1)

                    @block.tensor
                    def _(pe):
                        uses = [0]
                        pe.wait_ge(consts_in, 32)
                        for n in range(2):
                            nc.tensor.matmul(po[:, n], zeros[:, 0:P], zeros[:], start=True, stop=True)
                        loaded = [0]

                        def side_item(item):
                            n = uses[0]
                            uses[0] += 1
                            if n >= 2:
                                pe.wait_ge(side_read, n - 1)
                            slot = pm[:, n % 2]
                            if item[0] == "piece":
                                pc = works[item[1]]["pieces"][item[2]]
                                while loaded[0] < pc["load"]:
                                    pe.wait_ge(s_load[loaded[0]], 16 * len(loads[loaded[0]][0]))
                                    loaded[0] += 1
                                if item[1] == 0 and item[2] == 0:
                                    pe.wait_ge(s_set, len(shift_rows))
                                mm = nc.tensor.matmul(slot[:, 0:pc["w"]], pc["lhsT"], pc["rhs"], start=True, stop=True)
                            elif item[0] == "turn":
                                r = works[item[1]]["rows"]
                                pe.wait_ge(max_ready, item[1] + 1)
                                mm = nc.tensor.transpose(slot[0:r, 0:P], row_max[:, 0:r], ident[:])
                            else:
                                pe.wait_ge(acc_copied, item[1] + 1)
                                mm = nc.tensor.matmul(slot, sum_sel[:], acc_sb[:, item[1] % 2], start=True, stop=True)
                            mm.then_inc(side_ready, 1)

                        def values(i):
                            st = steps[i]
                            pe.wait_ge(probs_ready, 2 * (i + 1))
                            if st["diag"]:
                                pe.wait_ge(probs_masked, diag_before[i + 1])
                            if st["first"] and st["chunk"] >= 2:
                                pe.wait_ge(acc_copied, st["chunk"] - 1)
                            for j in range(GH):
                                mm = nc.tensor.matmul(po[32 * j:32 * j + VW, st["chunk"] % 2, st["off"]:C], st["values"](j),
                                                      probs[:, i % 3, j, st["off"]:C], start=st["first"], stop=st["last"],
                                                      tile_position=(0, 32 * j))
                            mm.then_inc(probs_used, 1)

                        for item in before:
                            side_item(item)
                        for i, st in enumerate(steps):
                            if first_of[st["unit"]] == i:
                                pe.wait_ge(shift_in[st["unit"] % 2], 32 * (st["unit"] // 2 + 1))
                            for pair in range(2):
                                if i:
                                    pe.wait_ge(probs_ready, 2 * (i - 1) + pair + 1)
                                for j in (2 * pair, 2 * pair + 1):
                                    mm = nc.tensor.matmul(ps[:, j, st["off"]:C], st["keys"](j), st["queries"](j), start=True, stop=True)
                                mm.then_inc(scores_ready, 1)
                            if i:
                                values(i - 1)
                            for item in side[i]:
                                side_item(item)
                        values(len(steps) - 1)
                        for i in range(len(steps), len(side)):
                            for item in side[i]:
                                side_item(item)

                    @block.scalar
                    def _(act):
                        for i, st in enumerate(steps):
                            for pair in range(2):
                                act.wait_ge(scores_ready, 2 * i + pair + 1)
                                if i >= 3 and pair == 0:
                                    act.wait_ge(probs_used, i - 2)
                                nc.scalar.activation(probs[:, i % 3, 2 * pair:2 * pair + 2, st["off"]:C],
                                                     ps[:, 2 * pair:2 * pair + 2, st["off"]:C], ACT.Exp,
                                                     scale=SCALE).then_inc(probs_ready, 1)

                    @block.vector
                    def _(dve):
                        uses = [0]
                        done = [0]
                        link = chain(dve, f"{tag}_dve_chain")
                        link(nc.vector.memset(piece_max[:], LOW))

                        def side_item(item):
                            n = uses[0]
                            uses[0] += 1
                            dve.wait_ge(side_ready, n + 1)
                            slot = pm[:, n % 2]
                            if item[0] == "piece":
                                pc = works[item[1]]["pieces"][item[2]]
                                to = piece_max[:, pc["row"], pc["at"]:pc["at"] + 1]
                                if pc["diag"]:
                                    ins = nc.vector.tensor_tensor_reduce(out=junk[:, n % 2, 0:pc["w"]], in0=slot[:, 0:pc["w"]],
                                                                         in1=causal_sb[:, C - pc["w"]:C], scale=1.0, scalar=LOW,
                                                                         op0=ALU.add, op1=ALU.max, accum_out=to)
                                else:
                                    ins = nc.vector.tensor_reduce(to, slot[:, 0:pc["w"]], AX.X, ALU.max)
                                ins.then_inc(side_read, 1)
                                if item[2] == len(works[item[1]]["pieces"]) - 1:
                                    dve.wait_ge(side_read, n + 1)
                                    r = works[item[1]]["rows"]
                                    nc.vector.tensor_reduce(row_max[:, 0:r], piece_max[:, 0:r], AX.X, ALU.max).then_inc(max_ready, 1)
                            elif item[0] == "turn":
                                u, r = item[1], works[item[1]]["rows"]
                                if u >= 2:
                                    dve.wait_ge(shift_in[u % 2], 32 * (u // 2))
                                link(nc.vector.tensor_scalar(shift[0:r, u % 2, 0], slot[0:r, 0:P], -1.0, None, ALU.mult))
                                nc.vector.scalar_tensor_tensor(out=shift[0:r, u % 2, 1], in0=slot[0:r, 0:P], scalar=-1.0,
                                                               in1=shift[0:r, u % 2, 0], op0=ALU.mult,
                                                               op1=ALU.subtract).then_inc(shift_ready, 1)
                                dve.wait_ge(shift_ready, u + 1)
                                nc.vector.memset(mark[:], 0.0).then_inc(side_read, 1)
                            else:
                                cc = item[1]
                                nc.vector.reciprocal(junk[:, n % 2], slot).then_inc(inverse_ready, 1)
                                dve.wait_ge(inverse_ready, cc + 1)
                                nc.vector.tensor_tensor(o_of(cc), acc_sb[:, cc % 2], junk[:, n % 2], ALU.mult).then_inc(side_read, 1)

                        for item in before:
                            side_item(item)
                        for i in range(len(side)):
                            if 1 <= i <= len(steps) and steps[i - 1]["last"]:
                                cc = steps[i - 1]["chunk"]
                                dve.wait_ge(probs_used, i)
                                nc.vector.tensor_copy(acc_sb[:, cc % 2], po[:, cc % 2]).then_inc(acc_copied, 1)
                            for item in side[i]:
                                side_item(item)

            stage = ExitStack()
            with stage:
                stack = [sb(stage, f"stack{g}", [P, 2, GH, T], BF16) for g in range(NG)]
                causal_sb = sb(stage, "causal_sb", [P, C])
                loads = []
                for g in range(NG):
                    pairs = [(causal_sb[:], causal)] if g == 0 else []
                    for n, ab in enumerate(PAIRS):
                        for s, src in enumerate((qparts, kparts)):
                            pairs.append((stack[g][n * DK:(n + 1) * DK, s],
                                          src[ab[s], g * GH * DK:(g + 1) * GH * DK, :].rearrange("(h i) t -> i h t", i=DK)))
                    loads.append((pairs, g))

                def o_self(g):
                    if g == 0:
                        return o_first[:]
                    return stack[g - 1][:, 0, 0:2, :].rearrange("p h t -> p (h t)").bitcast(F32)

                steps, works = [], []
                for g in range(NG):
                    pieces = []
                    for qt in range(NT):
                        for j in range(GH):
                            for n, a in enumerate(range(0, (qt + 1) * P, C)):
                                b = min(a + C, (qt + 1) * P)
                                pieces.append(dict(w=b - a, lhsT=stack[g][0:KS, 0, j, qt * P:(qt + 1) * P],
                                                   rhs=stack[g][0:KS, 1, j, a:b], row=j * NT + qt, at=n,
                                                   diag=b == (qt + 1) * P, load=g + 1))
                    works.append(dict(pieces=pieces, rows=GH * NT, spare=8,
                                      shift_to=[stack[g][KS + b:KS + b + 1, 0].rearrange("o h (n t) -> o (h n) t", t=P) for b in range(2)]))
                    for c in range(NC):
                        for kt in range((c + 1) * C // P):
                            off = max(0, kt * P - c * C)
                            steps.append(dict(
                                unit=g, chunk=g * NC + c, off=off, diag=int(kt * P >= c * C), first=kt == 0,
                                last=kt == (c + 1) * C // P - 1,
                                keys=lambda j, g=g, kt=kt: stack[g][0:KS + 2, 1, j, kt * P:(kt + 1) * P],
                                queries=lambda j, g=g, c=c, off=off: stack[g][0:KS + 2, 0, j, c * C + off:(c + 1) * C],
                                values=lambda j, g=g, kt=kt: V[:, kt, g * GH + j, :]))
                attention("self", stage, steps, works, KS, [stack[g][KS:KS + 2, 1] for g in range(NG)], loads, [],
                          lambda cc: o_self(cc // NC)[:, (cc % NC) * C:(cc % NC + 1) * C], causal_sb)

                o_dram = nc.dram_tensor("o_self", [NG, P, T], F32).ap()
                s_o = sem("o_self_out")
                with nc.Block() as block:
                    @block.sync
                    def _(sp):
                        for g in range(NG):
                            sp.dma_start(o_dram[g], o_self(g)).then_inc(s_o, 16)
                        sp.wait_ge(s_o, 16 * NG)

        def project_norm(tag, scope, o_src, o_dram, w_dram, res_dram, bias_dram, x_sb, xT_sb, extra):
            w_sb = sb(scope, f"{tag}_w", [P, NG, D])
            o_sb = o_src if o_src is not None else sb(scope, f"{tag}_o", [P, NG, T])
            b_sb = sb(scope, f"{tag}_b", [P, D])
            stats = sb(scope, f"{tag}_stats", [P, NT, 6])
            mv = sb(scope, f"{tag}_mv", [P, NT, 2])
            rstd = sb(scope, f"{tag}_rstd", [P, NT])
            py = psum(scope, f"{tag}_py", [P, 2, C])
            pt = psum(scope, f"{tag}_pt", [P, 2, C])
            s_in, s_wz, s_w = sem(f"{tag}_in"), sem(f"{tag}_w_zeroed"), sem(f"{tag}_w_in")
            y_ready, y_read = sem(f"{tag}_y_ready"), sem(f"{tag}_y_read")
            res_ready, normed = sem(f"{tag}_res_ready"), sem(f"{tag}_normed")
            var_ready, std_ready = sem(f"{tag}_var_ready"), sem(f"{tag}_std_ready")
            t_ready, t_read = sem(f"{tag}_t_ready"), sem(f"{tag}_t_read")
            n_in = (1 if res_dram is not None else 0) + (1 if bias_dram is not None else 0) + (1 if o_src is None else 0)

            with nc.Block() as block:
                @block.sync
                def _(sp):
                    if o_src is None:
                        sp.dma_start(o_sb[:], o_dram.rearrange("g p t -> p g t")).then_inc(s_in, 16)
                    if res_dram is not None:
                        sp.dma_start(x_sb[:], res_dram.rearrange("(n p) d -> p n d", p=P)).then_inc(s_in, 16)
                    if bias_dram is not None:
                        sp.dma_start(b_sb[:], bias_dram.rearrange("(a n) -> a n", a=1).to_broadcast([P, D])).then_inc(s_in, 16)
                    sp.wait_ge(s_wz, 1)
                    for j in range(GH):
                        sp.dma_start(w_sb[32 * j:32 * j + DK], w_dram.rearrange("(g h i) n -> h i g n", g=NG, h=GH)[j]).then_inc(s_w, 16)
                    for dst, src, s in extra:
                        sp.dma_start(dst, src).then_inc(s, 16)

                @block.gpsimd
                def _(pool):
                    nc.gpsimd.memset(w_sb[:], 0.0).then_inc(s_wz, 1)
                    if bias_dram is not None:
                        pool.wait_ge(s_in, 16 * n_in)
                        for n in range(NT):
                            nc.gpsimd.tensor_tensor(x_sb[:, n], x_sb[:, n], b_sb[:], ALU.add).then_inc(res_ready, 1)

                @block.tensor
                def _(pe):
                    if n_in:
                        pe.wait_ge(s_in, 16 * n_in)
                    pe.wait_ge(s_w, 16 * GH)
                    for n in range(NT):
                        if n >= 2:
                            pe.wait_ge(y_read, n - 1)
                        for g in range(NG):
                            mm = nc.tensor.matmul(py[:, n % 2, 0:D], o_sb[:, g, n * P:(n + 1) * P], w_sb[:, g], start=(g == 0), stop=(g == NG - 1))
                        mm.then_inc(y_ready, 1)
                    for n in range(KD * NC):
                        k, c = n % KD, n // KD
                        if n >= 2:
                            pe.wait_ge(t_read, n - 1)
                        pe.wait_ge(normed, 4 * (c + 1))
                        for q in range(4):
                            mm = nc.tensor.transpose(pt[:, n % 2, q * P:(q + 1) * P], x_sb[:, 4 * c + q, k * P:(k + 1) * P], ident[:])
                        mm.then_inc(t_ready, 1)

                @block.scalar
                def _(act):
                    act.wait_ge(var_ready, 1)
                    nc.scalar.activation(rstd[:], rstd[:], ACT.Sqrt).then_inc(std_ready, 1)
                    for n in range(KD * NC):
                        k, c = n % KD, n // KD
                        act.wait_ge(t_ready, n + 1)
                        nc.scalar.copy(xT_sb[:, k, c * C:(c + 1) * C], pt[:, n % 2]).then_inc(t_read, 1)

                @block.vector
                def _(dve):
                    norm_tiles(dve, tag, x_sb, stats, mv, rstd, var_ready, std_ready, normed, y_ready, y_read,
                               res_ready if bias_dram is not None else None, lambda n: py[:, n % 2, 0:D])

        def norm_tiles(dve, tag, x_sb, stats, mv, rstd, var_ready, std_ready, normed, y_ready, y_read, res_ready, y_of):
            link = chain(dve, f"{tag}_norm_chain")
            for n in range(NT):
                dve.wait_ge(y_ready, n + 1)
                if res_ready is not None:
                    dve.wait_ge(res_ready, n + 1)
                nc.vector.tensor_tensor(x_sb[:, n], y_of(n), x_sb[:, n], ALU.add).then_inc(y_read, 1)
                if n:
                    dve.wait_ge(y_read, n)
                    nc.vector.bn_stats(stats[:, n - 1], x_sb[:, n - 1])
            dve.wait_ge(y_read, NT)
            link(nc.vector.bn_stats(stats[:, NT - 1], x_sb[:, NT - 1]))
            for n in range(NT):
                last = nc.vector.bn_aggr(mv[:, n], stats[:, n])
            link(last)
            nc.vector.tensor_scalar_add(rstd[:], mv[:, :, 1], EPS).then_inc(var_ready, 1)
            dve.wait_ge(std_ready, 1)
            link(nc.vector.reciprocal(rstd[:], rstd[:]))
            for n in range(NT):
                nc.vector.tensor_scalar(x_sb[:, n], x_sb[:, n], mv[:, n, 0:1], rstd[:, n:n + 1],
                                        ALU.subtract, ALU.mult).then_inc(normed, 1)

        tail = ExitStack()
        with tail:
            x_sb = sb(tail, "x_sb", [P, NT, D])
            w1_sb = sb(tail, "w1_sb", [P, KD, W])
            w2_sb = sb(tail, "w2_sb", [P, WT, D])
            rw_sb = sb(tail, "rw_sb", [P, KD, E])
            stage = ExitStack()
            with stage:
                x1T = sb(stage, "x1T", [P, KD, T])
                ctx2 = sb(stage, "ctx2", [P, KD, M])
                xwq_sb = sb(stage, "xwq_sb", [P, KD, D])
                s_ctx2 = sem("ctx2_in")
                inner = ExitStack()
                with inner:
                    project_norm("n1", inner, None, o_dram, wo, x, bo, x_sb, x1T,
                                 [(ctx2[:], kt_view(ctxT), s_ctx2), (xwq_sb[:], kt_view(xwq), s_ctx2)])

                inner = ExitStack()
                with inner:
                    parts = sb(inner, "xparts_sb", [P, 2, 3, C], BF16)
                    rest = sb(inner, "xrest_sb", [P, C])
                    qp = sb(inner, "qp", [P, KD, T])
                    iota_sb = sb(inner, "iota_sb", [P, M])
                    near = sb(inner, "near", [P, 2, M])
                    best = sb(inner, "best", [P, 2, 8])
                    place = sb(inner, "place", [P, 2, 8], U32)
                    place_f = sb(inner, "place_f", [P, 2, 1])
                    chosen = sb(inner, "chosen", [P, 2, MP], BF16)
                    ones_b = sb(inner, "ones_b", [P, 1], BF16)
                    zeros_b = sb(inner, "zeros_b", [P, P], BF16)
                    count = sb(inner, "count", [P, MT])
                    absent = sb(inner, "absent", [P, MT])
                    pp = psum(inner, "pp", [P, 4, C])
                    pq = psum(inner, "pq2", [P, 2, C])
                    pc = psum(inner, "pc", [P, C])
                    pa = psum(inner, "pa", [P, C])
                    s_iota, set2 = sem("iota_in"), sem("set2")
                    s_xout = [sem(f"xparts_out{i}") for i in range(2)]
                    q_ready, q_copied, xp1, xrest, xp2, xp3 = (
                        sem("xq_ready"), sem("xq_copied"), sem("xp1"), sem("xrest"), sem("xp2"), sem("xp3"))
                    near_ready, near_copied, chosen_ready, counted = (
                        sem("near_ready"), sem("near_copied"), sem("chosen_ready"), sem("counted"))
                    absent_ready, absent_turned, mask_ready, mask_in = (
                        sem("absent_ready"), sem("absent_turned"), sem("mask_ready"), sem("mask_in"))
                    near_used = sem("near_used")
                    qunits = [(m, c) for c in range(NC) for m in range(KD)]
                    cols = [(a, min(a + C, M)) for a in range(0, M, C)]

                    with nc.Block() as block:
                        @block.sync
                        def _(sp):
                            sp.dma_start(iota_sb[:], iota).then_inc(s_iota, 16)
                            for n, (m, c) in enumerate(qunits):
                                sp.wait_ge(xp3, n + 1)
                                sp.dma_start(xparts[:, m * P:(m + 1) * P, c * C:(c + 1) * C].rearrange("r p t -> p r t"),
                                             parts[:, n % 2]).then_inc(s_xout[n % 2], 16)
                            sp.wait_ge(mask_ready, 1)
                            sp.dma_start(kx[KS:KS + 1, :].rearrange("o (n t) -> o n t", t=P), maskx[:]).then_inc(mask_in, 16)
                            sp.wait_ge(mask_in, 16)
                            for i in range(2):
                                sp.wait_ge(s_xout[i], 8 * len(qunits))

                        @block.gpsimd
                        def _(pool):
                            nc.gpsimd.memset(ones_b[:], 1.0).then_inc(set2, 1)
                            nc.gpsimd.memset(zeros_b[:], 0.0).then_inc(set2, 1)
                            nc.gpsimd.memset(chosen[:], 0.0).then_inc(set2, 1)

                        @block.tensor
                        def _(pe):
                            pe.wait_ge(s_ctx2, 32)
                            for n, (m, c) in enumerate(qunits):
                                if n >= 2:
                                    pe.wait_ge(xrest, n - 1)
                                for k in range(KD):
                                    mm = nc.tensor.matmul(pq[:, n % 2], xwq_sb[:, k, m * P:(m + 1) * P], x1T[:, k, c * C:(c + 1) * C],
                                                          start=(k == 0), stop=(k == KD - 1))
                                mm.then_inc(q_ready, 1)
                            pe.wait_ge(set2, 3)
                            nc.tensor.matmul(pc[:, 0:MT], zeros_b[:], zeros_b[:, 0:MT], start=True, stop=False, skip_group_check=True)

                            def tally(n):
                                pe.wait_ge(chosen_ready, n + 1)
                                for t in range(MT):
                                    mm = nc.tensor.matmul(pc[:, t:t + 1], chosen[:, n % 2, t * P:(t + 1) * P], ones_b[:],
                                                          start=False, stop=(n == NT - 1 and t == MT - 1), skip_group_check=True)
                                mm.then_inc(counted, 1)

                            pe.wait_ge(q_copied, len(qunits))
                            u = 0
                            for n in range(NT):
                                for a, b in cols:
                                    if u >= 4:
                                        pe.wait_ge(near_copied, u - 3)
                                    for k in range(KD):
                                        mm = nc.tensor.matmul(pp[:, u % 4, 0:b - a], qp[:, k, n * P:(n + 1) * P], ctx2[:, k, a:b],
                                                              start=(k == 0), stop=(k == KD - 1))
                                    mm.then_inc(near_ready, 1)
                                    u += 1
                                if n:
                                    tally(n - 1)
                            tally(NT - 1)
                            pe.wait_ge(absent_ready, 1)
                            nc.tensor.transpose(pa[0:MT, 0:P], absent[:], ident[:]).then_inc(absent_turned, 1)

                        @block.scalar
                        def _(act):
                            for n, (m, c) in enumerate(qunits):
                                act.wait_ge(q_ready, n + 1)
                                nc.scalar.copy(qp[:, m, c * C:(c + 1) * C], pq[:, n % 2]).then_inc(q_copied, 1)
                                if n >= 2:
                                    act.wait_ge(s_xout[n % 2], 16 * (n // 2))
                                nc.scalar.copy(parts[:, n % 2, 0], pq[:, n % 2]).then_inc(xp1, 1)
                                act.wait_ge(xrest, n + 1)
                                nc.scalar.copy(parts[:, n % 2, 1], rest[:]).then_inc(xp2, 1)
                            u = 0
                            for n in range(NT):
                                for a, b in cols:
                                    act.wait_ge(near_ready, u + 1)
                                    if n >= 2:
                                        act.wait_ge(near_used, n - 1)
                                    nc.scalar.copy(near[:, n % 2, a:b], pp[:, u % 4, 0:b - a]).then_inc(near_copied, 1)
                                    u += 1

                        @block.vector
                        def _(dve):
                            link = chain(dve, "choose_chain")
                            for n in range(len(qunits)):
                                dve.wait_ge(xp1, n + 1)
                                if n:
                                    dve.wait_ge(xp3, n)
                                nc.vector.tensor_tensor(rest[:], pq[:, n % 2], parts[:, n % 2, 0], ALU.subtract).then_inc(xrest, 1)
                                dve.wait_ge(xp2, n + 1)
                                nc.vector.tensor_tensor(parts[:, n % 2, 2], rest[:], parts[:, n % 2, 1], ALU.subtract).then_inc(xp3, 1)
                            dve.wait_ge(s_iota, 16)
                            dve.wait_ge(set2, 3)
                            for n in range(NT):
                                dve.wait_ge(near_copied, len(cols) * (n + 1))
                                link(nc.vector.max(best[:, n % 2], near[:, n % 2]))
                                nc.vector.max_index(place[:, n % 2], best[:, n % 2], near[:, n % 2]).then_inc(near_used, 1)
                                dve.wait_ge(near_used, n + 1)
                                link(nc.vector.tensor_copy(place_f[:, n % 2], place[:, n % 2, 0:1]))
                                if n >= 2:
                                    dve.wait_ge(counted, n - 1)
                                nc.vector.tensor_scalar(chosen[:, n % 2, 0:M], iota_sb[:], place_f[:, n % 2], None,
                                                        ALU.is_equal).then_inc(chosen_ready, 1)
                            dve.wait_ge(counted, NT)
                            link(nc.vector.tensor_copy(count[:], pc[:, 0:MT]))
                            nc.vector.tensor_scalar(absent[:], count[:], 0.0, MASKED, ALU.is_equal, ALU.mult).then_inc(absent_ready, 1)
                            for t in range(MT):
                                last = nc.vector.tensor_scalar(vx[:, t], vx[:, t], count[:, t:t + 1], None, ALU.mult)
                            link(last)
                            dve.wait_ge(absent_turned, 1)
                            nc.vector.tensor_copy(maskx[:], pa[0:MT, 0:P]).then_inc(mask_ready, 1)

            o_cross = sb(tail, "o_cross", [P, NG, T])
            stage = ExitStack()
            with stage:
                stackx = sb(stage, "stackx", [P, NC, H, C], BF16)
                loads = [([(stackx[n * DK:(n + 1) * DK, c], xparts[a, :, c * C:(c + 1) * C].rearrange("(h i) t -> i h t", i=DK))
                           for n, (a, _) in enumerate(PAIRS)], c) for c in range(NC)]
                steps, works = [], []
                PW = MP // 4
                for c in range(NC):
                    for g in range(NG):
                        u = c * NG + g
                        pieces = [dict(w=PW, lhsT=stackx[0:KS + 1, c, g * GH + j, q * P:(q + 1) * P],
                                       rhs=kx[0:KS + 1, n * PW:(n + 1) * PW], row=j * 4 + q, at=n, diag=False, load=c + 1)
                                  for j in range(GH) for q in range(4) for n in range(4)]
                        works.append(dict(pieces=pieces, rows=GH * 4, spare=3,
                                          shift_to=[stackx[KS + 1 + b:KS + 2 + b, c, g * GH:(g + 1) * GH, :].rearrange("o h (n t) -> o (h n) t", t=P) for b in range(2)]))
                        for t in range(MT):
                            steps.append(dict(unit=u, chunk=u, off=0, diag=0, first=t == 0, last=t == MT - 1,
                                              keys=lambda j, t=t: kx[0:KS + 3, t * P:(t + 1) * P],
                                              queries=lambda j, g=g, c=c: stackx[0:KS + 3, c, g * GH + j, :],
                                              values=lambda j, t=t: vx[:, t, :]))
                attention("cross", stage, steps, works, KS + 1, [stackx[KS:KS + 1]], loads,
                          [(w1_sb[:], kt_view(w1)), (w2_sb[:], kt_view(w2)), (rw_sb[:], kt_view(rw))],
                          lambda cc: o_cross[:, cc % NG, (cc // NG) * C:(cc // NG + 1) * C], None)

            x2T = sb(tail, "x2T", [P, KD, T])
            inner = ExitStack()
            with inner:
                project_norm("n2", inner, o_cross, None, xwc, None, None, x_sb, x2T, [])

            gate = sb(tail, "gate", [P, NT, E])
            top8 = sb(tail, "top8", [P, NT, 8])
            at8 = sb(tail, "at8", [P, NT, 8], U32)
            at_f = sb(tail, "at_f", [P, NT, 2])
            total = sb(tail, "total", [P, NT])
            mix = sb(tail, "mix", [P, NT, E])
            hot = sb(tail, "hot", [P, E])
            iota8 = sb(tail, "iota8", [P, E])
            hid = sb(tail, "hid", [P, WT, C])
            relu = sb(tail, "relu", [P, 3, C])
            stats = sb(tail, "n3_stats", [P, NT, 6])
            mv = sb(tail, "n3_mv", [P, NT, 2])
            rstd = sb(tail, "n3_rstd", [P, NT])
            pr = psum(tail, "pr", [P, NT, E])
            ph = psum(tail, "ph", [P, 3, C])
            py = psum(tail, "py", [P, 4, C])
            s_i8, r_ready, e_ready, h_ready, h_read = (sem("iota8_in"), sem("r_ready"), sem("e_ready"), sem("h_ready"), sem("h_read"))
            y_ready, y_read, hid_ready, s_out, normed = (sem("y_ready"), sem("y_read"), sem("hid_ready"), sem("out_done"), sem("n3_normed"))
            var_ready, std_ready = sem("n3_var_ready"), sem("n3_std_ready")
            starts = [sum(WIDTHS[:e]) // P for e in range(E + 1)]

            with nc.Block() as block:
                @block.sync
                def _(sp):
                    sp.dma_start(iota8[:], iota[:, 0:E]).then_inc(s_i8, 16)
                    for n in range(NT):
                        sp.wait_ge(normed, n + 1)
                        sp.dma_start(out[n * P:(n + 1) * P, :], x_sb[:, n]).then_inc(s_out, 16)
                    sp.wait_ge(s_out, 16 * NT)

                @block.tensor
                def _(pe):
                    for n in range(NT):
                        for k in range(KD):
                            mm = nc.tensor.matmul(pr[:, n], x2T[:, k, n * P:(n + 1) * P], rw_sb[:, k], start=(k == 0), stop=(k == KD - 1))
                    mm.then_inc(r_ready, 1)
                    u = y = 0
                    for c in range(NC):
                        for w in range(WT):
                            if u >= 3:
                                pe.wait_ge(h_read, u - 2)
                            for k in range(KD):
                                mm = nc.tensor.matmul(ph[:, u % 3], w1_sb[:, k, w * P:(w + 1) * P], x2T[:, k, c * C:(c + 1) * C],
                                                      start=(k == 0), stop=(k == KD - 1))
                            mm.then_inc(h_ready, 1)
                            u += 1
                        for q in range(4):
                            for e in range(E):
                                pe.wait_ge(hid_ready, c * WT + starts[e + 1])
                                if y >= 4:
                                    pe.wait_ge(y_read, y - 3)
                                for w in range(starts[e], starts[e + 1]):
                                    mm = nc.tensor.matmul(py[:, y % 4, 0:D], hid[:, w, q * P:(q + 1) * P], w2_sb[:, w],
                                                          start=(w == starts[e]), stop=(w == starts[e + 1] - 1))
                                mm.then_inc(y_ready, 1)
                                y += 1

                @block.scalar
                def _(act):
                    act.wait_ge(r_ready, 1)
                    nc.scalar.activation(gate[:], pr[:], ACT.Exp, scale=-1.0).then_inc(e_ready, 1)
                    for u in range(NC * WT):
                        act.wait_ge(h_ready, u + 1)
                        if u >= 3:
                            act.wait_ge(hid_ready, u - 2)
                        nc.scalar.activation(relu[:, u % 3], ph[:, u % 3], ACT.Relu).then_inc(h_read, 1)
                    act.wait_ge(var_ready, 1)
                    nc.scalar.activation(rstd[:], rstd[:], ACT.Sqrt).then_inc(std_ready, 1)

                @block.vector
                def _(dve):
                    link = chain(dve, "ffn_chain")
                    dve.wait_ge(e_ready, 1)
                    dve.wait_ge(s_i8, 16)
                    link(nc.vector.tensor_scalar_add(gate[:], gate[:], 1.0))
                    link(nc.vector.reciprocal(gate[:], gate[:]))
                    for n in range(NT):
                        last = nc.vector.max(top8[:, n], gate[:, n])
                    link(last)
                    for n in range(NT):
                        last = nc.vector.max_index(at8[:, n], top8[:, n], gate[:, n])
                    link(last)
                    link(nc.vector.tensor_copy(at_f[:], at8[:, :, 0:2]))
                    link(nc.vector.tensor_tensor(total[:], top8[:, :, 0], top8[:, :, 1], ALU.add))
                    link(nc.vector.tensor_scalar_add(total[:], total[:], 1e-20))
                    link(nc.vector.reciprocal(total[:], total[:]))
                    for n in range(NT):
                        link(nc.vector.tensor_scalar(top8[:, n, 0:2], top8[:, n, 0:2], total[:, n:n + 1], None, ALU.mult))
                        link(nc.vector.tensor_scalar(hot[:], iota8[:], at_f[:, n, 0:1], top8[:, n, 0:1], ALU.is_equal, ALU.mult))
                        link(nc.vector.tensor_scalar(mix[:, n], iota8[:], at_f[:, n, 1:2], top8[:, n, 1:2], ALU.is_equal, ALU.mult))
                        link(nc.vector.tensor_tensor(mix[:, n], mix[:, n], hot[:], ALU.add))
                    u = y = 0
                    for c in range(NC):
                        for w in range(WT):
                            dve.wait_ge(h_read, u + 1)
                            if w == 0 and c:
                                dve.wait_ge(y_ready, y)
                            nc.vector.tensor_tensor(hid[:, w], relu[:, u % 3], relu[:, u % 3], ALU.mult).then_inc(hid_ready, 1)
                            u += 1
                        for q in range(4):
                            for e in range(E):
                                n = 4 * c + q
                                dve.wait_ge(y_ready, y + 1)
                                if y:
                                    dve.wait_ge(y_read, y)
                                nc.vector.scalar_tensor_tensor(out=x_sb[:, n], in0=py[:, y % 4, 0:D], scalar=mix[:, n, e:e + 1],
                                                               in1=x_sb[:, n], op0=ALU.mult, op1=ALU.add).then_inc(y_read, 1)
                                y += 1
                    dve.wait_ge(y_read, y)
                    for n in range(NT):
                        last = nc.vector.bn_stats(stats[:, n], x_sb[:, n])
                    link(last)
                    for n in range(NT):
                        last = nc.vector.bn_aggr(mv[:, n], stats[:, n])
                    link(last)
                    nc.vector.tensor_scalar_add(rstd[:], mv[:, :, 1], EPS).then_inc(var_ready, 1)
                    dve.wait_ge(std_ready, 1)
                    link(nc.vector.reciprocal(rstd[:], rstd[:]))
                    for n in range(NT):
                        nc.vector.tensor_scalar(x_sb[:, n], x_sb[:, n], mv[:, n, 0:1], rstd[:, n:n + 1],
                                                ALU.subtract, ALU.mult).then_inc(normed, 1)


def kernel(x, ctx_1024, L0_attn_WQ_w, L0_attn_WQ_b, L0_attn_WK_w, L0_attn_WK_b, L0_attn_WV_w, L0_attn_WV_b, L0_attn_Wo_w,
           L0_attn_Wo_b, L0_xattn_Wq, L0_xattn_Wkv, L0_xattn_Wc, L0_ffn_router_w, L0_ffn_w1, L0_ffn_w2):
    import numpy as np
    import concourse.bacc as bacc
    from concourse.bass_utils import run_bass_kernel_spmd

    half = DK // 2
    swap = np.arange(D).reshape(H, 2, half)[:, ::-1].reshape(D)
    freq = (1.0 / 10000.0 ** (2.0 * np.arange(half, dtype=np.float32) / DK)).astype(np.float32)
    angle = np.arange(T, dtype=np.float32)[:, None] * freq[None, :]
    cos = np.tile(np.cos(angle).T, (2 * P // DK, 1)).astype(np.float32)
    sin = np.tile(np.concatenate([-np.sin(angle).T, np.sin(angle).T]), (P // DK, 1)).astype(np.float32)
    rows = np.arange(P)
    sums = (rows[:, None] == 32 * (rows[None, :] // 32) + DK).astype(np.float32)
    tri = np.where(np.arange(P)[None, :] > rows[:, None], np.float32(MASKED), np.float32(0.0))
    causal = np.concatenate([np.zeros((P, C - P), np.float32), tri], 1)
    data = dict(
        x=x[0], xT=x[0].T, ctxT=ctx_1024[0].T,
        wq=L0_attn_WQ_w.T, wqs=L0_attn_WQ_w[swap].T, bq=L0_attn_WQ_b.reshape(KD, P).T, bqs=L0_attn_WQ_b[swap].reshape(KD, P).T,
        wk=L0_attn_WK_w.T, wks=L0_attn_WK_w[swap].T, bk=L0_attn_WK_b.reshape(KD, P).T, bks=L0_attn_WK_b[swap].reshape(KD, P).T,
        wv=L0_attn_WV_w.T, bv=L0_attn_WV_b, wo=L0_attn_Wo_w.T, bo=L0_attn_Wo_b,
        xwq=L0_xattn_Wq.T, xwk=L0_xattn_Wkv[:DK].T, xwv=L0_xattn_Wkv[DK:].T, xwc=L0_xattn_Wc.T,
        rw=L0_ffn_router_w.T, w1=L0_ffn_w1, w2=L0_ffn_w2,
        cosT=cos, sinT=sin, identity=np.eye(P, dtype=np.float32), sums=sums, causal=causal,
        iota=np.tile(np.arange(M, dtype=np.float32), (P, 1)))
    nc = bacc.Bacc("TRN2", target_bir_lowering=False, num_devices=1)
    arrays, args = {}, {}
    for name, a in data.items():
        a = np.ascontiguousarray(a)
        arrays[f"in_{name}"] = a
        args[name] = nc.dram_tensor(f"in_{name}", a.shape, mybir.dt.from_np(a.dtype), kind="ExternalInput").ap()
    out = nc.dram_tensor("out_0", (T, D), F32, kind="ExternalOutput").ap()
    decoder_layer(nc, out=out, **args)
    got = run_bass_kernel_spmd(nc, [arrays], core_ids=[0])
    return got.results[0]["out_0"].reshape(1, T, D)
```

```python
import concourse.bass as bass
from concourse import mybir
from contextlib import ExitStack

F32 = mybir.dt.float32
BF16 = mybir.dt.bfloat16
U32 = mybir.dt.uint32
I32 = mybir.dt.int32
ALU = mybir.AluOpType
ACT = mybir.ActivationFunctionType
AX = mybir.AxisListType

P = 128
T = 2048
D = 256
H = 16
DK = D // H
KD = D // P
NT = T // P
C = 512
NC = T // C
GH = 4
NG = H // GH
M = 1601
MT = -(-M // P)
MP = MT * P
FEW = 512
E = 8
WIDTHS = [256] * 4 + [512] * 4
W = sum(WIDTHS)
WT = W // P
PAIRS = [(0, 0), (0, 1), (1, 0), (0, 2), (2, 0), (1, 1)]
KS = len(PAIRS) * DK
VW = DK + 1
UR = GH * C // P
SB = 3
LEAD = 4
EVEN = 4
LOW = -3.0e38
MASKED = -1.0e30
SCALE = DK ** -0.5
EPS = 1e-5


class Count:

    def __init__(self, sem):
        self.sem, self.n = sem, 0

    def inc(self, ins, by=1):
        ins.then_inc(self.sem, by)
        self.n += by
        return self.n


def decoder_layer(nc, x, xT, ctxT, wq, wqs, bq, bqs, wk, wks, bk, bks, wv, bv, wo, bo, xwq, xwkv, xwc, rw, w1, w2,
                  cosT, sinT, identity, below, causal, iota, out):
    top = ExitStack()
    made = [0]

    def sem(name):
        return top.enter_context(nc.semaphore(name))

    def sb(scope, name, shape, dt=F32):
        return scope.enter_context(nc.sbuf_tensor(name, shape, dt))

    def psum(scope, name, shape, dt=F32):
        return scope.enter_context(nc.psum_tensor(name, shape, dt))

    def chain(eng, name):
        done = Count(sem(name))

        def link(ins):
            eng.wait_ge(done.sem, done.inc(ins))

        return link

    def o_unit(g, c):
        return o_tok[:, c * C // P:(c + 1) * C // P, g * GH * DK:(g + 1) * GH * DK].rearrange("p q (j i) -> p q j i", i=DK)

    def kt_view(w):
        return w.rearrange("(k p) n -> p k n", p=P)

    with top:
        qparts = nc.dram_tensor("qparts", [3, D, T], BF16).ap()
        kparts = nc.dram_tensor("kparts", [3, D, T], BF16).ap()
        xparts = nc.dram_tensor("xparts", [3, D, T], BF16).ap()

        ident = sb(top, "ident", [P, P])
        zeros = sb(top, "zeros", [P, C])
        kx = sb(top, "kx", [P, MP], BF16)
        kvx = sb(top, "kvx", [P, MT, DK + VW])
        kx_few = sb(top, "kx_few", [P, FEW], BF16)
        vx_few = sb(top, "vx_few", [P, FEW // P, VW])
        few = sb(top, "few", [P, 1], I32)
        o_tok = sb(top, "o_tok", [P, NT, D])
        maskx = sb(top, "maskx", [MT, P], BF16)

        consts_in = sem("consts_in")

        att = ExitStack()
        with att:
            V = sb(att, "V", [P, NT, H, VW])
            stage = ExitStack()
            with stage:
                xT_sb = sb(stage, "xT_sb", [P, KD, T])
                w_sb = sb(stage, "w_sb", [P, 5, KD, D])
                ctx_sb = sb(stage, "ctx_sb", [P, KD, M])
                wkv_sb = sb(stage, "wkv_sb", [P, KD, 2 * DK])
                cs = sb(stage, "cs", [P, 2, T])
                bias = sb(stage, "bias", [P, 4, KD])
                bv_all = sb(stage, "bv_all", [P, D])
                parts = sb(stage, "parts", [P, 2, 3, C], BF16)
                rest = sb(stage, "rest", [P, 2, C])
                turned = sb(stage, "turned", [P, 2, 2, C])
                whole = sb(stage, "whole", [P, 2, C])
                mk = sb(stage, "mk", [DK, MP])
                mk_rest = sb(stage, "mk_rest", [DK, MP])
                mk_parts = sb(stage, "mk_parts", [DK, 3, MP], BF16)
                pq = psum(stage, "pq", [P, 2, 2, C])
                pv = psum(stage, "pv", [P, 2, C])
                pk = psum(stage, "pk", [P, 2, C])

                s_x, s_w, s_b, s_ctx = sem("x_in"), sem("weights_in"), sem("bias_in"), sem("ctx_in")
                s_ones, s_mk_out = sem("ones_set"), sem("mk_out")
                s_parts_out = [sem(f"parts_out{i}") for i in range(2)]
                qk_ready, qk_read = sem("qk_ready"), sem("qk_read")
                v_ready, v_read = sem("v_ready"), sem("v_read")
                mk_ready, mv_ready, mv_read = sem("mk_ready"), sem("mv_ready"), sem("mv_read")
                whole_ready, p1_ready, rest_ready, p2_ready, p3_ready = (
                    sem("whole_ready"), sem("p1_ready"), sem("rest_ready"), sem("p2_ready"), sem("p3_ready"))
                mk_copied, mk1, mkr, mk2, mk3 = (sem("mk_copied"), sem("mk1"), sem("mkr"), sem("mk2"), sem("mk3"))
                units = [(t, m, c) for t in range(2) for m in range(KD) for c in range(NC)]
                mk_cols = [(a, min(a + C, M)) for a in range(0, M, C)]

                with nc.Block() as block:
                    @block.sync
                    def _(sp):
                        sp.dma_start(xT_sb[:], kt_view(xT)).then_inc(s_x, 16)
                        for n, w in enumerate((wq, wqs, wk, wks, wv)):
                            sp.dma_start(w_sb[:, n], kt_view(w)).then_inc(s_w, 16)
                        sp.dma_start(cs[:, 0], cosT).then_inc(s_b, 16)
                        sp.dma_start(cs[:, 1], sinT).then_inc(s_b, 16)
                        for n, b in enumerate((bq, bqs, bk, bks)):
                            sp.dma_start(bias[:, n], b).then_inc(s_b, 16)
                        sp.dma_start(bv_all[:], bv.rearrange("(a n) -> a n", a=1).to_broadcast([P, D])).then_inc(s_b, 16)
                        sp.dma_start(ctx_sb[:], kt_view(ctxT)).then_inc(s_ctx, 16)
                        sp.dma_start(wkv_sb[:], kt_view(xwkv)).then_inc(s_ctx, 16)
                        sp.dma_start(ident[:], identity).then_inc(consts_in, 16)
                        for n, (t, m, c) in enumerate(units):
                            dst = (qparts, kparts)[t][:, m * P:(m + 1) * P, c * C:(c + 1) * C].rearrange("r p t -> p r t")
                            sp.wait_ge(p3_ready, n + 1)
                            sp.dma_start(dst, parts[:, n % 2]).then_inc(s_parts_out[n % 2], 16)
                        sp.wait_ge(mk3, 1)
                        for n, (_, b) in enumerate(PAIRS):
                            sp.dma_start(kx[n * DK:(n + 1) * DK, :], mk_parts[:, b]).then_inc(s_mk_out, 16)
                        for i in range(2):
                            sp.wait_ge(s_parts_out[i], 8 * len(units))
                        sp.wait_ge(s_mk_out, 16 * len(PAIRS))
                        sp.wait_ge(consts_in, 16)

                    @block.gpsimd
                    def _(pool):
                        nc.gpsimd.memset(V[:, :, :, DK:VW], 1.0).then_inc(s_ones, 1)
                        nc.gpsimd.memset(zeros[:], 0.0).then_inc(s_ones, 1)
                        nc.gpsimd.memset(kvx[:], 0.0).then_inc(s_ones, 1)
                        pool.wait_ge(s_ones, 3)
                        nc.gpsimd.memset(kx[KS:KS + 3, :], 1.0).then_inc(s_ones, 1)
                        pool.wait_ge(s_ones, 4)
                        nc.gpsimd.memset(mk[:], 0.0).then_inc(s_ones, 1)
                        pool.wait_ge(s_ones, 5)

                    @block.tensor
                    def _(pe):
                        pe.wait_ge(s_x, 16)
                        pe.wait_ge(s_w, 16 * 5)
                        for n, (t, m, c) in enumerate(units):
                            if n >= 2:
                                pe.wait_ge(qk_read, n - 1)
                            for s in range(2):
                                for k in range(KD):
                                    last = nc.tensor.matmul(pq[:, n % 2, s], w_sb[:, 2 * t + s, k, m * P:(m + 1) * P],
                                                            xT_sb[:, k, c * C:(c + 1) * C], start=(k == 0), stop=(k == KD - 1))
                            last.then_inc(qk_ready, 1)
                            if n == 0:
                                pe.wait_ge(s_ctx, 32)
                            if n >= 2:
                                pe.wait_ge(v_read, n - 1)
                            for k in range(KD):
                                last = nc.tensor.matmul(pv[:, n % 2, 0:D], xT_sb[:, k, n * P:(n + 1) * P], w_sb[:, 4, k, :],
                                                        start=(k == 0), stop=(k == KD - 1))
                            last.then_inc(v_ready, 1)
                        for n, (a, b) in enumerate(mk_cols):
                            if n >= 2:
                                pe.wait_ge(mk_copied, n - 1)
                            for k in range(KD):
                                last = nc.tensor.matmul(pk[0:DK, n % 2, 0:b - a], wkv_sb[:, k, 0:DK], ctx_sb[:, k, a:b],
                                                        start=(k == 0), stop=(k == KD - 1))
                            last.then_inc(mk_ready, 1)
                        for n in range(MT):
                            rows = min(P, M - n * P)
                            pe.wait_ge(v_read, NT - 1 + (n % 2) if n < 2 else NT)
                            if n >= 2:
                                pe.wait_ge(mv_read, n - 1)
                            for k in range(KD):
                                last = nc.tensor.matmul(pv[0:rows, n % 2, 0:2 * DK], ctx_sb[:, k, n * P:n * P + rows],
                                                        wkv_sb[:, k, :], start=(k == 0), stop=(k == KD - 1))
                            last.then_inc(mv_ready, 1)

                    @block.scalar
                    def _(act):
                        for n in range(len(units)):
                            act.wait_ge(whole_ready, n + 1)
                            if n >= 2:
                                act.wait_ge(s_parts_out[n % 2], 16 * (n // 2))
                            nc.scalar.copy(parts[:, n % 2, 0], whole[:, n % 2]).then_inc(p1_ready, 1)
                            act.wait_ge(rest_ready, n + 1)
                            nc.scalar.copy(parts[:, n % 2, 1], rest[:, n % 2]).then_inc(p2_ready, 1)
                        act.wait_ge(s_ones, 5)
                        for n, (a, b) in enumerate(mk_cols):
                            act.wait_ge(mk_ready, n + 1)
                            nc.scalar.copy(mk[:, a:b], pk[0:DK, n % 2, 0:b - a]).then_inc(mk_copied, 1)
                        act.wait_ge(mk_copied, len(mk_cols))
                        nc.scalar.copy(mk_parts[:, 0], mk[:]).then_inc(mk1, 1)
                        act.wait_ge(mkr, 1)
                        nc.scalar.copy(mk_parts[:, 1], mk_rest[:]).then_inc(mk2, 1)

                    @block.vector
                    def _(dve):
                        link = chain(dve, "rope_chain")
                        dve.wait_ge(s_b, 16 * 7)
                        for n in range(len(units) + 1):
                            if n < len(units):
                                t, m, c = units[n]
                                dve.wait_ge(qk_ready, n + 1)
                                if n >= 2:
                                    dve.wait_ge(p1_ready, n - 1)
                                for s in range(2):
                                    last = nc.vector.scalar_tensor_tensor(
                                        out=turned[:, n % 2, s], in0=pq[:, n % 2, s], scalar=bias[:, 2 * t + s, m:m + 1],
                                        in1=cs[:, s, c * C:(c + 1) * C], op0=ALU.add, op1=ALU.mult)
                                last.then_inc(qk_read, 1)
                                dve.wait_ge(v_ready, n + 1)
                                nc.vector.tensor_tensor(V[:, n, :, 0:DK], pv[:, n % 2, 0:D].rearrange("p (h d) -> p h d", h=H),
                                                        bv_all[:].rearrange("p (h d) -> p h d", h=H), ALU.add).then_inc(v_read, 1)
                                dve.wait_ge(qk_read, n + 1)
                                nc.vector.tensor_tensor(whole[:, n % 2], turned[:, n % 2, 0], turned[:, n % 2, 1], ALU.add).then_inc(whole_ready, 1)
                            if n:
                                dve.wait_ge(p2_ready, n)
                                nc.vector.tensor_tensor(parts[:, (n - 1) % 2, 2], rest[:, (n - 1) % 2], parts[:, (n - 1) % 2, 1], ALU.subtract).then_inc(p3_ready, 1)
                            if n < len(units):
                                dve.wait_ge(p1_ready, n + 1)
                                nc.vector.tensor_tensor(rest[:, n % 2], whole[:, n % 2], parts[:, n % 2, 0], ALU.subtract).then_inc(rest_ready, 1)
                        dve.wait_ge(mk1, 1)
                        nc.vector.tensor_tensor(mk_rest[:], mk[:], mk_parts[:, 0], ALU.subtract).then_inc(mkr, 1)
                        dve.wait_ge(mk2, 1)
                        nc.vector.tensor_tensor(mk_parts[:, 2], mk_rest[:], mk_parts[:, 1], ALU.subtract).then_inc(mk3, 1)
                        dve.wait_ge(s_ones, 5)
                        for n in range(MT):
                            rows = min(P, M - n * P)
                            dve.wait_ge(mv_ready, n + 1)
                            nc.vector.tensor_copy(kvx[0:rows, n, 0:2 * DK], pv[0:rows, n % 2, 0:2 * DK]).then_inc(mv_read, 1)
                        for n in range(MT):
                            rows = min(P, M - n * P)
                            last = nc.vector.memset(kvx[0:rows, n, 2 * DK:DK + VW], 1.0)
                        link(last)

            def attention(tag, scope, plans, flag, ones_rows, loads, prefetch, o_of, causal_sb):
                probs = sb(scope, f"{tag}_probs", [P, 3, GH, C])
                acc_sb = sb(scope, f"{tag}_acc", [P, 2, C])
                piece_max = sb(scope, f"{tag}_piece_max", [P, 2, UR, 4])
                row_max = sb(scope, f"{tag}_row_max", [P, 2, UR])
                shift = sb(scope, f"{tag}_shift", [UR, 2, 2, P], BF16)
                junk = sb(scope, f"{tag}_junk", [P, SB, C], BF16)
                inverse = sb(scope, f"{tag}_inverse", [P, 2, C // P, GH])
                mark = sb(scope, f"{tag}_mark", [P, 1])
                ps = psum(scope, f"{tag}_scores", [P, GH, C])
                po = psum(scope, f"{tag}_out", [P, C])
                pm = psum(scope, f"{tag}_max", [P, SB, C])
                s_load = [sem(f"{tag}_load{n}") for n in range(len(loads))]
                scores_ready, probs_ready, probs_masked, probs_used = (
                    sem(f"{tag}_scores_ready"), sem(f"{tag}_probs_ready"), sem(f"{tag}_probs_masked"), sem(f"{tag}_probs_used"))
                side_ready, side_read = sem(f"{tag}_side_ready"), sem(f"{tag}_side_read")
                acc_copied, inverse_ready = sem(f"{tag}_acc_copied"), sem(f"{tag}_inverse_ready")
                max_ready, shift_ready = sem(f"{tag}_max_ready"), sem(f"{tag}_shift_ready")
                shift_in = [sem(f"{tag}_shift_in{i}") for i in range(2)]
                s_set, s_pre = sem(f"{tag}_set"), sem(f"{tag}_prefetched")

                def schedule(steps, works):
                    stream = []
                    for u, wk_ in enumerate(works):
                        stream += [("piece", u, k) for k in range(len(wk_["pieces"]))]
                        stream.append(("turn", u))
                    order, late = [], []
                    for item in stream:
                        if item[0] == "turn" and item[1]:
                            late.append([3, item])
                            continue
                        order.append(item)
                        for w in late:
                            w[0] -= 1
                        order += [w[1] for w in late if w[0] == 0]
                        late = [w for w in late if w[0] > 0]
                    order += [w[1] for w in late]
                    first_of = {}
                    for i, st in enumerate(steps):
                        first_of.setdefault(st["unit"], i)
                    where = {item: n for n, item in enumerate(order)}
                    before = order[:where[("turn", 0)] + 1]
                    due, at = [], len(before)
                    side = []
                    for i in range(len(steps)):
                        need = at
                        for u in range(len(works)):
                            if first_of[u] - LEAD > i:
                                left = where[("turn", u)] + 1 - at
                                need = max(need, at + -(-left // (first_of[u] - LEAD - i)))
                            elif first_of[u] > i:
                                need = max(need, where[("turn", u)] + 1)
                        need = min(max(need, min(at + EVEN, len(order))), len(order))
                        side.append(order[at:need])
                        at = need
                    assert at == len(order)
                    side += [[], [], []]
                    for i, st in enumerate(steps):
                        if st["last"]:
                            side[i + 2] = side[i + 2] + [("sums", st["unit"])]
                    thirds = [[it[0:(len(it) + 2) // 3], it[(len(it) + 2) // 3:(2 * len(it) + 2) // 3], it[(2 * len(it) + 2) // 3:]] for it in side]
                    diag_before = [0]
                    for st in steps:
                        diag_before.append(diag_before[-1] + st["diag"])
                    return steps, works, first_of, before, thirds, diag_before

                plans = [schedule(*p) for p in plans]

                def either(eng, program):
                    if flag is None:
                        program(*plans[0])
                        return
                    chosen = eng.value_load(flag[0:1, 0:1])
                    with eng.If(chosen > 0):
                        program(*plans[0])
                    with eng.Else():
                        program(*plans[1])

                with nc.Block() as block:
                    @block.sync
                    def _(sp):
                        def load(n):
                            for dst, src in loads[n]:
                                sp.dma_start(dst, src).then_inc(s_load[n], 16)

                        for n in range(2):
                            load(n)

                        def program(steps, works, first_of, before, thirds, diag_before):
                            for u, wk_ in enumerate(works):
                                sp.wait_ge(shift_ready, u + 1)
                                for b, dst in enumerate(wk_["shift_to"]):
                                    sp.dma_start(dst, shift[:, u % 2, b]).then_inc(shift_in[u % 2], 16)
                                if u + 2 < len(loads):
                                    load(u + 2)
                                if u == len(loads):
                                    for dst, src in prefetch:
                                        sp.dma_start(dst, src).then_inc(s_pre, 16)
                            for i in range(2):
                                sp.wait_ge(shift_in[i], 16 * len(works))
                            if prefetch:
                                sp.wait_ge(s_pre, 16 * len(prefetch))

                        either(sp, program)

                    @block.gpsimd
                    def _(pool):
                        for n, ap in enumerate(ones_rows):
                            nc.gpsimd.memset(ap, 1.0).then_inc(s_set, 1)
                            pool.wait_ge(s_set, n + 1)

                        def program(steps, works, first_of, before, thirds, diag_before):
                            for i, st in enumerate(steps):
                                if st["diag"]:
                                    pool.wait_ge(probs_ready, 2 * (i + 1))
                                    blk = probs[:, i % 3, :, st["off"]:st["off"] + P]
                                    nc.gpsimd.affine_select(out=blk, in_=blk, compare_op=ALU.is_ge, fill=0.0, base=0,
                                                            pattern=[[0, GH], [1, P]], channel_multiplier=-1).then_inc(probs_masked, 1)

                        if causal_sb is not None:
                            either(pool, program)

                    @block.tensor
                    def _(pe):
                        def program(steps, works, first_of, before, thirds, diag_before):
                            uses, loaded = [0], [0]
                            nc.tensor.matmul(po[:], zeros[:, 0:P], zeros[:], start=True, stop=True)

                            def side_item(item):
                                n = uses[0]
                                uses[0] += 1
                                if n >= SB:
                                    pe.wait_ge(side_read, n - SB + 1)
                                slot = pm[:, n % SB]
                                if item[0] == "piece":
                                    pc = works[item[1]]["pieces"][item[2]]
                                    while loaded[0] < pc["load"]:
                                        pe.wait_ge(s_load[loaded[0]], 16 * len(loads[loaded[0]]))
                                        loaded[0] += 1
                                    if item[1] == 0 and item[2] == 0:
                                        pe.wait_ge(s_set, len(ones_rows))
                                    mm = nc.tensor.matmul(slot[:, 0:pc["w"]], pc["lhsT"], pc["rhs"], start=True, stop=True)
                                elif item[0] == "turn":
                                    pe.wait_ge(max_ready, item[1] + 1)
                                    mm = nc.tensor.transpose(slot[0:UR, 0:P], row_max[:, item[1] % 2], ident[:])
                                else:
                                    pe.wait_ge(acc_copied, item[1] + 1)
                                    for q in range(C // P):
                                        mm = nc.tensor.transpose(slot[:, q * P:(q + 1) * P], acc_sb[:, item[1] % 2, q * P:(q + 1) * P], ident[:])
                                mm.then_inc(side_ready, 1)

                            def scores(i, pair):
                                st = steps[i]
                                if i:
                                    pe.wait_ge(probs_ready, 2 * (i - 1) + pair + 1)
                                for j in (2 * pair, 2 * pair + 1):
                                    mm = nc.tensor.matmul(ps[:, j, st["off"]:C], st["keys"](j), st["queries"](j), start=True, stop=True)
                                mm.then_inc(scores_ready, 1)

                            def values(i):
                                st = steps[i]
                                pe.wait_ge(probs_ready, 2 * (i + 1))
                                if st["diag"]:
                                    pe.wait_ge(probs_masked, diag_before[i + 1])
                                if st["first"] and st["unit"]:
                                    pe.wait_ge(acc_copied, st["unit"])
                                for j in range(GH):
                                    mm = nc.tensor.matmul(po[32 * j:32 * j + VW, st["off"]:C], st["values"](j),
                                                          probs[:, i % 3, j, st["off"]:C], start=st["first"], stop=st["last"],
                                                          tile_position=(0, 32 * j))
                                mm.then_inc(probs_used, 1)

                            for item in before:
                                side_item(item)
                            for i in range(len(thirds)):
                                if i < len(steps):
                                    if first_of[steps[i]["unit"]] == i:
                                        u = steps[i]["unit"]
                                        pe.wait_ge(shift_in[u % 2], 32 * (u // 2 + 1))
                                    scores(i, 0)
                                for item in thirds[i][0]:
                                    side_item(item)
                                if i < len(steps):
                                    scores(i, 1)
                                for item in thirds[i][1]:
                                    side_item(item)
                                if 1 <= i <= len(steps):
                                    values(i - 1)
                                for item in thirds[i][2]:
                                    side_item(item)

                        either(pe, program)

                    @block.scalar
                    def _(act):
                        def program(steps, works, first_of, before, thirds, diag_before):
                            for i, st in enumerate(steps):
                                for pair in range(2):
                                    act.wait_ge(scores_ready, 2 * i + pair + 1)
                                    if i >= 3 and pair == 0:
                                        act.wait_ge(probs_used, i - 2)
                                    nc.scalar.activation(probs[:, i % 3, 2 * pair:2 * pair + 2, st["off"]:C],
                                                         ps[:, 2 * pair:2 * pair + 2, st["off"]:C], ACT.Exp,
                                                         scale=SCALE).then_inc(probs_ready, 1)

                        either(act, program)

                    @block.vector
                    def _(dve):
                        link = chain(dve, f"{tag}_dve_chain")
                        link(nc.vector.memset(piece_max[:], LOW))

                        def program(steps, works, first_of, before, thirds, diag_before):
                            uses = [0]

                            def side_item(item):
                                n = uses[0]
                                uses[0] += 1
                                dve.wait_ge(side_ready, n + 1)
                                slot = pm[:, n % SB]
                                if item[0] == "piece":
                                    u = item[1]
                                    pc = works[u]["pieces"][item[2]]
                                    to = piece_max[:, u % 2, pc["row"], pc["at"]:pc["at"] + 1]
                                    if pc["diag"]:
                                        ins = nc.vector.tensor_tensor_reduce(out=junk[:, n % SB, 0:pc["w"]], in0=slot[:, 0:pc["w"]],
                                                                             in1=causal_sb[:, C - pc["w"]:C], scale=1.0, scalar=LOW,
                                                                             op0=ALU.add, op1=ALU.max, accum_out=to)
                                    else:
                                        ins = nc.vector.tensor_reduce(to, slot[:, 0:pc["w"]], AX.X, ALU.max)
                                    ins.then_inc(side_read, 1)
                                    if item[2] == len(works[u]["pieces"]) - 1:
                                        dve.wait_ge(side_read, n + 1)
                                        nc.vector.tensor_reduce(row_max[:, u % 2], piece_max[:, u % 2], AX.X, ALU.max).then_inc(max_ready, 1)
                                elif item[0] == "turn":
                                    u = item[1]
                                    if u >= 2:
                                        dve.wait_ge(shift_in[u % 2], 32 * (u // 2))
                                    link(nc.vector.tensor_scalar(shift[:, u % 2, 0], slot[0:UR, 0:P], -1.0, None, ALU.mult))
                                    nc.vector.scalar_tensor_tensor(out=shift[:, u % 2, 1], in0=slot[0:UR, 0:P], scalar=-1.0,
                                                                   in1=shift[:, u % 2, 0], op0=ALU.mult,
                                                                   op1=ALU.subtract).then_inc(shift_ready, 1)
                                    dve.wait_ge(shift_ready, u + 1)
                                    nc.vector.memset(mark[:], 0.0).then_inc(side_read, 1)
                                else:
                                    u = item[1]
                                    heads = slot.rearrange("p (q j i) -> p q j i", j=GH, i=32)
                                    nc.vector.reciprocal(inverse[:, u % 2], heads[:, :, :, DK]).then_inc(inverse_ready, 1)
                                    dve.wait_ge(inverse_ready, u + 1)
                                    nc.vector.tensor_tensor(o_of(u), heads[:, :, :, 0:DK],
                                                            inverse[:, u % 2].rearrange("p q (j o) -> p q j o", o=1).to_broadcast([P, C // P, GH, DK]),
                                                            ALU.mult).then_inc(side_read, 1)

                            for item in before:
                                side_item(item)
                            for i in range(len(thirds)):
                                for item in thirds[i][0] + thirds[i][1]:
                                    side_item(item)
                                if 1 <= i <= len(steps) and steps[i - 1]["last"]:
                                    u = steps[i - 1]["unit"]
                                    dve.wait_ge(probs_used, i)
                                    nc.vector.tensor_copy(acc_sb[:, u % 2], po[:]).then_inc(acc_copied, 1)
                                for item in thirds[i][2]:
                                    side_item(item)

                        either(dve, program)

            stage = ExitStack()
            with stage:
                stack_q = [sb(stage, f"stack_q{g}", [P, NC, GH, C], BF16) for g in range(NG)]
                stack_k = [sb(stage, f"stack_k{g}", [P, GH, T], BF16) for g in range(NG)]
                causal_sb = sb(stage, "causal_sb", [P, C])
                loads = []
                for g, c0, c1 in [(0, c, c + 1) for c in range(NC)] + [(g, 0, NC) for g in range(1, NG)]:
                    pairs = [(causal_sb[:], causal)] if not loads else []
                    heads = slice(g * GH * DK, (g + 1) * GH * DK)
                    cols = slice(c0 * C, c1 * C)
                    for n, (a, b) in enumerate(PAIRS):
                        rows = slice(n * DK, (n + 1) * DK)
                        for c in range(c0, c1):
                            pairs.append((stack_q[g][rows, c], qparts[a, heads, c * C:(c + 1) * C].rearrange("(h i) t -> i h t", i=DK)))
                        pairs.append((stack_k[g][rows, :, cols], kparts[b, heads, cols].rearrange("(h i) t -> i h t", i=DK)))
                    loads.append(pairs)

                steps, works = [], []
                for g in range(NG):
                    for c in range(NC):
                        u = g * NC + c
                        pieces = []
                        for q in range(C // P):
                            end = c * C + (q + 1) * P
                            for j in range(GH):
                                for n, a in enumerate(range(0, end, C)):
                                    b = min(a + C, end)
                                    pieces.append(dict(w=b - a, lhsT=stack_q[g][0:KS, c, j, q * P:(q + 1) * P],
                                                       rhs=stack_k[g][0:KS, j, a:b], row=j * GH + q, at=n,
                                                       diag=b == end, load=c + 1 if g == 0 else NC + g))
                        works.append(dict(pieces=pieces,
                                          shift_to=[stack_q[g][KS + b:KS + b + 1, c].rearrange("o h (n t) -> o (h n) t", t=P) for b in range(2)]))
                        for kt in range((c + 1) * C // P):
                            off = max(0, kt * P - c * C)
                            steps.append(dict(
                                unit=u, off=off, diag=int(kt * P >= c * C), first=kt == 0, last=kt == (c + 1) * C // P - 1,
                                keys=lambda j, g=g, kt=kt: stack_k[g][0:KS + 2, j, kt * P:(kt + 1) * P],
                                queries=lambda j, g=g, c=c, off=off: stack_q[g][0:KS + 2, c, j, off:C],
                                values=lambda j, g=g, kt=kt: V[:, kt, g * GH + j, :]))
                attention("self", stage, [(steps, works)], None, [stack_k[g][KS:KS + 2] for g in range(NG)], loads, [],
                          lambda u: o_unit(u // NC, u % NC), causal_sb)

        def project_norm(tag, scope, w_dram, res_dram, bias_dram, x_sb, xT_sb, extra):
            w_sb = sb(scope, f"{tag}_w", [P, KD, D])
            oT = sb(scope, f"{tag}_oT", [P, KD, T])
            b_sb = sb(scope, f"{tag}_b", [P, D])
            stats = sb(scope, f"{tag}_stats", [P, NT, 6])
            mv = sb(scope, f"{tag}_mv", [P, NT, 2])
            rstd = sb(scope, f"{tag}_rstd", [P, NT])
            py = psum(scope, f"{tag}_py", [P, 2, C])
            pt = psum(scope, f"{tag}_pt", [P, 3, C])
            s_in, s_w = sem(f"{tag}_in"), sem(f"{tag}_w_in")
            y_ready, y_read = sem(f"{tag}_y_ready"), sem(f"{tag}_y_read")
            res_ready, normed = sem(f"{tag}_res_ready"), sem(f"{tag}_normed")
            var_ready, std_ready = sem(f"{tag}_var_ready"), sem(f"{tag}_std_ready")
            t_ready, t_read = sem(f"{tag}_t_ready"), sem(f"{tag}_t_read")
            banks = [(src, c, k) for src in range(2) for c in range(NC) for k in range(KD)]

            with nc.Block() as block:
                @block.sync
                def _(sp):
                    sp.dma_start(w_sb[:], kt_view(w_dram)).then_inc(s_w, 16)
                    if res_dram is not None:
                        sp.dma_start(x_sb[:], res_dram.rearrange("(n p) d -> p n d", p=P)).then_inc(s_in, 16)
                        sp.dma_start(b_sb[:], bias_dram.rearrange("(a n) -> a n", a=1).to_broadcast([P, D])).then_inc(s_in, 16)
                    for dst, src, s in extra:
                        sp.dma_start(dst, src).then_inc(s, 16)

                @block.gpsimd
                def _(pool):
                    if bias_dram is not None:
                        pool.wait_ge(s_in, 32)
                        for n in range(NT):
                            nc.gpsimd.tensor_tensor(x_sb[:, n], x_sb[:, n], b_sb[:], ALU.add).then_inc(res_ready, 1)

                @block.tensor
                def _(pe):
                    def turn(n):
                        src, c, k = banks[n]
                        if n >= 3:
                            pe.wait_ge(t_read, n - 2)
                        if src:
                            pe.wait_ge(normed, 4 * (c + 1))
                        for q in range(4):
                            mm = nc.tensor.transpose(pt[:, n % 3, q * P:(q + 1) * P],
                                                     (o_tok, x_sb)[src][:, 4 * c + q, k * P:(k + 1) * P], ident[:])
                        mm.then_inc(t_ready, 1)

                    for n in range(KD):
                        turn(n)
                    pe.wait_ge(s_w, 16)
                    for c in range(NC):
                        if c + 1 < NC:
                            for k in range(KD):
                                turn((c + 1) * KD + k)
                        pe.wait_ge(t_read, (c + 1) * KD)
                        for n in range(4 * c, 4 * c + 4):
                            if n >= 2:
                                pe.wait_ge(y_read, n - 1)
                            for k in range(KD):
                                mm = nc.tensor.matmul(py[:, n % 2, 0:D], oT[:, k, n * P:(n + 1) * P], w_sb[:, k], start=(k == 0), stop=(k == KD - 1))
                            mm.then_inc(y_ready, 1)
                    for n in range(KD * NC, 2 * KD * NC):
                        turn(n)

                @block.scalar
                def _(act):
                    for n, (src, c, k) in enumerate(banks):
                        if n == KD * NC:
                            act.wait_ge(var_ready, 1)
                            nc.scalar.activation(rstd[:], rstd[:], ACT.Sqrt).then_inc(std_ready, 1)
                        act.wait_ge(t_ready, n + 1)
                        nc.scalar.copy((oT, xT_sb)[src][:, k, c * C:(c + 1) * C], pt[:, n % 3]).then_inc(t_read, 1)

                @block.vector
                def _(dve):
                    norm_tiles(dve, tag, x_sb, stats, mv, rstd, var_ready, std_ready, normed, y_ready, y_read,
                               res_ready if bias_dram is not None else None, lambda n: py[:, n % 2, 0:D])

        def norm_tiles(dve, tag, x_sb, stats, mv, rstd, var_ready, std_ready, normed, y_ready, y_read, res_ready, y_of):
            link = chain(dve, f"{tag}_norm_chain")
            for n in range(NT):
                dve.wait_ge(y_ready, n + 1)
                if res_ready is not None:
                    dve.wait_ge(res_ready, n + 1)
                nc.vector.tensor_tensor(x_sb[:, n], y_of(n), x_sb[:, n], ALU.add).then_inc(y_read, 1)
                if n:
                    dve.wait_ge(y_read, n)
                    nc.vector.bn_stats(stats[:, n - 1], x_sb[:, n - 1])
            dve.wait_ge(y_read, NT)
            link(nc.vector.bn_stats(stats[:, NT - 1], x_sb[:, NT - 1]))
            for n in range(NT):
                last = nc.vector.bn_aggr(mv[:, n], stats[:, n])
            link(last)
            nc.vector.tensor_scalar_add(rstd[:], mv[:, :, 1], EPS).then_inc(var_ready, 1)
            dve.wait_ge(std_ready, 1)
            link(nc.vector.reciprocal(rstd[:], rstd[:]))
            for n in range(NT):
                nc.vector.tensor_scalar(x_sb[:, n], x_sb[:, n], mv[:, n, 0:1], rstd[:, n:n + 1],
                                        ALU.subtract, ALU.mult).then_inc(normed, 1)

        tail = ExitStack()
        with tail:
            x_sb = sb(tail, "x_sb", [P, NT, D])
            w1_sb = sb(tail, "w1_sb", [P, KD, W])
            w2_sb = sb(tail, "w2_sb", [P, WT, D])
            rw_sb = sb(tail, "rw_sb", [P, KD, E])
            stage = ExitStack()
            with stage:
                x1T = sb(stage, "x1T", [P, KD, T])
                ctx2 = sb(stage, "ctx2", [P, KD, M])
                xwq_sb = sb(stage, "xwq_sb", [P, KD, D])
                s_ctx2 = sem("ctx2_in")
                inner = ExitStack()
                with inner:
                    project_norm("n1", inner, wo, x, bo, x_sb, x1T,
                                 [(ctx2[:], kt_view(ctxT), s_ctx2), (xwq_sb[:], kt_view(xwq), s_ctx2)])

                inner = ExitStack()
                with inner:
                    parts = sb(inner, "xparts_sb", [P, 2, 3, C], BF16)
                    rest = sb(inner, "xrest_sb", [P, C])
                    qp = sb(inner, "qp", [P, KD, T])
                    iota_sb = sb(inner, "iota_sb", [P, M])
                    near = sb(inner, "near", [P, 2, M])
                    best = sb(inner, "best", [P, 2, 8])
                    place = sb(inner, "place", [P, 2, 8], U32)
                    place_f = sb(inner, "place_f", [P, 2, 1])
                    chosen = sb(inner, "chosen", [P, 2, MP], BF16)
                    ones_b = sb(inner, "ones_b", [P, 1], BF16)
                    zeros_b = sb(inner, "zeros_b", [P, P], BF16)
                    count = sb(inner, "count", [P, MT])
                    absent = sb(inner, "absent", [P, MT])
                    used = sb(inner, "used", [P, MT + 1])
                    place_of = sb(inner, "place_of", [P, MT])
                    chosen_n = sb(inner, "chosen_n", [P, 1])
                    below_sb = sb(inner, "below_sb", [P, P])
                    ones_f = sb(inner, "ones_f", [P, P])
                    sel = sb(inner, "sel", [P, 2, FEW])
                    mk_few = sb(inner, "mk_few", [DK, FEW])
                    mk_few_rest = sb(inner, "mk_few_rest", [DK, FEW])
                    mk_few_parts = sb(inner, "mk_few_parts", [DK, 3, FEW], BF16)
                    mask_few = sb(inner, "mask_few", [1, FEW], BF16)
                    pp = psum(inner, "pp", [P, 4, C])
                    pq = psum(inner, "pq2", [P, 2, C])
                    pc = psum(inner, "pc", [P, C])
                    pa = psum(inner, "pa", [P, C])
                    s_iota, set2 = sem("iota_in"), sem("set2")
                    s_xout = [sem(f"xparts_out{i}") for i in range(2)]
                    q_ready, q_copied, xp1, xrest, xp2, xp3 = (
                        sem("xq_ready"), sem("xq_copied"), sem("xp1"), sem("xrest"), sem("xp2"), sem("xp3"))
                    near_ready, near_copied, chosen_ready, counted = (
                        sem("near_ready"), sem("near_copied"), sem("chosen_ready"), sem("counted"))
                    absent_ready, absent_turned, mask_ready, mask_in = (
                        sem("absent_ready"), sem("absent_turned"), sem("mask_ready"), sem("mask_in"))
                    near_used = sem("near_used")
                    used_ready, ranks_ready, sel_ready, sel_used, mask_few_ready, vx_few_done = (
                        sem("used_ready"), sem("ranks_ready"), sem("sel_ready"), sem("sel_used"), sem("mask_few_ready"), sem("vx_few_done"))
                    few_copied, few1, few_rest, few2, few3, few_in = (
                        sem("few_copied"), sem("few1"), sem("few_rest"), sem("few2"), sem("few3"), sem("few_in"))
                    qunits = [(m, c) for c in range(NC) for m in range(KD)]
                    cols = [(a, min(a + C, M)) for a in range(0, M, C)]

                    with nc.Block() as block:
                        @block.sync
                        def _(sp):
                            sp.dma_start(iota_sb[:], iota).then_inc(s_iota, 16)
                            sp.dma_start(below_sb[:], below).then_inc(s_iota, 16)
                            for n, (m, c) in enumerate(qunits):
                                sp.wait_ge(xp3, n + 1)
                                sp.dma_start(xparts[:, m * P:(m + 1) * P, c * C:(c + 1) * C].rearrange("r p t -> p r t"),
                                             parts[:, n % 2]).then_inc(s_xout[n % 2], 16)
                            sp.wait_ge(mask_ready, 1)
                            sp.dma_start(kx[KS:KS + 1, :].rearrange("o (n t) -> o n t", t=P), maskx[:]).then_inc(mask_in, 16)
                            sp.wait_ge(mask_few_ready, 1)
                            sp.dma_start(kx_few[KS:KS + 1, :], mask_few[:]).then_inc(few_in, 16)
                            sp.wait_ge(few3, 1)
                            for n, (_, b) in enumerate(PAIRS):
                                sp.dma_start(kx_few[n * DK:(n + 1) * DK, :], mk_few_parts[:, b]).then_inc(few_in, 16)
                            sp.wait_ge(few_in, 16 * (1 + len(PAIRS)))
                            sp.wait_ge(mask_in, 16)
                            for i in range(2):
                                sp.wait_ge(s_xout[i], 8 * len(qunits))

                        @block.gpsimd
                        def _(pool):
                            nc.gpsimd.memset(ones_b[:], 1.0).then_inc(set2, 1)
                            pool.wait_ge(set2, 1)
                            nc.gpsimd.memset(zeros_b[:], 0.0).then_inc(set2, 1)
                            pool.wait_ge(set2, 2)
                            nc.gpsimd.memset(chosen[:], 0.0).then_inc(set2, 1)
                            pool.wait_ge(set2, 3)
                            nc.gpsimd.memset(ones_f[:], 1.0).then_inc(set2, 1)
                            pool.wait_ge(set2, 4)
                            nc.gpsimd.memset(used[:], 0.0).then_inc(set2, 1)
                            pool.wait_ge(set2, 5)
                            nc.gpsimd.memset(kx_few[KS:KS + 3, :], 1.0).then_inc(set2, 1)

                        @block.tensor
                        def _(pe):
                            pe.wait_ge(s_ctx2, 32)
                            for n, (m, c) in enumerate(qunits):
                                if n >= 2:
                                    pe.wait_ge(xrest, n - 1)
                                for k in range(KD):
                                    mm = nc.tensor.matmul(pq[:, n % 2], xwq_sb[:, k, m * P:(m + 1) * P], x1T[:, k, c * C:(c + 1) * C],
                                                          start=(k == 0), stop=(k == KD - 1))
                                mm.then_inc(q_ready, 1)
                            pe.wait_ge(set2, 6)
                            nc.tensor.matmul(pc[:, 0:MT], zeros_b[:], zeros_b[:, 0:MT], start=True, stop=False, skip_group_check=True)

                            def tally(n):
                                pe.wait_ge(chosen_ready, n + 1)
                                for t in range(MT):
                                    mm = nc.tensor.matmul(pc[:, t:t + 1], chosen[:, n % 2, t * P:(t + 1) * P], ones_b[:],
                                                          start=False, stop=(n == NT - 1 and t == MT - 1), skip_group_check=True)
                                mm.then_inc(counted, 1)

                            pe.wait_ge(q_copied, len(qunits))
                            u = 0
                            for n in range(NT):
                                for a, b in cols:
                                    if u >= 4:
                                        pe.wait_ge(near_copied, u - 3)
                                    for k in range(KD):
                                        mm = nc.tensor.matmul(pp[:, u % 4, 0:b - a], qp[:, k, n * P:(n + 1) * P], ctx2[:, k, a:b],
                                                              start=(k == 0), stop=(k == KD - 1))
                                    mm.then_inc(near_ready, 1)
                                    u += 1
                                if n:
                                    tally(n - 1)
                            tally(NT - 1)
                            pe.wait_ge(absent_ready, 1)
                            nc.tensor.transpose(pa[0:MT, 0:P], absent[:], ident[:]).then_inc(absent_turned, 1)
                            pe.wait_ge(s_iota, 32)
                            pe.wait_ge(used_ready, 1)
                            pe.wait_ge(near_copied, NT * len(cols))
                            ranks = pp[:, 0, 0:MT + 1]
                            nc.tensor.matmul(ranks, below_sb[:], used[:], start=True, stop=False, skip_group_check=True)
                            for t in range(MT):
                                mm = nc.tensor.matmul(pp[:, 0, t + 1:MT + 1], ones_f[:], used[:, t:t + 1].to_broadcast([P, MT - t]),
                                                      start=False, stop=t == MT - 1, skip_group_check=True)
                            mm.then_inc(ranks_ready, 1)
                            pe.wait_ge(xrest, len(qunits))
                            pe.wait_ge(xp1, len(qunits))
                            nc.tensor.matmul(pq[:, 1, 0:FEW // P * VW], zeros[:, 0:P], zeros[:, 0:FEW // P * VW], start=True, stop=False, skip_group_check=True)
                            for t in range(MT):
                                pe.wait_ge(sel_ready, t + 1)
                                nc.tensor.matmul(pq[0:DK, 0], kvx[:, t, 0:DK], sel[:, t % 2], start=t == 0, stop=t == MT - 1)
                                for n in range(FEW // P):
                                    mm = nc.tensor.matmul(pq[:, 1, n * VW:(n + 1) * VW], sel[:, t % 2, n * P:(n + 1) * P], kvx[:, t, DK:DK + VW],
                                                          start=False, stop=t == MT - 1, skip_group_check=True)
                                mm.then_inc(sel_used, 1)

                        @block.scalar
                        def _(act):
                            for n, (m, c) in enumerate(qunits):
                                act.wait_ge(q_ready, n + 1)
                                nc.scalar.copy(qp[:, m, c * C:(c + 1) * C], pq[:, n % 2]).then_inc(q_copied, 1)
                                if n >= 2:
                                    act.wait_ge(s_xout[n % 2], 16 * (n // 2))
                                nc.scalar.copy(parts[:, n % 2, 0], pq[:, n % 2]).then_inc(xp1, 1)
                                act.wait_ge(xrest, n + 1)
                                nc.scalar.copy(parts[:, n % 2, 1], rest[:]).then_inc(xp2, 1)
                            u = 0
                            for n in range(NT):
                                for a, b in cols:
                                    act.wait_ge(near_ready, u + 1)
                                    if n >= 2:
                                        act.wait_ge(near_used, n - 1)
                                    nc.scalar.copy(near[:, n % 2, a:b], pp[:, u % 4, 0:b - a]).then_inc(near_copied, 1)
                                    u += 1
                            act.wait_ge(sel_used, MT)
                            nc.scalar.copy(mk_few[:], pq[0:DK, 0]).then_inc(few_copied, 1)
                            act.wait_ge(few_copied, 1)
                            nc.scalar.copy(mk_few_parts[:, 0], mk_few[:]).then_inc(few1, 1)
                            act.wait_ge(few_rest, 1)
                            nc.scalar.copy(mk_few_parts[:, 1], mk_few_rest[:]).then_inc(few2, 1)

                        @block.vector
                        def _(dve):
                            link = chain(dve, "choose_chain")
                            for n in range(len(qunits)):
                                dve.wait_ge(xp1, n + 1)
                                if n:
                                    dve.wait_ge(xp3, n)
                                nc.vector.tensor_tensor(rest[:], pq[:, n % 2], parts[:, n % 2, 0], ALU.subtract).then_inc(xrest, 1)
                                dve.wait_ge(xp2, n + 1)
                                nc.vector.tensor_tensor(parts[:, n % 2, 2], rest[:], parts[:, n % 2, 1], ALU.subtract).then_inc(xp3, 1)
                            dve.wait_ge(s_iota, 32)
                            dve.wait_ge(set2, 6)
                            for n in range(NT):
                                dve.wait_ge(near_copied, len(cols) * (n + 1))
                                link(nc.vector.max(best[:, n % 2], near[:, n % 2]))
                                nc.vector.max_index(place[:, n % 2], best[:, n % 2], near[:, n % 2]).then_inc(near_used, 1)
                                dve.wait_ge(near_used, n + 1)
                                link(nc.vector.tensor_copy(place_f[:, n % 2], place[:, n % 2, 0:1]))
                                if n >= 2:
                                    dve.wait_ge(counted, n - 1)
                                nc.vector.tensor_scalar(chosen[:, n % 2, 0:M], iota_sb[:], place_f[:, n % 2], None,
                                                        ALU.is_equal).then_inc(chosen_ready, 1)
                            dve.wait_ge(counted, NT)
                            link(nc.vector.tensor_copy(count[:], pc[:, 0:MT]))
                            nc.vector.tensor_scalar(absent[:], count[:], 0.0, MASKED, ALU.is_equal, ALU.mult).then_inc(absent_ready, 1)
                            nc.vector.tensor_scalar(used[:, 0:MT], count[:], 0.0, None, ALU.is_gt).then_inc(used_ready, 1)
                            for t in range(MT):
                                last = nc.vector.tensor_scalar(kvx[:, t, DK:DK + VW], kvx[:, t, DK:DK + VW], count[:, t:t + 1], None, ALU.mult)
                            link(last)
                            dve.wait_ge(absent_turned, 1)
                            nc.vector.tensor_copy(maskx[:], pa[0:MT, 0:P]).then_inc(mask_ready, 1)
                            dve.wait_ge(ranks_ready, 1)
                            nc.vector.tensor_scalar(few[:], pp[:, 0, MT:MT + 1], float(FEW), None, ALU.is_le)
                            nc.vector.tensor_copy(chosen_n[:], pp[:, 0, MT:MT + 1])
                            link(nc.vector.scalar_tensor_tensor(out=place_of[:], in0=pp[:, 0, 0:MT], scalar=1.0, in1=used[:, 0:MT],
                                                                op0=ALU.add, op1=ALU.mult))
                            link(nc.vector.tensor_scalar_add(place_of[:], place_of[:], -1.0))
                            nc.vector.tensor_scalar(mask_few[:], iota_sb[0:1, 0:FEW], chosen_n[0:1], MASKED, ALU.is_ge, ALU.mult).then_inc(mask_few_ready, 1)
                            for t in range(MT):
                                if t >= 2:
                                    dve.wait_ge(sel_used, t - 1)
                                nc.vector.tensor_scalar(sel[:, t % 2], iota_sb[:, 0:FEW], place_of[:, t:t + 1], None, ALU.is_equal).then_inc(sel_ready, 1)
                            dve.wait_ge(sel_used, MT)
                            nc.vector.tensor_copy(vx_few[:], pq[:, 1, 0:FEW // P * VW].rearrange("p (n d) -> p n d", d=VW)).then_inc(vx_few_done, 1)
                            dve.wait_ge(few1, 1)
                            nc.vector.tensor_tensor(mk_few_rest[:], mk_few[:], mk_few_parts[:, 0], ALU.subtract).then_inc(few_rest, 1)
                            dve.wait_ge(few2, 1)
                            nc.vector.tensor_tensor(mk_few_parts[:, 2], mk_few_rest[:], mk_few_parts[:, 1], ALU.subtract).then_inc(few3, 1)

            stage = ExitStack()
            with stage:
                stackx = sb(stage, "stackx", [P, NC, H, C], BF16)
                loads = [[(stackx[n * DK:(n + 1) * DK, c], xparts[a, :, c * C:(c + 1) * C].rearrange("(h i) t -> i h t", i=DK))
                          for n, (a, _) in enumerate(PAIRS)] for c in range(NC)]

                def plan(keys, vals, n):
                    steps, works = [], []
                    width = C if n == FEW else n // 4
                    for c in range(NC):
                        for g in range(NG):
                            pieces = [dict(w=width, lhsT=stackx[0:KS + 1, c, g * GH + j, q * P:(q + 1) * P],
                                           rhs=keys[0:KS + 1, a * width:(a + 1) * width], row=j * GH + q, at=a, diag=False, load=c + 1)
                                      for j in range(GH) for q in range(C // P) for a in range(n // width)]
                            works.append(dict(pieces=pieces, shift_to=[
                                stackx[KS + 1 + b:KS + 2 + b, c, g * GH:(g + 1) * GH, :].rearrange("o h (n t) -> o (h n) t", t=P) for b in range(2)]))
                            for t in range(n // P):
                                steps.append(dict(unit=c * NG + g, off=0, diag=0, first=t == 0, last=t == n // P - 1,
                                                  keys=lambda j, t=t: keys[0:KS + 3, t * P:(t + 1) * P],
                                                  queries=lambda j, g=g, c=c: stackx[0:KS + 3, c, g * GH + j, :],
                                                  values=lambda j, t=t: vals(t)))
                    return steps, works

                attention("cross", stage, [plan(kx_few, lambda t: vx_few[:, t, :], FEW), plan(kx, lambda t: kvx[:, t, DK:DK + VW], MP)],
                          few, [stackx[KS:KS + 1]], loads,
                          [(w1_sb[:], kt_view(w1)), (w2_sb[:], kt_view(w2)), (rw_sb[:], kt_view(rw))],
                          lambda u: o_unit(u % NG, u // NG), None)

            x2T = sb(tail, "x2T", [P, KD, T])
            inner = ExitStack()
            with inner:
                project_norm("n2", inner, xwc, None, None, x_sb, x2T, [])

            gate = sb(tail, "gate", [P, NT, E])
            top8 = sb(tail, "top8", [P, NT, 8])
            at8 = sb(tail, "at8", [P, NT, 8], U32)
            at_f = sb(tail, "at_f", [P, NT, 2])
            total = sb(tail, "total", [P, NT])
            mix = sb(tail, "mix", [P, NT, E])
            hot = sb(tail, "hot", [P, E])
            iota8 = sb(tail, "iota8", [P, E])
            hid = sb(tail, "hid", [P, WT, C])
            relu = sb(tail, "relu", [P, 3, C])
            stats = sb(tail, "n3_stats", [P, NT, 6])
            mv = sb(tail, "n3_mv", [P, NT, 2])
            rstd = sb(tail, "n3_rstd", [P, NT])
            pr = psum(tail, "pr", [P, NT, E])
            ph = psum(tail, "ph", [P, 3, C])
            py = psum(tail, "py", [P, 4, C])
            s_i8, r_ready, e_ready, h_ready, h_read = (sem("iota8_in"), sem("r_ready"), sem("e_ready"), sem("h_ready"), sem("h_read"))
            y_ready, y_read, hid_ready, s_out, normed = (sem("y_ready"), sem("y_read"), sem("hid_ready"), sem("out_done"), sem("n3_normed"))
            var_ready, std_ready = sem("n3_var_ready"), sem("n3_std_ready")
            starts = [sum(WIDTHS[:e]) // P for e in range(E + 1)]

            with nc.Block() as block:
                @block.sync
                def _(sp):
                    sp.dma_start(iota8[:], iota[:, 0:E]).then_inc(s_i8, 16)
                    for n in range(NT):
                        sp.wait_ge(normed, n + 1)
                        sp.dma_start(out[n * P:(n + 1) * P, :], x_sb[:, n]).then_inc(s_out, 16)
                    sp.wait_ge(s_out, 16 * NT)

                @block.tensor
                def _(pe):
                    for n in range(NT):
                        for k in range(KD):
                            mm = nc.tensor.matmul(pr[:, n], x2T[:, k, n * P:(n + 1) * P], rw_sb[:, k], start=(k == 0), stop=(k == KD - 1))
                    mm.then_inc(r_ready, 1)
                    u = y = 0
                    for c in range(NC):
                        for w in range(WT):
                            if u >= 3:
                                pe.wait_ge(h_read, u - 2)
                            for k in range(KD):
                                mm = nc.tensor.matmul(ph[:, u % 3], w1_sb[:, k, w * P:(w + 1) * P], x2T[:, k, c * C:(c + 1) * C],
                                                      start=(k == 0), stop=(k == KD - 1))
                            mm.then_inc(h_ready, 1)
                            u += 1
                        for q in range(4):
                            for e in range(E):
                                pe.wait_ge(hid_ready, c * WT + starts[e + 1])
                                if y >= 4:
                                    pe.wait_ge(y_read, y - 3)
                                for w in range(starts[e], starts[e + 1]):
                                    mm = nc.tensor.matmul(py[:, y % 4, 0:D], hid[:, w, q * P:(q + 1) * P], w2_sb[:, w],
                                                          start=(w == starts[e]), stop=(w == starts[e + 1] - 1))
                                mm.then_inc(y_ready, 1)
                                y += 1

                @block.scalar
                def _(act):
                    act.wait_ge(r_ready, 1)
                    nc.scalar.activation(gate[:], pr[:], ACT.Exp, scale=-1.0).then_inc(e_ready, 1)
                    for u in range(NC * WT):
                        act.wait_ge(h_ready, u + 1)
                        if u >= 3:
                            act.wait_ge(hid_ready, u - 2)
                        nc.scalar.activation(relu[:, u % 3], ph[:, u % 3], ACT.Relu).then_inc(h_read, 1)
                    act.wait_ge(var_ready, 1)
                    nc.scalar.activation(rstd[:], rstd[:], ACT.Sqrt).then_inc(std_ready, 1)

                @block.vector
                def _(dve):
                    link = chain(dve, "ffn_chain")
                    dve.wait_ge(e_ready, 1)
                    dve.wait_ge(s_i8, 16)
                    link(nc.vector.tensor_scalar_add(gate[:], gate[:], 1.0))
                    link(nc.vector.reciprocal(gate[:], gate[:]))
                    for n in range(NT):
                        last = nc.vector.max(top8[:, n], gate[:, n])
                    link(last)
                    for n in range(NT):
                        last = nc.vector.max_index(at8[:, n], top8[:, n], gate[:, n])
                    link(last)
                    link(nc.vector.tensor_copy(at_f[:], at8[:, :, 0:2]))
                    link(nc.vector.tensor_tensor(total[:], top8[:, :, 0], top8[:, :, 1], ALU.add))
                    link(nc.vector.tensor_scalar_add(total[:], total[:], 1e-20))
                    link(nc.vector.reciprocal(total[:], total[:]))
                    for n in range(NT):
                        link(nc.vector.tensor_scalar(top8[:, n, 0:2], top8[:, n, 0:2], total[:, n:n + 1], None, ALU.mult))
                        link(nc.vector.tensor_scalar(hot[:], iota8[:], at_f[:, n, 0:1], top8[:, n, 0:1], ALU.is_equal, ALU.mult))
                        link(nc.vector.tensor_scalar(mix[:, n], iota8[:], at_f[:, n, 1:2], top8[:, n, 1:2], ALU.is_equal, ALU.mult))
                        link(nc.vector.tensor_tensor(mix[:, n], mix[:, n], hot[:], ALU.add))
                    u = y = 0
                    for c in range(NC):
                        for w in range(WT):
                            dve.wait_ge(h_read, u + 1)
                            if w == 0 and c:
                                dve.wait_ge(y_ready, y)
                            nc.vector.tensor_tensor(hid[:, w], relu[:, u % 3], relu[:, u % 3], ALU.mult).then_inc(hid_ready, 1)
                            u += 1
                        for q in range(4):
                            for e in range(E):
                                n = 4 * c + q
                                dve.wait_ge(y_ready, y + 1)
                                if y:
                                    dve.wait_ge(y_read, y)
                                nc.vector.scalar_tensor_tensor(out=x_sb[:, n], in0=py[:, y % 4, 0:D], scalar=mix[:, n, e:e + 1],
                                                               in1=x_sb[:, n], op0=ALU.mult, op1=ALU.add).then_inc(y_read, 1)
                                y += 1
                    dve.wait_ge(y_read, y)
                    for n in range(NT):
                        last = nc.vector.bn_stats(stats[:, n], x_sb[:, n])
                    link(last)
                    for n in range(NT):
                        last = nc.vector.bn_aggr(mv[:, n], stats[:, n])
                    link(last)
                    nc.vector.tensor_scalar_add(rstd[:], mv[:, :, 1], EPS).then_inc(var_ready, 1)
                    dve.wait_ge(std_ready, 1)
                    link(nc.vector.reciprocal(rstd[:], rstd[:]))
                    for n in range(NT):
                        nc.vector.tensor_scalar(x_sb[:, n], x_sb[:, n], mv[:, n, 0:1], rstd[:, n:n + 1],
                                                ALU.subtract, ALU.mult).then_inc(normed, 1)


def kernel(x, ctx_1024, L0_attn_WQ_w, L0_attn_WQ_b, L0_attn_WK_w, L0_attn_WK_b, L0_attn_WV_w, L0_attn_WV_b, L0_attn_Wo_w,
           L0_attn_Wo_b, L0_xattn_Wq, L0_xattn_Wkv, L0_xattn_Wc, L0_ffn_router_w, L0_ffn_w1, L0_ffn_w2):
    import numpy as np
    import concourse.bacc as bacc
    from concourse.bass_utils import run_bass_kernel_spmd

    half = DK // 2
    swap = np.arange(D).reshape(H, 2, half)[:, ::-1].reshape(D)
    freq = (1.0 / 10000.0 ** (2.0 * np.arange(half, dtype=np.float32) / DK)).astype(np.float32)
    angle = np.arange(T, dtype=np.float32)[:, None] * freq[None, :]
    cos = np.tile(np.cos(angle).T, (2 * P // DK, 1)).astype(np.float32)
    sin = np.tile(np.concatenate([-np.sin(angle).T, np.sin(angle).T]), (P // DK, 1)).astype(np.float32)
    rows = np.arange(P)
    below = (rows[:, None] < rows[None, :]).astype(np.float32)
    tri = np.where(np.arange(P)[None, :] > rows[:, None], np.float32(MASKED), np.float32(0.0))
    causal = np.concatenate([np.zeros((P, C - P), np.float32), tri], 1)
    data = dict(
        x=x[0], xT=x[0].T, ctxT=ctx_1024[0].T,
        wq=L0_attn_WQ_w.T, wqs=L0_attn_WQ_w[swap].T, bq=L0_attn_WQ_b.reshape(KD, P).T, bqs=L0_attn_WQ_b[swap].reshape(KD, P).T,
        wk=L0_attn_WK_w.T, wks=L0_attn_WK_w[swap].T, bk=L0_attn_WK_b.reshape(KD, P).T, bks=L0_attn_WK_b[swap].reshape(KD, P).T,
        wv=L0_attn_WV_w.T, bv=L0_attn_WV_b, wo=L0_attn_Wo_w.T, bo=L0_attn_Wo_b,
        xwq=L0_xattn_Wq.T, xwkv=L0_xattn_Wkv.T, xwc=L0_xattn_Wc.T,
        rw=L0_ffn_router_w.T, w1=L0_ffn_w1, w2=L0_ffn_w2,
        cosT=cos, sinT=sin, identity=np.eye(P, dtype=np.float32), below=below, causal=causal,
        iota=np.tile(np.arange(M, dtype=np.float32), (P, 1)))
    nc = bacc.Bacc("TRN2", target_bir_lowering=False, num_devices=1)
    arrays, args = {}, {}
    for name, a in data.items():
        a = np.ascontiguousarray(a)
        arrays[f"in_{name}"] = a
        args[name] = nc.dram_tensor(f"in_{name}", a.shape, mybir.dt.from_np(a.dtype), kind="ExternalInput").ap()
    out = nc.dram_tensor("out_0", (T, D), F32, kind="ExternalOutput").ap()
    decoder_layer(nc, out=out, **args)
    got = run_bass_kernel_spmd(nc, [arrays], core_ids=[0])
    return got.results[0]["out_0"].reshape(1, T, D)
```

```python
import concourse.bass as bass
from concourse import mybir
from contextlib import ExitStack

F32 = mybir.dt.float32
BF16 = mybir.dt.bfloat16
F32R = mybir.dt.float32r
U32 = mybir.dt.uint32
I32 = mybir.dt.int32
ALU = mybir.AluOpType
ACT = mybir.ActivationFunctionType
AX = mybir.AxisListType

P = 128
T = 2048
D = 256
H = 16
DK = D // H
KD = D // P
NT = T // P
C = 512
TC = C // P
NC = T // C
GH = 4
NG = H // GH
M = 1601
MT = -(-M // P)
MP2 = M + M % 2
MP = MT * P
FEW = 512
FT = FEW // P
RW = 6 * DK + 2
E = 8
WIDTHS = [256] * 4 + [512] * 4
W = sum(WIDTHS)
WT = W // P
PAIRS = [(0, 0), (0, 1), (1, 0), (0, 2), (2, 0), (1, 1)]
KS = len(PAIRS) * DK
VW = DK + 1
UR = GH * C // P
SB = 3
LEAD = 4
EVEN = 4
LOW = -3.0e38
MASKED = -1.0e30
SCALE = DK ** -0.5
EPS = 1e-5


class Count:

    def __init__(self, sem):
        self.sem, self.n = sem, 0

    def inc(self, ins, by=1):
        ins.then_inc(self.sem, by)
        self.n += by
        return self.n


def decoder_layer(nc, x, xT, ctxT, wq, wqs, bq, bqs, wk, wks, bk, bks, wv, bv, wo, bo, xwq, xwkv, xwc, rw, w1, w2,
                  cosT, sinT, identity, below, causal, iota, out):
    top = ExitStack()

    def sem(name):
        return top.enter_context(nc.semaphore(name))

    def sb(scope, name, shape, dt=F32):
        return scope.enter_context(nc.sbuf_tensor(name, shape, dt))

    def psum(scope, name, shape, dt=F32):
        return scope.enter_context(nc.psum_tensor(name, shape, dt))

    def chain(eng, name):
        done = Count(sem(name))

        def link(ins):
            eng.wait_ge(done.sem, done.inc(ins))

        return link

    def o_unit(g, c):
        return o_tok[:, c * C // P:(c + 1) * C // P, g * GH * DK:(g + 1) * GH * DK].rearrange("p q (j i) -> p q j i", i=DK)

    def product(out, lhsT, rhs, first, last):
        terms = [(0, 0), (0, 1), (1, 0)]
        for n, (a, b) in enumerate(terms):
            ins = nc.tensor.matmul(out, lhsT[a], rhs[b], start=first and n == 0, stop=last and n == len(terms) - 1)
        return ins

    def raw_view(raw, n, first):
        return raw[:, n % raw.shape[1], 0:first.shape[1] * first.shape[2]].rearrange("p (a d) -> p a d", d=first.shape[2])

    def load_pieces(sp, pieces, raw, piece_in, split_done):
        slots = raw.shape[1]
        for n, (src, first, _) in enumerate(pieces):
            if n >= slots:
                sp.wait_ge(split_done, n - slots + 1)
            sp.dma_start(raw_view(raw, n, first), src.rearrange("(a p) d -> p a d", p=P)).then_inc(piece_in[n % slots], 16)

    def first_of_piece(eng, copy, n, pieces, raw, piece_in, first_done):
        _, first, _ = pieces[n]
        eng.wait_ge(piece_in[n % len(piece_in)], 16 * (n // len(piece_in) + 1))
        copy(first, raw_view(raw, n, first)).then_inc(first_done, 1)

    def rest_of_piece(pool, n, pieces, raw, first_done, split_done):
        _, first, rest = pieces[n]
        pool.wait_ge(first_done, n + 1)
        nc.gpsimd.tensor_tensor(rest, raw_view(raw, n, first), first.bitcast(F32), ALU.subtract).then_inc(split_done, 1)

    def kt_view(w):
        return w.rearrange("(k p) n -> p k n", p=P)

    with top:
        qparts = nc.dram_tensor("qparts", [3, D, T], BF16).ap()
        kparts = nc.dram_tensor("kparts", [3, D, T], BF16).ap()
        xparts = nc.dram_tensor("xparts", [3, D, T], BF16).ap()

        ident = sb(top, "ident", [P, P])
        zeros = sb(top, "zeros", [P, C])
        kx = sb(top, "kx", [P, MP], BF16)
        kvx = sb(top, "kvx", [P, MT, DK + VW])
        kx_few = sb(top, "kx_few", [P, FEW], BF16)
        vx_few = sb(top, "vx_few", [P, FEW // P, VW])
        few = sb(top, "few", [P, 1], I32)
        o_tok = sb(top, "o_tok", [P, NT, D])
        maskx = sb(top, "maskx", [MT, P], BF16)

        consts_in = sem("consts_in")

        att = ExitStack()
        with att:
            V = sb(att, "V", [P, NT, H, VW])
            stage = ExitStack()
            with stage:
                xT_sb = sb(stage, "xT_sb", [P, KD, T])
                w_sb = sb(stage, "w_sb", [P, 5, KD, D])
                ctx_sb = sb(stage, "ctx_sb", [P, KD, M])
                wkv_sb = sb(stage, "wkv_sb", [P, KD, 2 * DK])
                cs = sb(stage, "cs", [P, 2, T])
                bias = sb(stage, "bias", [P, 4, KD])
                bv_all = sb(stage, "bv_all", [P, D])
                parts = sb(stage, "parts", [P, 2, 3, C], BF16)
                rest = sb(stage, "rest", [P, 2, C])
                turned = sb(stage, "turned", [P, 2, 2, C])
                whole = sb(stage, "whole", [P, 2, C])
                mk = sb(stage, "mk", [DK, MP])
                mk_rest = sb(stage, "mk_rest", [DK, MP])
                mk_parts = sb(stage, "mk_parts", [DK, 3, MP], BF16)
                pq = psum(stage, "pq", [P, 2, 2, C])
                pv = psum(stage, "pv", [P, 2, C])
                pk = psum(stage, "pk", [P, 2, C])

                s_w, s_b, s_ctx = sem("weights_in"), sem("bias_in"), sem("ctx_in")
                s_x = [None] + [sem(f"x_in{c}") for c in range(1, NC)]
                s_ones, s_mk_out = sem("ones_set"), sem("mk_out")
                s_parts_out = [sem(f"parts_out{i}") for i in range(2)]
                qk_ready, qk_read = sem("qk_ready"), sem("qk_read")
                v_ready, v_read = sem("v_ready"), sem("v_read")
                mk_ready, mv_ready = sem("mk_ready"), sem("mv_ready")
                whole_ready, p1_ready, rest_ready, p2_ready, p3_ready = (
                    sem("whole_ready"), sem("p1_ready"), sem("rest_ready"), sem("p2_ready"), sem("p3_ready"))
                mk_copied, mk1, mkr, mk2, mk3 = (sem("mk_copied"), sem("mk1"), sem("mkr"), sem("mk2"), sem("mk3"))
                units = [(t, m, c) for c in range(NC) for t in range(2) for m in range(KD)]
                MK_AT = 5
                mk_cols = [(a, min(a + C, M)) for a in range(0, M, C)]

                with nc.Block() as block:
                    @block.sync
                    def _(sp):
                        def load_chunk(c, s_tokens, s_turns):
                            cols = slice(c * C, (c + 1) * C)
                            sp.dma_start(xT_sb[:, :, cols], kt_view(xT)[:, :, cols]).then_inc(s_tokens, 16)
                            sp.dma_start(cs[:, 0, cols], cosT[:, cols]).then_inc(s_turns, 16)
                            sp.dma_start(cs[:, 1, cols], sinT[:, cols]).then_inc(s_turns, 16)

                        for n, w in enumerate((wq, wqs, wk, wks, wv)):
                            sp.dma_start(w_sb[:, n], kt_view(w)).then_inc(s_w, 16)
                        load_chunk(0, s_w, s_b)
                        for n, b in enumerate((bq, bqs, bk, bks)):
                            sp.dma_start(bias[:, n], b).then_inc(s_b, 16)
                        sp.dma_start(bv_all[:], bv.rearrange("(a n) -> a n", a=1).to_broadcast([P, D])).then_inc(s_b, 16)
                        load_chunk(1, s_x[1], s_x[1])
                        sp.dma_start(ctx_sb[:], kt_view(ctxT)[:, :, 0:M]).then_inc(s_ctx, 16)
                        sp.dma_start(wkv_sb[:], kt_view(xwkv)).then_inc(s_ctx, 16)
                        for c in range(2, NC):
                            load_chunk(c, s_x[c], s_x[c])
                        sp.dma_start(ident[:], identity).then_inc(consts_in, 16)
                        for n, (t, m, c) in enumerate(units):
                            dst = (qparts, kparts)[t][:, m * P:(m + 1) * P, c * C:(c + 1) * C].rearrange("r p t -> p r t")
                            if n == len(units) - 1:
                                sp.wait_ge(mk3, 1)
                                for i, (_, b) in enumerate(PAIRS):
                                    sp.dma_start(kx[i * DK:(i + 1) * DK, :], mk_parts[:, b]).then_inc(s_mk_out, 16)
                            sp.wait_ge(p3_ready, n + 1)
                            sp.dma_start(dst, parts[:, n % 2]).then_inc(s_parts_out[n % 2], 16)
                        for i in range(2):
                            sp.wait_ge(s_parts_out[i], 8 * len(units))
                        sp.wait_ge(s_mk_out, 16 * len(PAIRS))
                        sp.wait_ge(consts_in, 16)

                    @block.gpsimd
                    def _(pool):
                        nc.gpsimd.memset(V[:, :, :, DK:VW], 1.0).then_inc(s_ones, 1)
                        nc.gpsimd.memset(zeros[:], 0.0).then_inc(s_ones, 1)
                        nc.gpsimd.memset(kvx[:], 0.0).then_inc(s_ones, 1)
                        pool.wait_ge(s_ones, 3)
                        nc.gpsimd.memset(kx[KS:KS + 3, :], 1.0).then_inc(s_ones, 1)
                        pool.wait_ge(s_ones, 4)
                        nc.gpsimd.memset(mk[:], 0.0).then_inc(s_ones, 1)
                        pool.wait_ge(s_ones, 5)
                        for n in range(len(units)):
                            pool.wait_ge(p2_ready, n + 1)
                            if n:
                                pool.wait_ge(p3_ready, n)
                            nc.gpsimd.tensor_tensor(parts[:, n % 2, 2], rest[:, n % 2], parts[:, n % 2, 1], ALU.subtract).then_inc(p3_ready, 1)

                    @block.tensor
                    def _(pe):
                        pe.wait_ge(s_w, 16 * 6)
                        for n, (t, m, c) in enumerate(units):
                            if c and (t, m) == (0, 0):
                                pe.wait_ge(s_x[c], 16 * 3)
                            if n >= 2:
                                pe.wait_ge(qk_read, n - 1)
                            for s in range(2):
                                for k in range(KD):
                                    last = nc.tensor.matmul(pq[:, n % 2, s], w_sb[:, 2 * t + s, k, m * P:(m + 1) * P],
                                                            xT_sb[:, k, c * C:(c + 1) * C], start=(k == 0), stop=(k == KD - 1))
                            last.then_inc(qk_ready, 1)
                            if n >= 2:
                                pe.wait_ge(v_read, n - 1)
                            for k in range(KD):
                                last = nc.tensor.matmul(pv[:, n % 2, 0:D], xT_sb[:, k, n * P:(n + 1) * P], w_sb[:, 4, k, :],
                                                        start=(k == 0), stop=(k == KD - 1))
                            last.then_inc(v_ready, 1)
                            i = n - MK_AT
                            if i == 0:
                                pe.wait_ge(s_ctx, 32)
                            if 0 <= i < len(mk_cols):
                                a, b = mk_cols[i]
                                if i >= 2:
                                    pe.wait_ge(mk_copied, i - 1)
                                for k in range(KD):
                                    last = nc.tensor.matmul(pk[0:DK, i % 2, 0:b - a], wkv_sb[:, k, 0:DK], ctx_sb[:, k, a:b],
                                                            start=(k == 0), stop=(k == KD - 1))
                                last.then_inc(mk_ready, 1)
                            if i == len(mk_cols):
                                pe.wait_ge(mk_copied, len(mk_cols))
                                for r in range(MT):
                                    rows = min(P, M - r * P)
                                    for k in range(KD):
                                        last = nc.tensor.matmul(pk[0:rows, 0, r * 2 * DK:(r + 1) * 2 * DK], ctx_sb[:, k, r * P:r * P + rows],
                                                                wkv_sb[:, k, :], start=(k == 0), stop=(k == KD - 1))
                                last.then_inc(mv_ready, 1)

                    @block.scalar
                    def _(act):
                        for n in range(len(units)):
                            i = n - MK_AT - 1
                            if i == 0:
                                act.wait_ge(s_ones, 5)
                            if 0 <= i < len(mk_cols):
                                a, b = mk_cols[i]
                                act.wait_ge(mk_ready, i + 1)
                                nc.scalar.copy(mk[:, a:b], pk[0:DK, i % 2, 0:b - a]).then_inc(mk_copied, 1)
                            if i == len(mk_cols):
                                act.wait_ge(mk_copied, len(mk_cols))
                                nc.scalar.copy(mk_parts[:, 0], mk[:]).then_inc(mk1, 1)
                            if i == len(mk_cols) + 3:
                                act.wait_ge(mkr, 1)
                                nc.scalar.copy(mk_parts[:, 1], mk_rest[:]).then_inc(mk2, 1)
                            act.wait_ge(whole_ready, n + 1)
                            if n >= 2:
                                act.wait_ge(s_parts_out[n % 2], 16 * (n // 2))
                            nc.scalar.copy(parts[:, n % 2, 0], whole[:, n % 2]).then_inc(p1_ready, 1)
                            act.wait_ge(rest_ready, n + 1)
                            nc.scalar.copy(parts[:, n % 2, 1], rest[:, n % 2]).then_inc(p2_ready, 1)

                    @block.vector
                    def _(dve):
                        link = chain(dve, "rope_chain")
                        dve.wait_ge(s_b, 16 * 7)
                        for n in range(len(units)):
                            t, m, c = units[n]
                            if c and (t, m) == (0, 0):
                                dve.wait_ge(s_x[c], 16 * 3)
                            dve.wait_ge(qk_ready, n + 1)
                            if n >= 2:
                                dve.wait_ge(p1_ready, n - 1)
                            for s in range(2):
                                last = nc.vector.scalar_tensor_tensor(
                                    out=turned[:, n % 2, s], in0=pq[:, n % 2, s], scalar=bias[:, 2 * t + s, m:m + 1],
                                    in1=cs[:, s, c * C:(c + 1) * C], op0=ALU.add, op1=ALU.mult)
                            last.then_inc(qk_read, 1)
                            dve.wait_ge(v_ready, n + 1)
                            nc.vector.tensor_tensor(V[:, n, :, 0:DK], pv[:, n % 2, 0:D].rearrange("p (h d) -> p h d", h=H),
                                                    bv_all[:].rearrange("p (h d) -> p h d", h=H), ALU.add).then_inc(v_read, 1)
                            dve.wait_ge(qk_read, n + 1)
                            nc.vector.tensor_tensor(whole[:, n % 2], turned[:, n % 2, 0], turned[:, n % 2, 1], ALU.add).then_inc(whole_ready, 1)
                            dve.wait_ge(p1_ready, n + 1)
                            if n >= 2:
                                dve.wait_ge(p3_ready, n - 1)
                            nc.vector.tensor_tensor(rest[:, n % 2], whole[:, n % 2], parts[:, n % 2, 0], ALU.subtract).then_inc(rest_ready, 1)
                            i = n - MK_AT - len(mk_cols)
                            if i == 2:
                                dve.wait_ge(s_ones, 5)
                                dve.wait_ge(mv_ready, 1)
                                for a, b, rows in ((0, M // P, P), (M // P, MT, M % P)):
                                    found = pk[0:rows, 0, a * 2 * DK:b * 2 * DK].rearrange("p (n d) -> p n d", d=2 * DK)
                                    nc.vector.tensor_copy(kvx[0:rows, a:b, 0:2 * DK], found)
                                    last = nc.vector.memset(kvx[0:rows, a:b, 2 * DK:DK + VW], 1.0)
                                link(last)
                            if i == 3:
                                dve.wait_ge(mk1, 1)
                                nc.vector.tensor_tensor(mk_rest[:], mk[:], mk_parts[:, 0], ALU.subtract).then_inc(mkr, 1)
                            if i == 5:
                                dve.wait_ge(mk2, 1)
                                nc.vector.tensor_tensor(mk_parts[:, 2], mk_rest[:], mk_parts[:, 1], ALU.subtract).then_inc(mk3, 1)

            def attention(tag, scope, plans, flag, ones_rows, loads, pieces, o_of, causal_sb):
                probs = sb(scope, f"{tag}_probs", [P, 3, GH, C])
                acc_sb = sb(scope, f"{tag}_acc", [P, 2, C])
                piece_max = sb(scope, f"{tag}_piece_max", [P, 2, UR, 4])
                row_max = sb(scope, f"{tag}_row_max", [P, 2, UR])
                shift = sb(scope, f"{tag}_shift", [UR, 2, 2, P], BF16)
                junk = sb(scope, f"{tag}_junk", [P, SB, C], BF16) if causal_sb is not None else None
                inverse = sb(scope, f"{tag}_inverse", [P, 2, C // P, GH])
                mark = sb(scope, f"{tag}_mark", [P, 1])
                ps = psum(scope, f"{tag}_scores", [P, GH, C])
                po = psum(scope, f"{tag}_out", [P, C])
                pm = psum(scope, f"{tag}_max", [P, SB, C])
                s_load = [sem(f"{tag}_load{n}") for n in range(len(loads))]
                scores_ready, probs_ready, probs_masked, probs_used = (
                    sem(f"{tag}_scores_ready"), sem(f"{tag}_probs_ready"), sem(f"{tag}_probs_masked"), sem(f"{tag}_probs_used"))
                side_ready, side_read = sem(f"{tag}_side_ready"), sem(f"{tag}_side_read")
                acc_copied, inverse_ready = sem(f"{tag}_acc_copied"), sem(f"{tag}_inverse_ready")
                max_ready, shift_high, shift_ready = sem(f"{tag}_max_ready"), sem(f"{tag}_shift_high"), sem(f"{tag}_shift_ready")
                shift_in = [sem(f"{tag}_shift_in{i}") for i in range(2)]
                s_set = sem(f"{tag}_set")
                if pieces:
                    first_done, split_done = sem(f"{tag}_first_done"), sem(f"{tag}_split_done")
                    piece_in = [sem(f"{tag}_piece_in{i}") for i in range(2)]
                    raw = sb(scope, f"{tag}_raw", [P, 2, max(first.shape[1] * first.shape[2] for _, first, _ in pieces)])

                def schedule(steps, works):
                    stream = []
                    for u, work in enumerate(works):
                        stream += [("piece", u, k) for k in range(len(work["pieces"]))]
                        stream.append(("turn", u))
                    order, late = [], []
                    for item in stream:
                        if item[0] == "turn" and item[1]:
                            late.append([3, item])
                            continue
                        order.append(item)
                        for w in late:
                            w[0] -= 1
                        order += [w[1] for w in late if w[0] == 0]
                        late = [w for w in late if w[0] > 0]
                    order += [w[1] for w in late]
                    first_of = {}
                    for i, st in enumerate(steps):
                        first_of.setdefault(st["unit"], i)
                    where = {item: n for n, item in enumerate(order)}
                    before = order[:where[("turn", 0)] + 1]
                    due, at = [], len(before)
                    side = []
                    for i in range(len(steps)):
                        need = at
                        for u in range(len(works)):
                            if first_of[u] - LEAD > i:
                                left = where[("turn", u)] + 1 - at
                                need = max(need, at + -(-left // (first_of[u] - LEAD - i)))
                            elif first_of[u] > i:
                                need = max(need, where[("turn", u)] + 1)
                        need = min(max(need, min(at + EVEN, len(order))), len(order))
                        side.append(order[at:need])
                        at = need
                    assert at == len(order)
                    side += [[], [], []]
                    for i, st in enumerate(steps):
                        if st["last"]:
                            side[i + 2] = side[i + 2] + [("sums", st["unit"])]
                    thirds = [[it[0:(len(it) + 2) // 3], it[(len(it) + 2) // 3:(2 * len(it) + 2) // 3], it[(2 * len(it) + 2) // 3:]] for it in side]
                    diag_before = [0]
                    for st in steps:
                        diag_before.append(diag_before[-1] + st["diag"])
                    return steps, works, first_of, before, thirds, diag_before

                plans = [schedule(*p) for p in plans]

                def either(eng, program):
                    if flag is None:
                        program(*plans[0])
                        return
                    chosen = eng.value_load(flag[0:1, 0:1])
                    with eng.If(chosen > 0):
                        program(*plans[0])
                    with eng.Else():
                        program(*plans[1])

                with nc.Block() as block:
                    @block.sync
                    def _(sp):
                        def load(n):
                            for dst, src in loads[n]:
                                sp.dma_start(dst, src).then_inc(s_load[n], 16)

                        for n in range(2):
                            load(n)

                        def program(steps, works, first_of, before, thirds, diag_before):
                            for u, work in enumerate(works):
                                sp.wait_ge(shift_ready, u + 1)
                                for b, dst in enumerate(work["shift_to"]):
                                    sp.dma_start(dst, shift[:, u % 2, b]).then_inc(shift_in[u % 2], 16)
                                if u + 2 < len(loads):
                                    load(u + 2)
                                if u == len(loads) and pieces:
                                    load_pieces(sp, pieces, raw, piece_in, split_done)
                            for i in range(2):
                                sp.wait_ge(shift_in[i], 16 * len(works))

                        either(sp, program)

                    @block.gpsimd
                    def _(pool):
                        ones_ahead = NC if causal_sb is not None else len(ones_rows)
                        for n, ap in enumerate(ones_rows[0:ones_ahead]):
                            if n:
                                pool.wait_ge(s_set, n)
                            nc.gpsimd.memset(ap, 1.0).then_inc(s_set, 1)

                        def program(steps, works, first_of, before, thirds, diag_before):
                            for i, st in enumerate(steps):
                                if st["first"] and ones_ahead + st["unit"] < len(ones_rows):
                                    pool.wait_ge(s_set, ones_ahead + st["unit"])
                                    if diag_before[i]:
                                        pool.wait_ge(probs_masked, diag_before[i])
                                    nc.gpsimd.memset(ones_rows[ones_ahead + st["unit"]], 1.0).then_inc(s_set, 1)
                                if st["diag"]:
                                    pool.wait_ge(probs_ready, 2 * (i + 1))
                                    pool.wait_ge(s_set, min(len(ones_rows), ones_ahead + st["unit"] + 1))
                                    blk = probs[:, i % 3, :, st["off"]:st["off"] + P]
                                    nc.gpsimd.affine_select(out=blk, in_=blk, compare_op=ALU.is_ge, fill=0.0, base=0,
                                                            pattern=[[0, GH], [1, P]], channel_multiplier=-1).then_inc(probs_masked, 1)

                        if causal_sb is not None:
                            either(pool, program)
                        if pieces:
                            pool.wait_ge(s_set, len(ones_rows))
                        for n in range(len(pieces)):
                            if n:
                                pool.wait_ge(split_done, n)
                            first_of_piece(pool, nc.gpsimd.tensor_copy, n, pieces, raw, piece_in, first_done)
                            rest_of_piece(pool, n, pieces, raw, first_done, split_done)
                        if pieces:
                            pool.wait_ge(split_done, len(pieces))

                    @block.tensor
                    def _(pe):
                        def program(steps, works, first_of, before, thirds, diag_before):
                            uses, loaded = [0], [0]
                            nc.tensor.matmul(po[:], zeros[:, 0:P], zeros[:], start=True, stop=True)

                            def side_item(item):
                                n = uses[0]
                                uses[0] += 1
                                if n >= SB:
                                    pe.wait_ge(side_read, n - SB + 1)
                                slot = pm[:, n % SB]
                                if item[0] == "piece":
                                    pc = works[item[1]]["pieces"][item[2]]
                                    while loaded[0] < pc["load"]:
                                        pe.wait_ge(s_load[loaded[0]], 16 * len(loads[loaded[0]]))
                                        loaded[0] += 1
                                    if causal_sb is None and item[2] == 0:
                                        pe.wait_ge(s_set, item[1] + 1)
                                    mm = nc.tensor.matmul(slot[:, 0:pc["w"]], pc["lhsT"], pc["rhs"], start=True, stop=True)
                                elif item[0] == "turn":
                                    pe.wait_ge(max_ready, item[1] + 1)
                                    mm = nc.tensor.transpose(slot[0:UR, 0:P], row_max[:, item[1] % 2], ident[:])
                                else:
                                    pe.wait_ge(acc_copied, item[1] + 1)
                                    for q in range(C // P):
                                        mm = nc.tensor.transpose(slot[:, q * P:(q + 1) * P], acc_sb[:, item[1] % 2, q * P:(q + 1) * P], ident[:])
                                mm.then_inc(side_ready, 1)

                            def scores(i, pair):
                                st = steps[i]
                                if i:
                                    pe.wait_ge(probs_ready, 2 * (i - 1) + pair + 1)
                                for j in (2 * pair, 2 * pair + 1):
                                    mm = nc.tensor.matmul(ps[:, j, st["off"]:C], st["keys"](j), st["queries"](j), start=True, stop=True)
                                mm.then_inc(scores_ready, 1)

                            def values(i):
                                st = steps[i]
                                pe.wait_ge(probs_ready, 2 * (i + 1))
                                if st["diag"]:
                                    pe.wait_ge(probs_masked, diag_before[i + 1])
                                if st["first"] and st["unit"]:
                                    pe.wait_ge(acc_copied, st["unit"])
                                for j in range(GH):
                                    mm = nc.tensor.matmul(po[32 * j:32 * j + VW, st["off"]:C], st["values"](j),
                                                          probs[:, i % 3, j, st["off"]:C], start=st["first"], stop=st["last"],
                                                          tile_position=(0, 32 * j))
                                mm.then_inc(probs_used, 1)

                            for item in before:
                                side_item(item)
                            for i in range(len(thirds)):
                                if i < len(steps):
                                    if first_of[steps[i]["unit"]] == i:
                                        u = steps[i]["unit"]
                                        pe.wait_ge(shift_in[u % 2], 32 * (u // 2 + 1))
                                        pe.wait_ge(s_set, u + 1)
                                    scores(i, 0)
                                for item in thirds[i][0]:
                                    side_item(item)
                                if i < len(steps):
                                    scores(i, 1)
                                for item in thirds[i][1]:
                                    side_item(item)
                                if 1 <= i <= len(steps):
                                    values(i - 1)
                                for item in thirds[i][2]:
                                    side_item(item)

                        either(pe, program)

                    @block.scalar
                    def _(act):
                        def program(steps, works, first_of, before, thirds, diag_before):
                            for i, st in enumerate(steps):
                                for pair in range(2):
                                    act.wait_ge(scores_ready, 2 * i + pair + 1)
                                    if i >= 3 and pair == 0:
                                        act.wait_ge(probs_used, i - 2)
                                    nc.scalar.activation(probs[:, i % 3, 2 * pair:2 * pair + 2, st["off"]:C],
                                                         ps[:, 2 * pair:2 * pair + 2, st["off"]:C], ACT.Exp,
                                                         scale=SCALE).then_inc(probs_ready, 1)

                        either(act, program)

                    @block.vector
                    def _(dve):
                        link = chain(dve, f"{tag}_dve_chain")
                        link(nc.vector.memset(piece_max[:], LOW))

                        def program(steps, works, first_of, before, thirds, diag_before):
                            uses = [0]

                            def side_item(item):
                                n = uses[0]
                                uses[0] += 1
                                dve.wait_ge(side_ready, n + 1)
                                slot = pm[:, n % SB]
                                if item[0] == "piece":
                                    u = item[1]
                                    pc = works[u]["pieces"][item[2]]
                                    to = piece_max[:, u % 2, pc["row"], pc["at"]:pc["at"] + 1]
                                    if pc["diag"]:
                                        ins = nc.vector.tensor_tensor_reduce(out=junk[:, n % SB, 0:pc["w"]], in0=slot[:, 0:pc["w"]],
                                                                             in1=causal_sb[:, C - pc["w"]:C], scale=1.0, scalar=LOW,
                                                                             op0=ALU.add, op1=ALU.max, accum_out=to)
                                    else:
                                        ins = nc.vector.tensor_reduce(to, slot[:, 0:pc["w"]], AX.X, ALU.max)
                                    ins.then_inc(side_read, 1)
                                    if item[2] == len(works[u]["pieces"]) - 1:
                                        dve.wait_ge(side_read, n + 1)
                                        nc.vector.tensor_reduce(row_max[:, u % 2], piece_max[:, u % 2], AX.X, ALU.max).then_inc(max_ready, 1)
                                elif item[0] == "turn":
                                    u = item[1]
                                    if u >= 2:
                                        dve.wait_ge(shift_in[u % 2], 32 * (u // 2))
                                    nc.vector.tensor_scalar(shift[:, u % 2, 0], slot[0:UR, 0:P], -1.0, None, ALU.mult).then_inc(shift_high, 1)
                                    dve.wait_ge(shift_high, u + 1)
                                    nc.vector.scalar_tensor_tensor(out=shift[:, u % 2, 1], in0=slot[0:UR, 0:P], scalar=-1.0,
                                                                   in1=shift[:, u % 2, 0], op0=ALU.mult,
                                                                   op1=ALU.subtract).then_inc(shift_ready, 1)
                                    dve.wait_ge(shift_ready, u + 1)
                                    nc.vector.memset(mark[:], 0.0).then_inc(side_read, 1)
                                else:
                                    u = item[1]
                                    heads = slot.rearrange("p (q j i) -> p q j i", j=GH, i=32)
                                    nc.vector.reciprocal(inverse[:, u % 2], heads[:, :, :, DK]).then_inc(inverse_ready, 1)
                                    dve.wait_ge(inverse_ready, u + 1)
                                    nc.vector.tensor_tensor(o_of(u), heads[:, :, :, 0:DK],
                                                            inverse[:, u % 2].rearrange("p q (j o) -> p q j o", o=1).to_broadcast([P, C // P, GH, DK]),
                                                            ALU.mult).then_inc(side_read, 1)

                            for item in before:
                                side_item(item)
                            for i in range(len(thirds)):
                                for item in thirds[i][0] + thirds[i][1]:
                                    side_item(item)
                                if 1 <= i <= len(steps) and steps[i - 1]["last"]:
                                    u = steps[i - 1]["unit"]
                                    dve.wait_ge(probs_used, i)
                                    nc.vector.tensor_copy(acc_sb[:, u % 2], po[:]).then_inc(acc_copied, 1)
                                for item in thirds[i][2]:
                                    side_item(item)

                        either(dve, program)

            stage = ExitStack()
            with stage:
                stack_q = [sb(stage, f"stack_q{g}", [P, NC, GH, C], BF16) for g in range(NG)]
                stack_k = [sb(stage, f"stack_k{g}", [P, GH, T], BF16) for g in range(NG)]
                causal_sb = sb(stage, "causal_sb", [P, C])
                loads = []
                for g, c0, c1 in [(0, c, c + 1) for c in range(NC)] + [(g, 0, NC) for g in range(1, NG)]:
                    pairs = [(causal_sb[:], causal)] if not loads else []
                    heads = slice(g * GH * DK, (g + 1) * GH * DK)
                    cols = slice(c0 * C, c1 * C)
                    for n, (a, b) in enumerate(PAIRS):
                        rows = slice(n * DK, (n + 1) * DK)
                        for c in range(c0, c1):
                            pairs.append((stack_q[g][rows, c], qparts[a, heads, c * C:(c + 1) * C].rearrange("(h i) t -> i h t", i=DK)))
                        pairs.append((stack_k[g][rows, :, cols], kparts[b, heads, cols].rearrange("(h i) t -> i h t", i=DK)))
                    loads.append(pairs)

                steps, works = [], []
                chunks = [(g, c) for g in range(NG) for c in (range(NC) if g < NG - 1 else range(NC)[::-1])]
                for u, (g, c) in enumerate(chunks):
                    pieces = []
                    for q in range(C // P):
                        end = c * C + (q + 1) * P
                        for j in range(GH):
                            for n, a in enumerate(range(0, end, C)):
                                b = min(a + C, end)
                                pieces.append(dict(w=b - a, lhsT=stack_q[g][0:KS, c, j, q * P:(q + 1) * P],
                                                   rhs=stack_k[g][0:KS, j, a:b], row=j * GH + q, at=n,
                                                   diag=b == end, load=c + 1 if g == 0 else NC + g))
                    works.append(dict(pieces=pieces,
                                      shift_to=[stack_q[g][KS + b:KS + b + 1, c].rearrange("o h (n t) -> o (h n) t", t=P) for b in range(2)]))
                    for kt in range((c + 1) * C // P):
                        off = max(0, kt * P - c * C)
                        steps.append(dict(
                            unit=u, off=off, diag=int(kt * P >= c * C), first=kt == 0, last=kt == (c + 1) * C // P - 1,
                            keys=lambda j, g=g, kt=kt: stack_k[g][0:KS + 2, j, kt * P:(kt + 1) * P],
                            queries=lambda j, g=g, c=c, off=off: stack_q[g][0:KS + 2, c, j, off:C],
                            values=lambda j, g=g, kt=kt: V[:, kt, g * GH + j, :]))
                attention("self", stage, [(steps, works)], None, [stack_k[g][KS:KS + 2, :, c * C:(c + 1) * C] for g in range(NG) for c in range(NC)], loads, [],
                          lambda u: o_unit(*chunks[u]), causal_sb)

        def project_norm(tag, scope, w_dram, res_dram, bias_dram, x_sb, xT_parts, pieces, slots):
            w_sb = sb(scope, f"{tag}_w", [P, KD, D])
            oT = sb(scope, f"{tag}_oT", [P, KD, T])
            b_sb = sb(scope, f"{tag}_b", [P, D])
            stats = sb(scope, f"{tag}_stats", [P, NT, 6])
            mv = sb(scope, f"{tag}_mv", [P, NT, 2])
            rstd = sb(scope, f"{tag}_rstd", [P, NT])
            raw = sb(scope, f"{tag}_raw", [P, slots, max(first.shape[1] * first.shape[2] for _, first, _ in pieces)])
            py = psum(scope, f"{tag}_py", [P, 2, C])
            pt = psum(scope, f"{tag}_pt", [P, 3, C])
            s_w = sem(f"{tag}_w_in")
            if bias_dram is not None:
                s_in, s_more, res_ready = sem(f"{tag}_in"), sem(f"{tag}_more_in"), sem(f"{tag}_res_ready")
            y_ready, y_read = sem(f"{tag}_y_ready"), sem(f"{tag}_y_read")
            normed = sem(f"{tag}_normed")
            var_ready, std_ready = sem(f"{tag}_var_ready"), sem(f"{tag}_std_ready")
            t_ready, t_read = sem(f"{tag}_t_ready"), sem(f"{tag}_t_read")
            rest_read, first_done, split_done = sem(f"{tag}_rest_read"), sem(f"{tag}_first_done"), sem(f"{tag}_split_done")
            piece_in = [sem(f"{tag}_piece_in{i}") for i in range(slots)]
            banks = [(src, c, k) for src in range(2) for c in range(NC) for k in range(KD)]

            with nc.Block() as block:
                @block.sync
                def _(sp):
                    sp.dma_start(w_sb[:], kt_view(w_dram)).then_inc(s_w, 16)
                    if res_dram is not None:
                        rows = res_dram.rearrange("(n p) d -> p n d", p=P)
                        sp.dma_start(x_sb[:, 0:TC], rows[:, 0:TC]).then_inc(s_in, 16)
                        sp.dma_start(b_sb[:], bias_dram.rearrange("(a n) -> a n", a=1).to_broadcast([P, D])).then_inc(s_in, 16)
                        sp.dma_start(x_sb[:, TC:NT], rows[:, TC:NT]).then_inc(s_more, 16)
                    load_pieces(sp, pieces, raw, piece_in, split_done)

                @block.gpsimd
                def _(pool):
                    if bias_dram is not None:
                        pool.wait_ge(s_in, 32)
                        for n in range(NT):
                            if n == TC:
                                pool.wait_ge(s_more, 16)
                            nc.gpsimd.tensor_tensor(x_sb[:, n], x_sb[:, n], b_sb[:], ALU.add).then_inc(res_ready, 1)
                    for n in range(len(pieces)):
                        rest_of_piece(pool, n, pieces, raw, first_done, split_done)
                    pool.wait_ge(split_done, len(pieces))

                @block.tensor
                def _(pe):
                    def turn(n):
                        src, c, k = banks[n]
                        if n >= 3:
                            pe.wait_ge(t_read, n - 2)
                        if n >= KD * NC + 3:
                            pe.wait_ge(rest_read, n - 2 - KD * NC)
                        if src:
                            pe.wait_ge(normed, 4 * (c + 1))
                        for q in range(4):
                            mm = nc.tensor.transpose(pt[:, n % 3, q * P:(q + 1) * P],
                                                     (o_tok, x_sb)[src][:, 4 * c + q, k * P:(k + 1) * P], ident[:])
                        mm.then_inc(t_ready, 1)

                    def turns(n):
                        for k in range(KD):
                            turn(n * KD + k)

                    turns(0)
                    pe.wait_ge(s_w, 16)
                    for c in range(NC):
                        if c + 1 < NC:
                            turns(c + 1)
                        pe.wait_ge(t_read, (c + 1) * KD)
                        for n in range(TC * c, TC * (c + 1)):
                            if n >= 2:
                                pe.wait_ge(y_read, n - 1)
                            for k in range(KD):
                                mm = nc.tensor.matmul(py[:, n % 2, 0:D], oT[:, k, n * P:(n + 1) * P], w_sb[:, k], start=(k == 0), stop=(k == KD - 1))
                            mm.then_inc(y_ready, 1)
                        if c >= 2:
                            turns(NC + c - 2)
                    turns(2 * NC - 2)
                    turns(2 * NC - 1)

                @block.scalar
                def _(act):
                    for n, (src, c, k) in enumerate(banks):
                        act.wait_ge(t_ready, n + 1)
                        nc.scalar.copy((oT, xT_parts[0])[src][:, k, c * C:(c + 1) * C], pt[:, n % 3]).then_inc(t_read, 1)
                        if n >= 3 and n - 3 < len(pieces):
                            first_of_piece(act, nc.scalar.copy, n - 3, pieces, raw, piece_in, first_done)
                        if k == KD - 1 and 2 <= n // KD < 2 + NC:
                            deviation(act, n // KD - 2, rstd, var_ready, std_ready)

                @block.vector
                def _(dve):
                    link = chain(dve, f"{tag}_norm_chain")

                    def rest_of(c):
                        for k in range(KD):
                            n = (NC + c) * KD + k
                            dve.wait_ge(t_read, n + 1)
                            nc.vector.tensor_tensor(xT_parts[1][:, k, c * C:(c + 1) * C], pt[:, n % 3],
                                                    xT_parts[0][:, k, c * C:(c + 1) * C].bitcast(F32), ALU.subtract).then_inc(rest_read, 1)

                    for c in range(NC):
                        for n in range(TC * c, TC * (c + 1)):
                            dve.wait_ge(y_ready, n + 1)
                            if bias_dram is not None:
                                dve.wait_ge(res_ready, n + 1)
                            nc.vector.tensor_tensor(x_sb[:, n], py[:, n % 2, 0:D], x_sb[:, n], ALU.add).then_inc(y_read, 1)
                            if n % TC:
                                dve.wait_ge(y_read, n)
                                nc.vector.bn_stats(stats[:, n - 1], x_sb[:, n - 1])
                        dve.wait_ge(y_read, TC * (c + 1))
                        link(nc.vector.bn_stats(stats[:, n], x_sb[:, n]))
                        variance(link, c, stats, mv, rstd, var_ready)
                        if c:
                            normalise(dve, link, c - 1, x_sb, mv, rstd, std_ready, normed)
                        if c >= 2:
                            rest_of(c - 2)
                    normalise(dve, link, NC - 1, x_sb, mv, rstd, std_ready, normed)
                    for c in range(NC - 2, NC):
                        rest_of(c)

        def variance(link, c, stats, mv, rstd, var_ready):
            for n in range(TC * c, TC * (c + 1)):
                last = nc.vector.bn_aggr(mv[:, n], stats[:, n])
            link(last)
            nc.vector.tensor_scalar_add(rstd[:, TC * c:TC * (c + 1)], mv[:, TC * c:TC * (c + 1), 1], EPS).then_inc(var_ready, 1)

        def deviation(act, c, rstd, var_ready, std_ready):
            act.wait_ge(var_ready, c + 1)
            nc.scalar.activation(rstd[:, TC * c:TC * (c + 1)], rstd[:, TC * c:TC * (c + 1)], ACT.Sqrt).then_inc(std_ready, 1)

        def normalise(dve, link, c, x_sb, mv, rstd, std_ready, normed):
            dve.wait_ge(std_ready, c + 1)
            link(nc.vector.reciprocal(rstd[:, TC * c:TC * (c + 1)], rstd[:, TC * c:TC * (c + 1)]))
            for n in range(TC * c, TC * (c + 1)):
                nc.vector.tensor_scalar(x_sb[:, n], x_sb[:, n], mv[:, n, 0:1], rstd[:, n:n + 1],
                                        ALU.subtract, ALU.mult).then_inc(normed, 1)

        tail = ExitStack()
        with tail:
            x_sb = sb(tail, "x_sb", [P, NT, D])
            stage = ExitStack()
            with stage:
                x1T = [sb(stage, f"x1T_{n}", [P, KD, T], F32R) for n in ("first", "rest")]
                ctx2 = [sb(stage, f"ctx2_{n}", [P, KD, MP2], F32R) for n in ("first", "rest")]
                xwq_sb = [sb(stage, f"xwq_{n}", [P, KD, D], F32R) for n in ("first", "rest")]
                inner = ExitStack()
                with inner:
                    project_norm("n1", inner, wo, x, bo, x_sb, x1T,
                                 [(xwq, xwq_sb[0][:], xwq_sb[1][:])]
                                 + [(ctxT[k * P:(k + 1) * P], ctx2[0][:, k:k + 1], ctx2[1][:, k:k + 1]) for k in range(KD)], 1 + KD)

                inner = ExitStack()
                with inner:
                    parts = sb(inner, "xparts_sb", [P, 2, 3, C], BF16)
                    rest = sb(inner, "xrest_sb", [P, 2, C])
                    qp = [sb(inner, f"qp_{n}", [P, KD, T], F32R) for n in ("first", "rest")]
                    iota_sb = sb(inner, "iota_sb", [P, M])
                    near = sb(inner, "near", [P, 2, MP2])
                    best = sb(inner, "best", [P, 2, 8])
                    place = sb(inner, "place", [P, 2, 8], U32)
                    place_f = sb(inner, "place_f", [P, 2, 1])
                    chosen = sb(inner, "chosen", [P, 2, MP], BF16)
                    ones_b = sb(inner, "ones_b", [P, P], BF16)
                    zeros_b = sb(inner, "zeros_b", [P, C], BF16)
                    below_sb = sb(inner, "below_sb", [P, P])
                    below_b = sb(inner, "below_b", [P, P], BF16)
                    count = sb(inner, "count", [P, MT])
                    absent = sb(inner, "absent", [P, MT])
                    used = sb(inner, "used", [P, MT + 1], BF16)
                    place_of = sb(inner, "place_of", [P, MT])
                    sel = sb(inner, "sel", [P, 4, FEW], BF16)
                    row_parts = sb(inner, "row_parts", [P, MT, RW], BF16)
                    row_rest = sb(inner, "row_rest", [P, MT, 2 * DK])
                    few_rows = sb(inner, "few_rows", [P, FT, KS + 3])
                    few_values = sb(inner, "few_values", [P, FT, DK])
                    few_count = sb(inner, "few_count", [P, FT, 1])
                    pp = psum(inner, "pp", [P, 4, C])
                    pq = psum(inner, "pq2", [P, 2, C])
                    pc = psum(inner, "pc", [P, C])
                    pa = psum(inner, "pa", [P, C])
                    s_iota, set2 = sem("iota_in"), sem("set2")
                    s_xout = [sem(f"xparts_out{i}") for i in range(2)]
                    q_ready, q_copied, qp_ready, xp1, xrest, xp2, xp3 = (
                        sem("xq_ready"), sem("xq_copied"), sem("qp_ready"), sem("xp1"), sem("xrest"), sem("xp2"), sem("xp3"))
                    near_ready, near_copied, near_best, near_placed, near_place_f, chosen_ready, counted = (
                        sem("near_ready"), sem("near_copied"), sem("near_best"), sem("near_placed"), sem("near_place_f"),
                        sem("chosen_ready"), sem("counted"))
                    absent_ready, absent_turned, mask_ready, mask_in = (
                        sem("absent_ready"), sem("absent_turned"), sem("mask_ready"), sem("mask_in"))
                    row_parts_done, row_counts_done, used_ready, ranks_ready, sel_ready, sel_used = (
                        sem("row_parts_done"), sem("row_counts_done"), sem("used_ready"), sem("ranks_ready"), sem("sel_ready"), sem("sel_used"))
                    few_rows_ready, few_mask_ready, few_turned, kx_few_ready = (
                        sem("few_rows_ready"), sem("few_mask_ready"), sem("few_turned"), sem("kx_few_ready"))
                    qunits = [(m, c) for c in range(NC) for m in range(KD)]
                    cols = [(a, min(a + C, MP2)) for a in range(0, MP2, C)]
                    ahead = [[] for _ in range(NT)]
                    for n, (m, c) in enumerate(qunits):
                        ahead[max(1, TC * (c - 1) - 1) if c else 0].append(n)

                    with nc.Block() as block:
                        @block.sync
                        def _(sp):
                            sp.dma_start(iota_sb[:], iota).then_inc(s_iota, 16)
                            sp.dma_start(below_sb[:], below).then_inc(s_iota, 16)
                            for n, (m, c) in enumerate(qunits):
                                sp.wait_ge(xp3, n + 1)
                                sp.dma_start(xparts[:, m * P:(m + 1) * P, c * C:(c + 1) * C].rearrange("r p t -> p r t"),
                                             parts[:, n % 2]).then_inc(s_xout[n % 2], 16)
                            sp.wait_ge(mask_ready, 1)
                            sp.dma_start(kx[KS:KS + 1, :].rearrange("o (n t) -> o n t", t=P), maskx[:]).then_inc(mask_in, 16)
                            sp.wait_ge(mask_in, 16)
                            for i in range(2):
                                sp.wait_ge(s_xout[i], 8 * len(qunits))

                        @block.gpsimd
                        def _(pool):
                            link = chain(pool, "rows_chain")
                            nc.gpsimd.memset(ones_b[:], 1.0).then_inc(set2, 1)
                            nc.gpsimd.memset(zeros_b[:], 0.0).then_inc(set2, 1)
                            nc.gpsimd.memset(chosen[:], 0.0).then_inc(set2, 1)
                            nc.gpsimd.memset(used[:], 0.0).then_inc(set2, 1)
                            nc.gpsimd.memset(few_rows[:], 1.0).then_inc(set2, 1)
                            pool.wait_ge(s_iota, 32)
                            nc.gpsimd.tensor_copy(below_b[:], below_sb[:]).then_inc(set2, 1)
                            rows = kvx[:, :, 0:2 * DK]
                            part = [row_parts[:, :, n * 2 * DK:(n + 1) * 2 * DK] for n in range(3)]
                            link(nc.gpsimd.tensor_copy(part[0], rows))
                            link(nc.gpsimd.tensor_tensor(row_rest[:], rows, part[0], ALU.subtract))
                            link(nc.gpsimd.tensor_copy(part[1], row_rest[:]))
                            nc.gpsimd.tensor_tensor(part[2], row_rest[:], part[1], ALU.subtract).then_inc(row_parts_done, 1)

                        @block.tensor
                        def _(pe):
                            def project(n):
                                m, c = qunits[n]
                                if n >= 2:
                                    pe.wait_ge(xrest, n - 1)
                                    pe.wait_ge(xp1, n - 1)
                                for k in range(KD):
                                    mm = product(pq[:, n % 2], [w[:, k, m * P:(m + 1) * P] for w in xwq_sb],
                                                 [xt[:, k, c * C:(c + 1) * C] for xt in x1T], k == 0, k == KD - 1)
                                mm.then_inc(q_ready, 1)

                            def tally(n):
                                pe.wait_ge(chosen_ready, n + 1)
                                for t in range(MT):
                                    mm = nc.tensor.matmul(pc[:, t:t + 1], chosen[:, n % 2, t * P:(t + 1) * P], ones_b[:, 0:1],
                                                          start=False, stop=(n == NT - 1 and t == MT - 1), skip_group_check=True)
                                mm.then_inc(counted, 1)

                            pe.wait_ge(set2, 6)
                            nc.tensor.matmul(pc[:, 0:MT], zeros_b[:, 0:P], zeros_b[:, 0:MT], start=True, stop=False, skip_group_check=True)
                            u = 0
                            for n in range(NT):
                                for i in ahead[n]:
                                    project(i)
                                if n % TC == 0:
                                    pe.wait_ge(qp_ready, KD * (n // TC + 1))
                                for a, b in cols:
                                    if u >= 4:
                                        pe.wait_ge(near_copied, u - 3)
                                    for k in range(KD):
                                        mm = product(pp[:, u % 4, 0:b - a], [q[:, k, n * P:(n + 1) * P] for q in qp],
                                                     [w[:, k, a:b] for w in ctx2], k == 0, k == KD - 1)
                                    mm.then_inc(near_ready, 1)
                                    u += 1
                                if n >= 2:
                                    tally(n - 2)
                            tally(NT - 2)
                            tally(NT - 1)
                            pe.wait_ge(used_ready, 1)
                            pe.wait_ge(near_copied, NT * len(cols))
                            nc.tensor.matmul(pp[:, 0, 0:MT + 1], below_b[:], used[:], start=True, stop=False, skip_group_check=True)
                            for t in range(MT):
                                mm = nc.tensor.matmul(pp[:, 0, t + 1:MT + 1], ones_b[:], used[:, t:t + 1].to_broadcast([P, MT - t]),
                                                      start=False, stop=t == MT - 1, skip_group_check=True)
                            mm.then_inc(ranks_ready, 1)
                            pe.wait_ge(absent_ready, 1)
                            nc.tensor.transpose(pa[0:MT, 0:P], absent[:], ident[:]).then_inc(absent_turned, 1)
                            pe.wait_ge(row_parts_done, 1)
                            pe.wait_ge(row_counts_done, 2)
                            nc.tensor.matmul(pp[:, 1, 0:FT * RW], zeros_b[:, 0:P], zeros_b[:, 0:FT * RW], start=True, stop=False, skip_group_check=True)
                            for t in range(MT):
                                pe.wait_ge(sel_ready, t + 1)
                                for n in range(FT):
                                    mm = nc.tensor.matmul(pp[:, 1, n * RW:(n + 1) * RW], sel[:, t % 4, n * P:(n + 1) * P], row_parts[:, t],
                                                          start=False, stop=t == MT - 1, skip_group_check=True)
                                mm.then_inc(sel_used, 1)
                            pe.wait_ge(few_rows_ready, 1)
                            pe.wait_ge(few_mask_ready, 1)
                            for n in range(FT):
                                mm = nc.tensor.transpose(pp[0:KS + 3, 2, n * P:(n + 1) * P], few_rows[:, n], ident[:])
                            mm.then_inc(few_turned, 1)

                        @block.scalar
                        def _(act):
                            def split(n):
                                m, c = qunits[n]
                                act.wait_ge(q_ready, n + 1)
                                nc.scalar.copy(qp[0][:, m, c * C:(c + 1) * C], pq[:, n % 2]).then_inc(q_copied, 1)
                                if n >= 2:
                                    act.wait_ge(s_xout[n % 2], 16 * (n // 2))
                                nc.scalar.copy(parts[:, n % 2, 0], pq[:, n % 2]).then_inc(xp1, 1)

                            def split_rest(n):
                                act.wait_ge(xrest, n + 1)
                                nc.scalar.copy(parts[:, n % 2, 1], rest[:, n % 2]).then_inc(xp2, 1)

                            u = 0
                            for n in range(NT):
                                for i in ahead[n]:
                                    split(i)
                                for i in ahead[n]:
                                    split_rest(i)
                                for a, b in cols:
                                    act.wait_ge(near_ready, u + 1)
                                    if n >= 2:
                                        act.wait_ge(near_placed, n - 1)
                                    nc.scalar.copy(near[:, n % 2, a:b], pp[:, u % 4, 0:b - a]).then_inc(near_copied, 1)
                                    u += 1
                            act.wait_ge(set2, 5)
                            act.wait_ge(sel_used, MT)
                            found = pp[:, 1, 0:FT * RW].rearrange("p (n d) -> p n d", d=RW)
                            for i, (_, b) in enumerate(PAIRS):
                                last = nc.scalar.copy(few_rows[:, :, i * DK:(i + 1) * DK], found[:, :, 2 * b * DK:(2 * b + 1) * DK])
                            last.then_inc(few_rows_ready, 1)
                            act.wait_ge(few_turned, 1)
                            nc.scalar.copy(kx_few[0:KS + 3, :], pp[0:KS + 3, 2]).then_inc(kx_few_ready, 1)
                            act.wait_ge(kx_few_ready, 1)

                        @block.vector
                        def _(dve):
                            link = chain(dve, "choose_chain")

                            def split(n):
                                m, c = qunits[n]
                                mine = slice(c * C, (c + 1) * C)
                                dve.wait_ge(q_copied, n + 1)
                                dve.wait_ge(xp1, n + 1)
                                nc.vector.tensor_tensor(qp[1][:, m, mine], pq[:, n % 2], qp[0][:, m, mine].bitcast(F32), ALU.subtract).then_inc(qp_ready, 1)
                                if n >= 2:
                                    dve.wait_ge(xp3, n - 1)
                                nc.vector.tensor_tensor(rest[:, n % 2], pq[:, n % 2], parts[:, n % 2, 0], ALU.subtract).then_inc(xrest, 1)

                            def split_rest(n):
                                dve.wait_ge(xp2, n + 1)
                                nc.vector.tensor_tensor(parts[:, n % 2, 2], rest[:, n % 2], parts[:, n % 2, 1], ALU.subtract).then_inc(xp3, 1)

                            def place_of_best(n):
                                dve.wait_ge(near_placed, n + 1)
                                if n >= 2:
                                    dve.wait_ge(chosen_ready, n - 1)
                                nc.vector.tensor_copy(place_f[:, n % 2], place[:, n % 2, 0:1]).then_inc(near_place_f, 1)

                            def mark_chosen(n):
                                dve.wait_ge(near_place_f, n + 1)
                                if n >= 2:
                                    dve.wait_ge(counted, n - 1)
                                nc.vector.tensor_scalar(chosen[:, n % 2, 0:M], iota_sb[:], place_f[:, n % 2], None,
                                                        ALU.is_equal).then_inc(chosen_ready, 1)

                            for n in range(NT):
                                for i in ahead[n]:
                                    split(i)
                                for i in ahead[n]:
                                    split_rest(i)
                                dve.wait_ge(near_copied, len(cols) * (n + 1))
                                if n >= 2:
                                    dve.wait_ge(near_placed, n - 1)
                                nc.vector.max(best[:, n % 2], near[:, n % 2, 0:M]).then_inc(near_best, 1)
                                if n == 0:
                                    dve.wait_ge(s_iota, 32)
                                    dve.wait_ge(set2, 6)
                                else:
                                    place_of_best(n - 1)
                                    mark_chosen(n - 1)
                                dve.wait_ge(near_best, n + 1)
                                if n >= 2:
                                    dve.wait_ge(near_place_f, n - 1)
                                nc.vector.max_index(place[:, n % 2], best[:, n % 2], near[:, n % 2, 0:M]).then_inc(near_placed, 1)
                            place_of_best(NT - 1)
                            mark_chosen(NT - 1)
                            dve.wait_ge(counted, NT)
                            nc.vector.tensor_scalar(used[:, 0:MT], pc[:, 0:MT], 0.0, None, ALU.is_gt).then_inc(used_ready, 1)
                            link(nc.vector.tensor_copy(count[:], pc[:, 0:MT]))
                            nc.vector.tensor_scalar(absent[:], count[:], 0.0, MASKED, ALU.is_equal, ALU.mult).then_inc(absent_ready, 1)
                            counts = [row_parts[:, :, 6 * DK + n:6 * DK + n + 1].rearrange("p t o -> p (t o)") for n in range(2)]
                            nc.vector.tensor_copy(counts[0], count[:]).then_inc(row_counts_done, 1)
                            dve.wait_ge(ranks_ready, 1)
                            dve.wait_ge(row_counts_done, 1)
                            link(nc.vector.scalar_tensor_tensor(out=place_of[:], in0=pp[:, 0, 0:MT], scalar=1.0, in1=used[:, 0:MT],
                                                                op0=ALU.add, op1=ALU.mult))
                            nc.vector.tensor_tensor(counts[1], count[:], counts[0], ALU.subtract).then_inc(row_counts_done, 1)
                            link(nc.vector.tensor_scalar_add(place_of[:], place_of[:], -1.0))
                            for t in range(MT):
                                if t >= 4:
                                    dve.wait_ge(sel_used, t - 3)
                                nc.vector.tensor_scalar(sel[:, t % 4], iota_sb[:, 0:FEW], place_of[:, t:t + 1], None, ALU.is_equal).then_inc(sel_ready, 1)
                            link(nc.vector.tensor_scalar(few[:], pp[:, 0, MT:MT + 1], float(FEW), None, ALU.is_le))
                            dve.wait_ge(absent_turned, 1)
                            nc.vector.tensor_copy(maskx[:], pa[0:MT, 0:P]).then_inc(mask_ready, 1)
                            weights = kvx[:, :, DK:DK + VW]
                            dve.wait_ge(row_parts_done, 1)
                            link(nc.vector.tensor_tensor(weights, weights, count[:].rearrange("p (t o) -> p t o", o=1).to_broadcast([P, MT, VW]), ALU.mult))
                            dve.wait_ge(few_rows_ready, 1)
                            found = pp[:, 1, 0:FT * RW].rearrange("p (n d) -> p n d", d=RW)
                            nc.vector.tensor_copy(few_count[:], found[:, :, 6 * DK:6 * DK + 1])
                            link(nc.vector.tensor_copy(few_values[:], found[:, :, DK:2 * DK]))
                            nc.vector.tensor_tensor(few_count[:], few_count[:], found[:, :, 6 * DK + 1:6 * DK + 2], ALU.add)
                            link(nc.vector.tensor_tensor(few_values[:], few_values[:], found[:, :, 3 * DK:4 * DK], ALU.add))
                            dve.wait_ge(set2, 5)
                            nc.vector.tensor_scalar(few_rows[:, :, KS:KS + 1], few_count[:], 0.0, MASKED, ALU.is_equal, ALU.mult).then_inc(few_mask_ready, 1)
                            link(nc.vector.tensor_tensor(few_values[:], few_values[:], found[:, :, 5 * DK:6 * DK], ALU.add))
                            nc.vector.tensor_copy(vx_few[:, :, DK:VW], few_count[:])
                            link(nc.vector.tensor_tensor(vx_few[:, :, 0:DK], few_values[:], few_count[:].to_broadcast([P, FT, DK]), ALU.mult))

            w1_sb = [sb(tail, f"w1_{n}", [P, KD, W], F32R) for n in ("first", "rest")]
            w1_cut = W // 2
            stage = ExitStack()
            with stage:
                stackx = sb(stage, "stackx", [P, NC, H, C], BF16)
                loads = [[(stackx[n * DK:(n + 1) * DK, c], xparts[a, :, c * C:(c + 1) * C].rearrange("(h i) t -> i h t", i=DK))
                          for n, (a, _) in enumerate(PAIRS)] for c in range(NC)]

                def plan(keys, vals, n):
                    steps, works = [], []
                    width = C if n == FEW else n // 4
                    for c in range(NC):
                        for g in range(NG):
                            pieces = [dict(w=width, lhsT=stackx[0:KS + 1, c, g * GH + j, q * P:(q + 1) * P],
                                           rhs=keys[0:KS + 1, a * width:(a + 1) * width], row=j * GH + q, at=a, diag=False, load=c + 1)
                                      for j in range(GH) for q in range(C // P) for a in range(n // width)]
                            works.append(dict(pieces=pieces, shift_to=[
                                stackx[KS + 1 + b:KS + 2 + b, c, g * GH:(g + 1) * GH, :].rearrange("o h (n t) -> o (h n) t", t=P) for b in range(2)]))
                            for t in range(n // P):
                                steps.append(dict(unit=c * NG + g, off=0, diag=0, first=t == 0, last=t == n // P - 1,
                                                  keys=lambda j, t=t: keys[0:KS + 3, t * P:(t + 1) * P],
                                                  queries=lambda j, g=g, c=c: stackx[0:KS + 3, c, g * GH + j, :],
                                                  values=lambda j, t=t: vals(t)))
                    return steps, works

                attention("cross", stage, [plan(kx_few, lambda t: vx_few[:, t, :], FEW), plan(kx, lambda t: kvx[:, t, DK:DK + VW], MP)],
                          few, [stackx[KS:KS + 1, c, g * GH:(g + 1) * GH] for c in range(NC) for g in range(NG)], loads,
                          [(w1[k * P:(k + 1) * P, a:a + w1_cut], w1_sb[0][:, k:k + 1, a:a + w1_cut], w1_sb[1][:, k:k + 1, a:a + w1_cut])
                           for k in range(KD) for a in range(0, W, w1_cut)],
                          lambda u: o_unit(u % NG, u // NG), None)

            x2T = [sb(tail, f"x2T_{n}", [P, KD, T], F32R) for n in ("first", "rest")]
            w2_sb = [sb(tail, f"w2_{n}", [P, WT, D], F32R) for n in ("first", "rest")]
            rw_sb = [sb(tail, f"rw_{n}", [P, KD, E], F32R) for n in ("first", "rest")]
            w2_cut = WT // 6
            inner = ExitStack()
            with inner:
                project_norm("n2", inner, xwc, None, None, x_sb, x2T,
                             [(rw, rw_sb[0][:], rw_sb[1][:])]
                             + [(w2[w * P:(w + w2_cut) * P], w2_sb[0][:, w:w + w2_cut], w2_sb[1][:, w:w + w2_cut])
                                for w in range(0, WT, w2_cut)], 3)

            gate = sb(tail, "gate", [P, NT, E])
            top8 = sb(tail, "top8", [P, NT, 8])
            at8 = sb(tail, "at8", [P, NT, 8], U32)
            at_f = sb(tail, "at_f", [P, NT, 2])
            total = sb(tail, "total", [P, NT, 1])
            mix = sb(tail, "mix", [P, NT, E])
            hot = sb(tail, "hot", [P, NT, E])
            iota8 = sb(tail, "iota8", [P, E])
            hid = [sb(tail, f"hid_{n}", [P, 2, max(WIDTHS) // P, C], F32R) for n in ("first", "rest")]
            relu = o_tok[:, 0:3 * C // D].rearrange("p (n a) d -> p n (a d)", a=C // D)
            logits = o_tok[:, 6 * C // D:8 * C // D].rearrange("p (n a) d -> p n (a d)", a=C // D)
            square = o_tok[:, 3 * C // D:6 * C // D].rearrange("p (n a) d -> p n (a d)", a=C // D)
            stats = sb(tail, "n3_stats", [P, NT, 6])
            mv = sb(tail, "n3_mv", [P, NT, 2])
            rstd = sb(tail, "n3_rstd", [P, NT])
            pr = psum(tail, "pr", [P, NT, E])
            ph = psum(tail, "ph", [P, 3, C])
            py = psum(tail, "py", [P, 4, C])
            s_i8, r_ready, e_ready, h_ready, h_read = (sem("iota8_in"), sem("r_ready"), sem("e_ready"), sem("h_ready"), sem("h_read"))
            y_ready, y_read, hid_ready, s_out, normed = (sem("y_ready"), sem("y_read"), sem("hid_ready"), sem("out_done"), sem("n3_normed"))
            var_ready, std_ready = sem("n3_var_ready"), sem("n3_std_ready")
            logits_ready, logits_copied = sem("logits_ready"), sem("logits_copied")
            square_ready, first_ready = sem("square_ready"), sem("hid_first_ready")
            starts = [sum(WIDTHS[:e]) // P for e in range(E + 1)]
            jobs = [(c, e) for c in range(NC) for e in range(E)]
            tiles_before = [sum(WIDTHS[e] // P for _, e in jobs[:i]) for i in range(len(jobs) + 1)]

            with nc.Block() as block:
                @block.sync
                def _(sp):
                    sp.dma_start(iota8[:], iota[:, 0:E]).then_inc(s_i8, 16)
                    for n in range(NT):
                        sp.wait_ge(normed, n + 1)
                        sp.dma_start(out[n * P:(n + 1) * P, :], x_sb[:, n]).then_inc(s_out, 16)
                    sp.wait_ge(s_out, 16 * NT)

                @block.tensor
                def _(pe):
                    for c in range(NC):
                        for k in range(KD):
                            mm = product(py[0:E, c], [w[:, k] for w in rw_sb], [xt[:, k, c * C:(c + 1) * C] for xt in x2T], k == 0, k == KD - 1)
                        mm.then_inc(logits_ready, 1)
                    for c in range(NC):
                        pe.wait_ge(logits_copied, c + 1)
                        for q in range(TC):
                            mm = nc.tensor.transpose(pr[:, TC * c + q], logits[0:E, c % 2, q * P:(q + 1) * P], ident[0:E, 0:E])
                        mm.then_inc(r_ready, 1)
                    u = y = 0

                    def hidden(i):
                        nonlocal u
                        c, e = jobs[i]
                        for w in range(starts[e], starts[e + 1]):
                            if u >= 3:
                                pe.wait_ge(h_read, u - 2)
                            for k in range(KD):
                                mm = product(ph[:, u % 3], [v[:, k, w * P:(w + 1) * P] for v in w1_sb],
                                             [xt[:, k, c * C:(c + 1) * C] for xt in x2T], k == 0, k == KD - 1)
                            mm.then_inc(h_ready, 1)
                            u += 1

                    hidden(0)
                    for i, (c, e) in enumerate(jobs):
                        if i + 1 < len(jobs):
                            hidden(i + 1)
                        pe.wait_ge(hid_ready, tiles_before[i + 1])
                        for q in range(4):
                            if y >= 4:
                                pe.wait_ge(y_read, y - 3)
                            for w in range(WIDTHS[e] // P):
                                mm = product(py[:, y % 4, 0:D], [h[:, i % 2, w, q * P:(q + 1) * P] for h in hid],
                                             [v[:, starts[e] + w] for v in w2_sb], w == 0, w == WIDTHS[e] // P - 1)
                            mm.then_inc(y_ready, 1)
                            y += 1

                @block.scalar
                def _(act):
                    for c in range(NC):
                        act.wait_ge(logits_ready, c + 1)
                        if c >= 2:
                            act.wait_ge(r_ready, c - 1)
                        nc.scalar.copy(logits[0:E, c % 2], py[0:E, c]).then_inc(logits_copied, 1)
                    u = 0
                    for c, e in jobs:
                        for _ in range(WIDTHS[e] // P):
                            act.wait_ge(h_ready, u + 1)
                            if u >= 3:
                                act.wait_ge(hid_ready, u - 2)
                            nc.scalar.activation(relu[:, u % 3], ph[:, u % 3], ACT.Relu).then_inc(h_read, 1)
                            act.wait_ge(h_read, u + 1)
                            nc.scalar.activation(square[:, u % 3], relu[:, u % 3], ACT.Square).then_inc(square_ready, 1)
                            u += 1
                        if (c, e) == jobs[0]:
                            act.wait_ge(r_ready, NC)
                            nc.scalar.activation(gate[:], pr[:], ACT.Exp, scale=-1.0).then_inc(e_ready, 1)
                        if e == 1 and c:
                            deviation(act, c - 1, rstd, var_ready, std_ready)
                    deviation(act, NC - 1, rstd, var_ready, std_ready)

                @block.vector
                def _(dve):
                    link = chain(dve, "ffn_chain")
                    u = y = 0

                    def split(i):
                        nonlocal u
                        if i >= 2:
                            dve.wait_ge(y_ready, 4 * (i - 1))
                        for w in range(WIDTHS[jobs[i][1]] // P):
                            dve.wait_ge(square_ready, u + 1)
                            nc.vector.tensor_copy(hid[0][:, i % 2, w], square[:, u % 3]).then_inc(first_ready, 1)
                            dve.wait_ge(first_ready, u + 1)
                            nc.vector.tensor_tensor(hid[1][:, i % 2, w], square[:, u % 3], hid[0][:, i % 2, w].bitcast(F32),
                                                    ALU.subtract).then_inc(hid_ready, 1)
                            u += 1

                    split(0)
                    split(1)
                    dve.wait_ge(e_ready, 1)
                    dve.wait_ge(s_i8, 16)
                    link(nc.vector.tensor_scalar_add(gate[:], gate[:], 1.0))
                    link(nc.vector.reciprocal(gate[:], gate[:]))
                    for n in range(NT):
                        last = nc.vector.max(top8[:, n], gate[:, n])
                    link(last)
                    for n in range(NT):
                        last = nc.vector.max_index(at8[:, n], top8[:, n], gate[:, n])
                    link(last)
                    nc.vector.tensor_copy(at_f[:], at8[:, :, 0:2])
                    link(nc.vector.tensor_tensor(total[:], top8[:, :, 0:1], top8[:, :, 1:2], ALU.add))
                    link(nc.vector.tensor_scalar_add(total[:], total[:], 1e-20))
                    link(nc.vector.reciprocal(total[:], total[:]))
                    link(nc.vector.tensor_tensor(top8[:, :, 0:2], top8[:, :, 0:2], total[:].to_broadcast([P, NT, 2]), ALU.mult))
                    every = iota8[:].rearrange("p (o e) -> p o e", o=1).to_broadcast([P, NT, E])
                    nc.vector.tensor_tensor(hot[:], every, at_f[:, :, 0:1].to_broadcast([P, NT, E]), ALU.is_equal)
                    link(nc.vector.tensor_tensor(mix[:], every, at_f[:, :, 1:2].to_broadcast([P, NT, E]), ALU.is_equal))
                    nc.vector.tensor_tensor(hot[:], hot[:], top8[:, :, 0:1].to_broadcast([P, NT, E]), ALU.mult)
                    link(nc.vector.tensor_tensor(mix[:], mix[:], top8[:, :, 1:2].to_broadcast([P, NT, E]), ALU.mult))
                    link(nc.vector.tensor_tensor(mix[:], mix[:], hot[:], ALU.add))
                    for i, (c, e) in enumerate(jobs):
                        if i and i + 1 < len(jobs):
                            split(i + 1)
                        for q in range(4):
                            n = 4 * c + q
                            dve.wait_ge(y_ready, y + 1)
                            if y:
                                dve.wait_ge(y_read, y)
                            nc.vector.scalar_tensor_tensor(out=x_sb[:, n], in0=py[:, y % 4, 0:D], scalar=mix[:, n, e:e + 1],
                                                           in1=x_sb[:, n], op0=ALU.mult, op1=ALU.add).then_inc(y_read, 1)
                            y += 1
                        if e == 1 and c:
                            normalise(dve, link, c - 1, x_sb, mv, rstd, std_ready, normed)
                        if e == E - 1:
                            dve.wait_ge(y_read, y)
                            for n in range(TC * c, TC * (c + 1)):
                                last = nc.vector.bn_stats(stats[:, n], x_sb[:, n])
                            link(last)
                            variance(link, c, stats, mv, rstd, var_ready)
                    normalise(dve, link, NC - 1, x_sb, mv, rstd, std_ready, normed)


def kernel(x, ctx_1024, L0_attn_WQ_w, L0_attn_WQ_b, L0_attn_WK_w, L0_attn_WK_b, L0_attn_WV_w, L0_attn_WV_b, L0_attn_Wo_w,
           L0_attn_Wo_b, L0_xattn_Wq, L0_xattn_Wkv, L0_xattn_Wc, L0_ffn_router_w, L0_ffn_w1, L0_ffn_w2):
    import numpy as np
    import concourse.bacc as bacc
    from concourse.bass_utils import run_bass_kernel_spmd

    half = DK // 2
    swap = np.arange(D).reshape(H, 2, half)[:, ::-1].reshape(D)
    freq = (1.0 / 10000.0 ** (2.0 * np.arange(half, dtype=np.float32) / DK)).astype(np.float32)
    angle = np.arange(T, dtype=np.float32)[:, None] * freq[None, :]
    cos = np.tile(np.cos(angle).T, (2 * P // DK, 1)).astype(np.float32)
    sin = np.tile(np.concatenate([-np.sin(angle).T, np.sin(angle).T]), (P // DK, 1)).astype(np.float32)
    rows = np.arange(P)
    below = (rows[:, None] < rows[None, :]).astype(np.float32)
    tri = np.where(np.arange(P)[None, :] > rows[:, None], np.float32(MASKED), np.float32(0.0))
    causal = np.concatenate([np.zeros((P, C - P), np.float32), tri], 1)
    data = dict(
        x=x[0], xT=x[0].T, ctxT=np.pad(ctx_1024[0].T, ((0, 0), (0, M % 2))),
        wq=L0_attn_WQ_w.T, wqs=L0_attn_WQ_w[swap].T, bq=L0_attn_WQ_b.reshape(KD, P).T, bqs=L0_attn_WQ_b[swap].reshape(KD, P).T,
        wk=L0_attn_WK_w.T, wks=L0_attn_WK_w[swap].T, bk=L0_attn_WK_b.reshape(KD, P).T, bks=L0_attn_WK_b[swap].reshape(KD, P).T,
        wv=L0_attn_WV_w.T, bv=L0_attn_WV_b, wo=L0_attn_Wo_w.T, bo=L0_attn_Wo_b,
        xwq=L0_xattn_Wq.T, xwkv=L0_xattn_Wkv.T, xwc=L0_xattn_Wc.T,
        rw=L0_ffn_router_w.T, w1=L0_ffn_w1, w2=L0_ffn_w2,
        cosT=cos, sinT=sin, identity=np.eye(P, dtype=np.float32), below=below, causal=causal,
        iota=np.tile(np.arange(M, dtype=np.float32), (P, 1)))
    nc = bacc.Bacc("TRN2", target_bir_lowering=False, num_devices=1)
    arrays, args = {}, {}
    for name, a in data.items():
        a = np.ascontiguousarray(a)
        arrays[f"in_{name}"] = a
        args[name] = nc.dram_tensor(f"in_{name}", a.shape, mybir.dt.from_np(a.dtype), kind="ExternalInput").ap()
    out = nc.dram_tensor("out_0", (T, D), F32, kind="ExternalOutput").ap()
    decoder_layer(nc, out=out, **args)
    got = run_bass_kernel_spmd(nc, [arrays], core_ids=[0])
    return got.results[0]["out_0"].reshape(1, T, D)
```
